# Optimizing a Trainium2 kernel written in Bass

```python
import numpy as np
import jax
import jax.numpy as jnp

def _softmax(x, axis=-1):
    return jax.nn.softmax(x, axis=axis)

def _gelu(x):
    return jax.nn.gelu(x, approximate=True)

def _silu(x):
    return jax.nn.silu(x)

def _sigmoid(x):
    return jax.nn.sigmoid(x)

def _layernorm(x, axis=-1, eps=1e-05):
    m = jnp.mean(x, axis=axis, keepdims=True)
    v = jnp.var(x, axis=axis, keepdims=True)
    return (x - m) / jnp.sqrt(v + eps)

def _scatter_add(tgt, idx, src, axis=0):
    return tgt.at[idx].add(src)

def _segment_sum(src, seg, n):
    return jax.ops.segment_sum(src, seg, n)
kernel_name = 'mk_gnn_ffn_d2_gnn_r16_3c8294'

def setup_inputs(seed: int=0):
    np.random.seed(seed)
    _w = jnp.asarray

    def _rec_inputs():
        import jax
        import jax.numpy as jnp
        _gk = jax.random.key(seed)
        x = -8.776e-05 + 1 * jax.random.normal(jax.random.fold_in(_gk, 1), (3125, 256), jnp.float32)
        _s = jax.random.randint(jax.random.fold_in(_gk, 2), (25000,), 0, 3125, jnp.int32)
        _d = jax.random.randint(jax.random.fold_in(_gk, 3), (25000,), 0, 3125, jnp.int32)
        _loop = jnp.arange(3125, dtype=jnp.int32)
        src = jnp.concatenate([_s, _d, _loop])
        dst = jnp.concatenate([_d, _s, _loop])
        _o = jnp.argsort(dst, stable=True)
        src = src[_o]
        dst = dst[_o]
        edge_type_3 = jax.random.randint(jax.random.fold_in(_gk, 13), (53125,), 0, 3, jnp.int32)
        edge_weight = jax.random.uniform(jax.random.fold_in(_gk, 14), (53125,), jnp.float32, 0.0, 0.999998)
        return (x, src, dst, edge_type_3, edge_weight)
    x, src, dst, edge_type_3, edge_weight = _rec_inputs()

    def _L0_gnn_setup():
        import jax, jax.numpy as jnp
        import numpy as np
        H = 4
        DH = 64
        HID = 256
        EPS = 1e-05
        N_NODES = 1250
        N_EDGES = 20000
        N_LAYERS = 3

        def _layer_norm(x, g, b):
            mu = jnp.mean(x, axis=-1, keepdims=True)
            var = jnp.mean((x - mu) ** 2, axis=-1, keepdims=True)
            return (x - mu) * jax.lax.rsqrt(var + EPS) * g + b

        def _message_passing(h, src, tgt, et, Wq, bq, Wk, bk, Wv, bv, Ee, Wo, bo, n_nodes):
            Q = (h @ Wq.T + bq).reshape(-1, H, DH)
            K = (h @ Wk.T + bk).reshape(-1, H, DH)
            V = (h @ Wv.T + bv).reshape(-1, H, DH)
            scores = jnp.einsum('ehd,egd->ehg', Q[src], K[tgt]) / jnp.sqrt(jnp.float32(DH))
            attn = jax.nn.softmax(scores, axis=-1)
            msg = jnp.einsum('ehg,egd->ehd', attn, V[tgt]).reshape(-1, HID)
            msg = msg + Ee[et]
            proj = msg @ Wo.T + bo
            return jax.ops.segment_sum(proj, src, num_segments=n_nodes)
        key = jax.random.key(seed)
        ks = jax.random.split(key, 16)

        def w(k, shape, s=0.05):
            return jax.random.normal(k, shape, jnp.float32) * s
        return {'x': jax.random.normal(ks[0], (N_NODES, HID), jnp.float32), 'edges': jax.random.randint(ks[1], (N_EDGES, 2), 0, N_NODES), 'edge_types': jax.random.randint(ks[2], (N_EDGES,), 0, 3), 'Win': w(ks[3], (HID, HID)), 'b_in': jnp.zeros((HID,), jnp.float32), 'Wq': w(ks[4], (N_LAYERS, HID, HID)), 'bq': jnp.zeros((N_LAYERS, HID), jnp.float32), 'Wk': w(ks[5], (N_LAYERS, HID, HID)), 'bk': jnp.zeros((N_LAYERS, HID), jnp.float32), 'Wv': w(ks[6], (N_LAYERS, HID, HID)), 'bv': jnp.zeros((N_LAYERS, HID), jnp.float32), 'Eemb': w(ks[7], (N_LAYERS, 3, HID)), 'Wo': w(ks[8], (N_LAYERS, HID, HID)), 'bo': jnp.zeros((N_LAYERS, HID), jnp.float32), 'ln_g': jnp.ones((N_LAYERS, HID), jnp.float32), 'ln_b': jnp.zeros((N_LAYERS, HID), jnp.float32), 'W1': w(ks[9], (HID, HID)), 'b1': jnp.zeros((HID,), jnp.float32), 'W2': w(ks[10], (HID, HID)), 'b2': jnp.zeros((HID,), jnp.float32)}
    _L0_gnn_all = _L0_gnn_setup()
    _L0_gnn_in = {k: v for k, v in _L0_gnn_all.items() if k in ('Win', 'b_in', 'Wq', 'bq', 'Wk', 'bk', 'Wv', 'bv', 'Eemb', 'Wo', 'bo', 'ln_g', 'ln_b', 'W1', 'b1', 'W2', 'b2')}
    del _L0_gnn_all

    def _L0_ffn_setup():
        import jax, jax.numpy as jnp
        import numpy as np
        B, K, D = (512, 16, 256)
        E = 32
        H = int(D * 0.25)
        key = jax.random.key(seed)
        ks = jax.random.split(key, 7)
        d_rs = D ** (-0.5)
        h_rs = H ** (-0.5)
        x = jax.random.normal(ks[0], (B, K, D), dtype=jnp.float32)
        router_w = jax.random.uniform(ks[1], (E, D), jnp.float32, -d_rs, d_rs)
        router_b = jax.random.uniform(ks[2], (E,), jnp.float32, -d_rs, d_rs)
        W1 = jax.random.uniform(ks[3], (E, D, H), jnp.float32, -h_rs, h_rs)
        b1 = jax.random.uniform(ks[4], (E, H), jnp.float32, -h_rs, h_rs)
        W2 = jax.random.uniform(ks[5], (E, H, D), jnp.float32, -d_rs, d_rs)
        b2 = jax.random.uniform(ks[6], (E, D), jnp.float32, -d_rs, d_rs)
        return {'x': x, 'router_w': router_w, 'router_b': router_b, 'W1': W1, 'b1': b1, 'W2': W2, 'b2': b2}
    _L0_ffn_all = _L0_ffn_setup()
    _L0_ffn_in = {k: v for k, v in _L0_ffn_all.items() if k in ('router_w', 'router_b', 'W1', 'b1', 'W2', 'b2')}
    del _L0_ffn_all

    def _L1_gnn_setup():
        import jax, jax.numpy as jnp
        import numpy as np
        N_NODES = 3125
        N_EDGES = 50000
        H, D_IN, D_OUT = (4, 256, 64)
        key = jax.random.key(seed)
        ks = jax.random.split(key, 7)
        x = jax.random.normal(ks[0], (N_NODES, D_IN), dtype=jnp.float32)
        idx = jax.random.randint(ks[1], (2, N_EDGES), 0, N_NODES, dtype=jnp.int32)
        elem = jax.random.uniform(ks[2], (N_EDGES,), dtype=jnp.float32)
        Ws = jax.random.normal(ks[3], (H, D_IN, D_OUT), dtype=jnp.float32) * 0.05
        bs = jax.random.normal(ks[4], (H, D_OUT), dtype=jnp.float32) * 0.05
        aw = jax.random.normal(ks[5], (H, 2 * D_OUT + 1), dtype=jnp.float32) * 0.05
        ab = jax.random.normal(ks[6], (H,), dtype=jnp.float32) * 0.05
        return {'x': x, 'idx': idx, 'elem': elem, 'Ws': Ws, 'bs': bs, 'aw': aw, 'ab': ab}
    _L1_gnn_all = _L1_gnn_setup()
    _L1_gnn_in = {k: v for k, v in _L1_gnn_all.items() if k in ('Ws', 'bs', 'aw', 'ab')}
    del _L1_gnn_all

    def _L1_ffn_setup():
        import math
        import jax, jax.numpy as jnp
        import numpy as np
        CAPACITY_FACTOR = 1.25
        TOP_K = 2
        LN_EPS = 1e-05

        def _layer_norm(x, gamma, beta):
            mu = jnp.mean(x, axis=-1, keepdims=True)
            var = jnp.var(x, axis=-1, keepdims=True)
            return (x - mu) * jax.lax.rsqrt(var + LN_EPS) * gamma + beta
        key = jax.random.key(seed)
        ks = jax.random.split(key, 4)
        B, S, D, F, E = (8, 256, 256, 512, 8)
        x = jax.random.normal(ks[0], (B, S, D), dtype=jnp.float32)
        Wr = jax.random.normal(ks[1], (D, E), dtype=jnp.float32) / np.sqrt(D)
        br = jnp.zeros((E,), jnp.float32)
        W1 = jax.random.normal(ks[2], (E, D, F), dtype=jnp.float32) / np.sqrt(D)
        b1 = jnp.zeros((E, F), jnp.float32)
        W2 = jax.random.normal(ks[3], (E, F, D), dtype=jnp.float32) / np.sqrt(F)
        b2 = jnp.zeros((E, D), jnp.float32)
        gamma = jnp.ones((D,), jnp.float32)
        beta = jnp.zeros((D,), jnp.float32)
        return {'x': x, 'Wr': Wr, 'br': br, 'W1': W1, 'b1': b1, 'W2': W2, 'b2': b2, 'gamma': gamma, 'beta': beta}
    _L1_ffn_all = _L1_ffn_setup()
    _L1_ffn_in = {k: v for k, v in _L1_ffn_all.items() if k in ('Wr', 'br', 'W1', 'b1', 'W2', 'b2', 'gamma', 'beta')}
    del _L1_ffn_all
    return {'x': x, 'src': src, 'dst': dst, 'edge_type_3': edge_type_3, 'edge_weight': edge_weight, 'L0_gnn_Win': _L0_gnn_in['Win'], 'L0_gnn_b_in': _L0_gnn_in['b_in'], 'L0_gnn_Wq': _L0_gnn_in['Wq'], 'L0_gnn_bq': _L0_gnn_in['bq'], 'L0_gnn_Wk': _L0_gnn_in['Wk'], 'L0_gnn_bk': _L0_gnn_in['bk'], 'L0_gnn_Wv': _L0_gnn_in['Wv'], 'L0_gnn_bv': _L0_gnn_in['bv'], 'L0_gnn_Eemb': _L0_gnn_in['Eemb'], 'L0_gnn_Wo': _L0_gnn_in['Wo'], 'L0_gnn_bo': _L0_gnn_in['bo'], 'L0_gnn_ln_g': _L0_gnn_in['ln_g'], 'L0_gnn_ln_b': _L0_gnn_in['ln_b'], 'L0_gnn_W1': _L0_gnn_in['W1'], 'L0_gnn_b1': _L0_gnn_in['b1'], 'L0_gnn_W2': _L0_gnn_in['W2'], 'L0_gnn_b2': _L0_gnn_in['b2'], 'L0_ffn_router_w': _L0_ffn_in['router_w'], 'L0_ffn_router_b': _L0_ffn_in['router_b'], 'L0_ffn_W1': _L0_ffn_in['W1'], 'L0_ffn_b1': _L0_ffn_in['b1'], 'L0_ffn_W2': _L0_ffn_in['W2'], 'L0_ffn_b2': _L0_ffn_in['b2'], 'L1_gnn_Ws': _L1_gnn_in['Ws'], 'L1_gnn_bs': _L1_gnn_in['bs'], 'L1_gnn_aw': _L1_gnn_in['aw'], 'L1_gnn_ab': _L1_gnn_in['ab'], 'L1_ffn_Wr': _L1_ffn_in['Wr'], 'L1_ffn_br': _L1_ffn_in['br'], 'L1_ffn_W1': _L1_ffn_in['W1'], 'L1_ffn_b1': _L1_ffn_in['b1'], 'L1_ffn_W2': _L1_ffn_in['W2'], 'L1_ffn_b2': _L1_ffn_in['b2'], 'L1_ffn_gamma': _L1_ffn_in['gamma'], 'L1_ffn_beta': _L1_ffn_in['beta']}

def reference(x, src, dst, edge_type_3, edge_weight, L0_gnn_Win, L0_gnn_b_in, L0_gnn_Wq, L0_gnn_bq, L0_gnn_Wk, L0_gnn_bk, L0_gnn_Wv, L0_gnn_bv, L0_gnn_Eemb, L0_gnn_Wo, L0_gnn_bo, L0_gnn_ln_g, L0_gnn_ln_b, L0_gnn_W1, L0_gnn_b1, L0_gnn_W2, L0_gnn_b2, L0_ffn_router_w, L0_ffn_router_b, L0_ffn_W1, L0_ffn_b1, L0_ffn_W2, L0_ffn_b2, L1_gnn_Ws, L1_gnn_bs, L1_gnn_aw, L1_gnn_ab, L1_ffn_Wr, L1_ffn_br, L1_ffn_W1, L1_ffn_b1, L1_ffn_W2, L1_ffn_b2, L1_ffn_gamma, L1_ffn_beta):
    import jax
    import jax.numpy as jnp

    def _L0_gnn_ref(x, edges, edge_types, Win, b_in, Wq, bq, Wk, bk, Wv, bv, Eemb, Wo, bo, ln_g, ln_b, W1, b1, W2, b2):
        import jax, jax.numpy as jnp
        import numpy as np
        H = 4
        DH = 64
        HID = 256
        EPS = 1e-05
        N_NODES = 1250
        N_EDGES = 20000
        N_LAYERS = 3

        def _layer_norm(x, g, b):
            mu = jnp.mean(x, axis=-1, keepdims=True)
            var = jnp.mean((x - mu) ** 2, axis=-1, keepdims=True)
            return (x - mu) * jax.lax.rsqrt(var + EPS) * g + b

        def _message_passing(h, src, tgt, et, Wq, bq, Wk, bk, Wv, bv, Ee, Wo, bo, n_nodes):
            Q = (h @ Wq.T + bq).reshape(-1, H, DH)
            K = (h @ Wk.T + bk).reshape(-1, H, DH)
            V = (h @ Wv.T + bv).reshape(-1, H, DH)
            scores = jnp.einsum('ehd,egd->ehg', Q[src], K[tgt]) / jnp.sqrt(jnp.float32(DH))
            attn = jax.nn.softmax(scores, axis=-1)
            msg = jnp.einsum('ehg,egd->ehd', attn, V[tgt]).reshape(-1, HID)
            msg = msg + Ee[et]
            proj = msg @ Wo.T + bo
            return jax.ops.segment_sum(proj, src, num_segments=n_nodes)
        n_nodes = x.shape[0]
        src, tgt = (edges[:, 0], edges[:, 1])
        hidden = x @ Win.T + b_in
        for l in range(N_LAYERS):
            m = _message_passing(hidden, src, tgt, edge_types, Wq[l], bq[l], Wk[l], bk[l], Wv[l], bv[l], Eemb[l], Wo[l], bo[l], n_nodes)
            hidden = jax.nn.relu(_layer_norm(hidden + m, ln_g[l], ln_b[l]))
        adjustment = jax.nn.relu(hidden @ W1.T + b1) @ W2.T + b2
        return x + adjustment

    def _L0_ffn_ref(x, router_w, router_b, W1, b1, W2, b2):
        import jax, jax.numpy as jnp
        import numpy as np
        B, K, D = (512, 16, 256)
        E = 32
        H = int(D * 0.25)
        xf = x.reshape(-1, D)
        logits = xf @ router_w.T + router_b
        idx = jnp.argmax(logits, axis=-1)
        w1t = jnp.take(W1, idx, axis=0)
        h = jnp.einsum('nd,ndh->nh', xf, w1t) + jnp.take(b1, idx, axis=0)
        h = jax.nn.relu(h)
        w2t = jnp.take(W2, idx, axis=0)
        out = jnp.einsum('nh,nhd->nd', h, w2t) + jnp.take(b2, idx, axis=0)
        out = jax.nn.relu(out)
        return out.reshape(x.shape)

    def _L1_gnn_ref(x, idx, elem, Ws, bs, aw, ab):
        import jax, jax.numpy as jnp
        import numpy as np
        N_NODES = 3125
        N_EDGES = 50000
        H, D_IN, D_OUT = (4, 256, 64)
        N = x.shape[0]
        O = Ws.shape[-1]
        feats = jnp.einsum('nd,hdo->hno', x, Ws) + bs[:, None, :]
        aw_src, aw_dst, aw_e = (aw[:, :O], aw[:, O:2 * O], aw[:, 2 * O])
        a_s = jnp.einsum('hno,ho->hn', feats, aw_src)
        a_d = jnp.einsum('hno,ho->hn', feats, aw_dst)
        src, dst = (idx[0], idx[1])
        score = a_s[:, src] + a_d[:, dst] + aw_e[:, None] * elem[None, :] + ab[:, None]
        w = jnp.exp(-jax.nn.relu(score / 20.0))
        dst_f = feats[:, dst]
        seg = lambda vals: jax.ops.segment_sum(vals, src, num_segments=N)
        pooled = jax.vmap(lambda wi, fi: seg(wi[:, None] * fi))(w, dst_f)
        row_sum = jax.vmap(lambda wi: seg(wi))(w)
        out = pooled / row_sum[:, :, None]
        return jnp.transpose(out, (1, 0, 2)).reshape(N, H * O)

    def _L1_ffn_ref(x, Wr, br, W1, b1, W2, b2, gamma, beta):
        import math
        import jax, jax.numpy as jnp
        import numpy as np
        CAPACITY_FACTOR = 1.25
        TOP_K = 2
        LN_EPS = 1e-05

        def _layer_norm(x, gamma, beta):
            mu = jnp.mean(x, axis=-1, keepdims=True)
            var = jnp.var(x, axis=-1, keepdims=True)
            return (x - mu) * jax.lax.rsqrt(var + LN_EPS) * gamma + beta
        B, S, D = x.shape
        E = Wr.shape[1]
        N = B * S
        K = TOP_K
        logits = jnp.mean(x, axis=1) @ Wr + br
        routing_weights = jax.nn.softmax(logits, axis=-1)
        capacity = float(math.ceil(N * CAPACITY_FACTOR / E))
        expected_loads = routing_weights.sum(axis=0) * (N / B)
        scale = jnp.where(expected_loads > capacity, capacity / expected_loads, 1.0)
        routing_weights = jax.nn.softmax(routing_weights * scale, axis=-1)
        rw_tok = jnp.broadcast_to(routing_weights[:, None, :], (B, S, E)).reshape(N, E)
        top_w, top_i = jax.lax.top_k(rw_tok, K)
        top_w = jax.nn.softmax(top_w, axis=-1)
        xf = x.reshape(N, D)
        h = jax.nn.gelu(jnp.einsum('nd,edf->enf', xf, W1) + b1[:, None, :], approximate=False)
        y = jnp.einsum('enf,efd->end', h, W2) + b2[:, None, :]
        w_dense = jnp.zeros((N, E), x.dtype).at[jnp.arange(N)[:, None], top_i].add(top_w)
        out = jnp.einsum('ne,end->nd', w_dense, y).reshape(B, S, D)
        out = _layer_norm(out + x, gamma, beta)
        return out
    edge_index = jnp.stack([src, dst])
    edge_index_t = jnp.stack([src, dst], axis=1)
    x = x + _L0_gnn_ref(_layernorm(x, axis=-1), edge_index_t, edge_type_3, L0_gnn_Win, L0_gnn_b_in, L0_gnn_Wq, L0_gnn_bq, L0_gnn_Wk, L0_gnn_bk, L0_gnn_Wv, L0_gnn_bv, L0_gnn_Eemb, L0_gnn_Wo, L0_gnn_bo, L0_gnn_ln_g, L0_gnn_ln_b, L0_gnn_W1, L0_gnn_b1, L0_gnn_W2, L0_gnn_b2)
    x = x + _L0_ffn_ref(_layernorm(x, axis=-1)[None], L0_ffn_router_w, L0_ffn_router_b, L0_ffn_W1, L0_ffn_b1, L0_ffn_W2, L0_ffn_b2)[0]
    x = x + _L1_gnn_ref(_layernorm(x, axis=-1), edge_index, edge_weight, L1_gnn_Ws, L1_gnn_bs, L1_gnn_aw, L1_gnn_ab)
    x = x + _L1_ffn_ref(_layernorm(x, axis=-1)[None], L1_ffn_Wr, L1_ffn_br, L1_ffn_W1, L1_ffn_b1, L1_ffn_W2, L1_ffn_b2, L1_ffn_gamma, L1_ffn_beta)[0]
    return x

_drawn_inputs = setup_inputs


def setup_inputs(seed=0):
    import zlib

    import numpy as np

    out = dict(_drawn_inputs(seed))
    spreads = {'L0_gnn_b_in': (0.0, 0.317),
     'L0_gnn_bq': (0.0, 0.534),
     'L0_gnn_bk': (0.0, 0.55),
     'L0_gnn_bv': (0.0, 0.1),
     'L0_gnn_bo': (0.0, 0.1),
     'L0_gnn_ln_g': (1.0, 0.2),
     'L0_gnn_ln_b': (0.0, 0.1),
     'L0_gnn_b1': (0.0, 0.267),
     'L0_gnn_b2': (0.0, 0.1),
     'L1_ffn_br': (0.0, 0.8),
     'L1_ffn_b1': (0.0, 0.505),
     'L1_ffn_b2': (0.0, 0.396),
     'L1_ffn_gamma': (1.0, 0.2),
     'L1_ffn_beta': (0.0, 0.1)}
    factors = {'edge_weight': 64.0,
     'L0_gnn_Win': 2.776,
     'L0_ffn_b1': 8.0,
     'L0_ffn_b2': 4.651,
     'L1_gnn_aw': 55.857,
     'L1_gnn_ab': 64.0}
    for name, (base, spread) in spreads.items():
        noise = np.random.default_rng([zlib.crc32(name.encode()), seed]).standard_normal(out[name].shape)
        drawn = base * np.exp(spread * noise) if base else spread * noise
        out[name] = jnp.asarray(drawn.astype(out[name].dtype))
    for name, factor in factors.items():
        out[name] = (out[name] * factor).astype(out[name].dtype)
    return out
```

```python
from contextlib import ExitStack, contextmanager

import numpy as np

import concourse.bass as bass
from concourse import mybir

F32, BF16, I32 = mybir.dt.float32, mybir.dt.bfloat16, mybir.dt.int32
ALU = mybir.AluOpType
ACT = mybir.ActivationFunctionType
AX = mybir.AxisListType

P = 128
N, D, E = 3125, 256, 53125
H, DH, LAYERS = 4, 64, 3
W = 16
HW = H * W
NODE_TILES = -(-N // P)
NP_ = NODE_TILES * P
BLOCKS = NP_ // W
CT = 5
CHUNKS = NODE_TILES // CT
CN = CT * P
CB = CN // W
HALF = CN // 2
EC = -(-E // P)
BT = 4
TILES = -(-(E // P + BLOCKS) // BT) * BT
BATCHES = TILES // BT
TG = -(-(TILES + BT) // P)
SETS = 4
TYPES = 16
MR = DH + TYPES
FR = DH + 1
FROW = H * FR + H
PR = 80
BIG = 1e30
EPS = 1e-5
EX0, H0 = 32, 64
HC = EX0 * H0 // P
EX1, FF = 8, 512
FC = FF // P
CAPACITY = float(-(-N * 5 // (4 * EX1)))
SRC_PAD = 4000
NOBODY = 4095
assert SRC_PAD // W >= BLOCKS and NOBODY >= NP_ and CHUNKS * CT == NODE_TILES and EC % 8 == 0


@contextmanager
def phase(nc, title, *names):
    sems = {}
    for name in names:
        name, _, many = name.partition("*")
        made = [nc.alloc_semaphore(f"{title}_{name}{i}") for i in range(int(many or 1))]
        sems[name] = made if many else made[0]
    flat = [s for x in sems.values() for s in (x if isinstance(x, list) else [x])]
    with nc.Block() as block:
        yield block, type("Sems", (), sems)
    nc.clear_and_free_semaphores(flat)
    nc.all_engine_barrier()


def batches(eng, first, last, peel, step):
    mid = (last - first - peel) // SETS
    for b in range(first, first + peel):
        step(b, b // SETS, b % SETS)
    b0 = first + peel
    if mid:
        with eng.Fori(0, mid) as i:
            for j in range(SETS):
                step(i * SETS + (b0 + j), i + (b0 + j) // SETS, (b0 + j) % SETS)
    for b in range(b0 + mid * SETS, last):
        step(b, b // SETS, b % SETS)


def after(b, k):
    return not isinstance(b, int) or b >= k


def bc(ap, axis, count):
    a = ap.unsqueeze(axis)
    shape = list(a.shape)
    shape[axis] = count
    return a.broadcast_to(shape)


def build(nc, t, out):
    ctx = ExitStack()

    def dram(name, shape, dt=F32):
        return nc.dram_tensor(name, list(shape), dt, kind="Internal").ap()

    slot_d = dram("slot_table", (P * TILES, 4))
    blk_d = dram("tile_block", (TG * P,), I32)
    outblk_d = dram("tile_out", (TG * P,), I32)
    keep_d = dram("tile_keep", (TG * P,))
    kv_d = dram("kv_table", (NP_, 2 * D))
    q_d = dram("q_blocks", (BLOCKS * P, P))
    m_d = dram("message_sums", ((BLOCKS + TILES) * MR, HW))
    f_d = dram("feature_table", (NP_, FROW))
    as_d = dram("a_src", (BLOCKS, W * H))
    p_d = dram("pooled_sums", ((BLOCKS + TILES) * PR, HW))

    with ctx:
        def sb(name, shape, dt=F32, stack=ctx):
            return stack.enter_context(nc.sbuf_tensor(name, list(shape), dt))

        def pb(stack, name, shape, dt=F32):
            return stack.enter_context(nc.psum_tensor(name, list(shape), dt))

        x = sb("x", (P, NODE_TILES, D))
        hid = sb("hid", (P, NODE_TILES, D))
        ident = sb("ident", (P, P))
        ident_b = sb("ident_b", (P, P), BF16)
        iota_w = sb("iota_w", (P, W))
        valid = sb("valid", (P, NODE_TILES))
        eps = sb("eps", (P, 1))
        keep = sb("keep", (P, TG * P))
        tile_blk = sb("tile_blk", (1, TG * P), I32)
        tile_out = sb("tile_out_row", (1, TG * P), I32)
        slots = sb("slots", (P, TILES + BT, 4))
        kv = sb("kv", (P, SETS, BT, 2 * D))
        node_sum = sb("node_sum", (P, 2))

        edge_sort(nc, t, sb, pb, locals())
        hidden_in(nc, t, sb, pb, locals())
        with nc.Fori(0, LAYERS) as layer:
            qkv(nc, t, sb, pb, locals(), layer)
            attention_edges(nc, t, sb, pb, locals())
            node_update(nc, t, sb, pb, locals(), layer)
        adjustment(nc, t, sb, pb, locals())
        expert_ffn(nc, t, sb, pb, locals())
        features(nc, t, sb, pb, locals())
        pooling_edges(nc, t, sb, pb, locals())
        pooled_nodes(nc, t, sb, pb, locals())
        routed_ffn(nc, t, sb, pb, locals(), out)


def edge_sort(nc, t, sb, pb, g):
    slot_d, blk_d, outblk_d, keep_d = g["slot_d"], g["blk_d"], g["outblk_d"], g["keep_d"]
    x, ident, ident_b, iota_w, valid, eps = (g[k] for k in ("x", "ident", "ident_b", "iota_w", "valid", "eps"))
    G8 = 8
    with ExitStack() as st:
        def s(name, shape, dt=F32):
            return sb(name, shape, dt, st)
        src = s("src_i", (P, EC), I32)
        dst = s("dst_i", (P, EC), I32)
        ety = s("ety_i", (P, EC), I32)
        ewt = s("edge_w", (P, EC))
        blk = s("edge_blk", (P, EC), I32)
        loc = s("edge_loc", (P, EC), I32)
        blk_f = s("edge_blk_f", (P, EC + 4))
        rec = s("rec", (P, EC, 4))
        iota_b = s("iota_b", (P, BLOCKS))
        onehot = s("onehot", (P, 2, G8, BLOCKS), BF16)
        before = s("before", (P, P))
        before_b = s("before_b", (P, P), BF16)
        ones_b = s("ones_b", (P, P), BF16)
        ones_f = s("ones_f", (1, P))
        zeros = s("zeros", (P, BLOCKS))
        zeros_b = s("zeros_b", (P, 2 * BLOCKS), BF16)
        empty = s("empty", (P, TILES, 4))
        count = s("count", (P, BLOCKS))
        count_i = s("count_i", (P, BLOCKS), I32)
        tiles = s("tiles", (P, BLOCKS))
        t_end = s("t_end", (P, BLOCKS))
        t_base = s("t_base", (P, BLOCKS))
        s_base = s("s_base", (P, BLOCKS))
        tcol = s("tcol", (P, TG))
        cmp = s("cmp", (P, 3, TG, BLOCKS))
        cols = s("cols", (P, 6, TG))
        cols_i = s("cols_i", (P, 2, TG), I32)

        with ExitStack() as ps_st, phase(
                nc, "count", "loaded", "x_loaded", "const_ready", "filled", "empty_ready", "split", "parts", "hot*2",
                "counted*2", "sum_ready") as (block, m):
            hist = pb(ps_st, "hist", (P, 2 * BLOCKS))

            @block.sync
            def _(sp):
                for a, b in ((src, t["src"]), (dst, t["dst"]), (ety, t["edge_type"]), (ewt, t["edge_weight"]), (iota_b, t["c_iota_b"]),
                             (before, t["c_before"]), (tcol, t["c_tcol"]), (ident, t["c_ident"]),
                             (iota_w, t["c_iota_w"]), (valid, t["c_valid"])):
                    sp.dma_start(a[:, :], b).then_inc(m.loaded, 16)
                sp.dma_start(x[:, :, :], t["x"]).then_inc(m.x_loaded, 16)
                sp.wait_ge(m.empty_ready, 1)
                sp.dma_start(slot_d.rearrange("(p t) f -> p t f", p=P), empty[:, :, :]).then_inc(m.filled, 16)
                sp.wait_ge(m.x_loaded, 16)
                sp.wait_ge(m.filled, 16)

            @block.gpsimd
            def _(pool):
                pool.memset(ones_b[:, :], 1.0)
                pool.memset(zeros[:, :], 0.0)
                pool.memset(ones_f[:, :], 1.0)
                pool.memset(eps[:, :], EPS)
                pool.memset(zeros_b[:, :], 0.0).then_inc(m.const_ready, 1)
                pool.memset(blk_f[:, EC:EC + 4], float(BLOCKS))
                pool.memset(empty[:, :, 0], float(NOBODY))
                pool.memset(empty[:, :, 1], 99.0)
                pool.memset(empty[:, :, 2], 99.0)
                pool.memset(empty[:, :, 3], 0.0).then_inc(m.empty_ready, 1)

            @block.scalar
            def _(act):
                act.wait_ge(m.loaded, 160)
                act.activation(ident_b[:, :], ident[:, :], ACT.Copy)
                act.activation(before_b[:, :], before[:, :], ACT.Copy)
                act.activation(rec[:, :, 2], ety[:, :], ACT.Copy)
                act.activation(rec[:, :, 0], dst[:, :], ACT.Copy)
                act.activation(rec[:, :, 3], ewt[:, :], ACT.Copy)

            @block.vector
            def _(v):
                v.wait_ge(m.loaded, 160)
                v.tensor_single_scalar(blk[:, :], src[:, :], 4, ALU.logical_shift_right).then_inc(m.split, 1)
                v.tensor_single_scalar(loc[:, :], src[:, :], W - 1, ALU.bitwise_and).then_inc(m.split, 1)
                v.wait_ge(m.split, 2)
                v.tensor_copy(blk_f[:, 0:EC], blk[:, :]).then_inc(m.parts, 1)
                v.tensor_copy(rec[:, :, 1], loc[:, :]).then_inc(m.parts, 1)
                v.wait_ge(m.parts, 1)
                with v.Fori(0, EC // (2 * G8)) as i:
                    for j in range(2):
                        v.wait_ge(m.counted[j], i)
                        v.tensor_tensor(onehot[:, j, :, :], bc(iota_b[:, :], 1, G8),
                                        bc(blk_f[:, bass.ds((i * 2 + j) * G8, G8)], 2, BLOCKS),
                                        ALU.is_equal).then_inc(m.hot[j], 1)

                v.wait_ge(m.sum_ready, 1)
                v.tensor_copy(count[:, :], hist[:, 0:BLOCKS]).then_inc(m.split, 1)
                v.wait_ge(m.split, 3)
                v.scalar_tensor_tensor(tiles[:, :], count[:, :], float(P - 1), hist[:, BLOCKS:2 * BLOCKS], ALU.add,
                                       ALU.add).then_inc(m.split, 1)
                v.wait_ge(m.split, 4)
                v.tensor_copy(count_i[:, :], tiles[:, :]).then_inc(m.split, 1)
                v.wait_ge(m.split, 5)
                v.tensor_single_scalar(count_i[:, :], count_i[:, :], 7, ALU.logical_shift_right).then_inc(m.split, 1)
                v.wait_ge(m.split, 6)
                v.tensor_single_scalar(tiles[:, :], count_i[:, :], 1.0, ALU.max).then_inc(m.split, 1)
                v.wait_ge(m.split, 7)
                v.wait_ge(m.const_ready, 1)
                v.tensor_tensor_scan(t_end[:, :], tiles[:, :], zeros[:, :], 0.0, ALU.add, ALU.add).then_inc(m.split, 1)
                v.wait_ge(m.split, 8)
                v.tensor_tensor(t_base[:, :], t_end[:, :], tiles[:, :], ALU.subtract).then_inc(m.split, 1)
                v.wait_ge(m.split, 9)
                v.tensor_single_scalar(s_base[:, :], t_base[:, :], float(P), ALU.mult).then_inc(m.split, 1)

            @block.tensor
            def _(pe):
                pe.wait_ge(m.const_ready, 1)
                pe.matmul(hist[:, :], ones_b[:, :], zeros_b[:, :], start=True, stop=False)
                with pe.Fori(0, EC // (2 * G8)) as i:
                    for j in range(2):
                        pe.wait_ge(m.hot[j], i + 1)
                        for c in range(0, G8, 2):
                            last = pe.matmul(hist[:, :], ones_b[:, :],
                                             onehot[:, j, c:c + 2, :].rearrange("p a b -> p (a b)"),
                                             start=False, stop=False)
                        last.then_inc(m.counted[j], 1)
                pe.matmul(hist[:, :], ones_b[:, :], zeros_b[:, :], start=False, stop=True).then_inc(m.sum_ready, 1)

        with phase(nc, "tables", "step", "stored", "loaded") as (block, m):
            tb = bc(tcol[:, :], 2, BLOCKS)

            @block.vector
            def _(v):
                v.tensor_tensor(cmp[:, 0, :, :], bc(t_end[:, :], 1, TG), tb, ALU.is_le)
                v.tensor_tensor(cmp[:, 2, :, :], bc(t_base[:, :], 1, TG), tb, ALU.is_equal)
                v.tensor_single_scalar(cols[:, 3, :], tcol[:, :], 1.0, ALU.add).then_inc(m.step, 1)
                v.wait_ge(m.step, 1)
                v.tensor_tensor(cmp[:, 1, :, :], bc(t_end[:, :], 1, TG), bc(cols[:, 3, :], 2, BLOCKS),
                                ALU.is_equal).then_inc(m.step, 1)
                v.wait_ge(m.step, 2)
                v.tensor_reduce(cols[:, 0:3, :], cmp[:, :, :, :], axis=AX.X, op=ALU.add).then_inc(m.step, 1)
                v.wait_ge(m.step, 3)
                v.tensor_single_scalar(cols_i[:, 0, :], cols[:, 0, :], float(BLOCKS - 1), ALU.min)
                v.tensor_single_scalar(cols[:, 4, :], tcol[:, :], float(BLOCKS), ALU.add)
                v.tensor_scalar(cols[:, 5, :], cols[:, 2, :], -1.0, 1.0, ALU.mult, ALU.add).then_inc(m.step, 1)
                v.wait_ge(m.step, 4)
                v.tensor_tensor(cols[:, 3, :], cols[:, 0, :], cols[:, 4, :], ALU.subtract).then_inc(m.step, 1)
                v.wait_ge(m.step, 5)
                v.tensor_tensor(cols[:, 2, :], cols[:, 3, :], cols[:, 1, :], ALU.mult).then_inc(m.step, 1)
                v.wait_ge(m.step, 6)
                v.tensor_tensor(cols_i[:, 1, :], cols[:, 2, :], cols[:, 4, :], ALU.add).then_inc(m.step, 1)

            @block.sync
            def _(sp):
                sp.wait_ge(m.step, 7)
                with nc.allow_non_contiguous_dma("tile tables, once"):
                    sp.dma_start(blk_d.rearrange("(g p) -> p g", p=P), cols_i[:, 0, :]).then_inc(m.stored, 16)
                    sp.dma_start(outblk_d.rearrange("(g p) -> p g", p=P), cols_i[:, 1, :]).then_inc(m.stored, 16)
                    sp.dma_start(keep_d.rearrange("(g p) -> p g", p=P), cols[:, 5, :]).then_inc(m.stored, 16)
                sp.wait_ge(m.stored, 48)
                sp.dma_start(g["tile_blk"][0:1, :], blk_d.unsqueeze(0)).then_inc(m.loaded, 16)
                sp.dma_start(g["tile_out"][0:1, :], outblk_d.unsqueeze(0)).then_inc(m.loaded, 16)
                sp.dma_start(g["keep"][:, :], keep_d.unsqueeze(0).broadcast_to([P, TG * P])).then_inc(m.loaded, 16)
                sp.wait_ge(m.loaded, 48)

        GR = 4
        TURNS = EC // GR
        pos = s("pos", (P, 2, GR))
        pos_i = s("pos_i", (P, 2, 3, GR), I32)
        beyond = s("beyond", (P, 2, GR))
        idx = s("idx", (P, 2, GR), I32)
        rec_c = s("rec_c", (P, 2, GR, 4))
        prod = s("prod", (P, GR, BLOCKS))
        given = s("given", (1, 2, BLOCKS))
        with ExitStack() as ps_st, phase(
                nc, "place", "hot*2", "bank_free", "ranked", "prior*4", "totaled", "given_ready", "turn", "step",
                "idx_ready*2", "written*2") as (block, m):
            taken = pb(ps_st, "taken", (P, GR, 512))
            total = pb(ps_st, "total", (P, 2, 512))

            @block.scalar
            def _(act):
                act.activation(given[0:1, 0, :], s_base[0:1, :], ACT.Copy).then_inc(m.given_ready, 1)
                with act.Fori(0, TURNS // 2) as it:
                    for j in range(2):
                        act.wait_ge(m.totaled, it * 2 + j + 1)
                        act.activation(given[0:1, 1 - j, :], total[0:1, j, 0:BLOCKS], ACT.Copy).then_inc(m.given_ready, 1)

            @block.vector
            def _(v):
                def hot(i, j):
                    v.tensor_tensor(onehot[:, j, 0:GR, :], bc(iota_b[:, :], 1, GR),
                                    bc(blk_f[:, bass.ds(i * GR, GR)], 2, BLOCKS), ALU.is_equal).then_inc(m.hot[j], 1)
                v.memset(pos[:, :, :], 0.0).then_inc(m.bank_free, 1)
                hot(0, 0)
                with v.Fori(0, TURNS // 2) as it:
                    for j in range(2):
                        i = it * 2 + j
                        v.wait_ge(m.totaled, i)
                        hot(i + 1, 1 - j)
                        v.wait_ge(m.hot[j], it + 1)
                        for k in range(GR):
                            v.wait_ge(m.prior[k], i + 1)
                            v.tensor_tensor_reduce(out=prod[:, k, :], in0=onehot[:, j, k, :],
                                                   in1=taken[:, k, 0:BLOCKS], scale=1.0, scalar=0.0, op0=ALU.mult,
                                                   op1=ALU.add, accum_out=pos[:, j, k:k + 1]).then_inc(m.ranked, 1)
                        v.tensor_scalar(beyond[:, j, :], blk_f[:, bass.ds(i * GR, GR)], float(BLOCKS) - 0.5,
                                        float(1 << 24), ALU.is_ge, ALU.mult).then_inc(m.step, 1)
                        v.wait_ge(m.step, i * 4 + 1)
                        v.wait_ge(m.ranked, (i + 1) * GR)
                        v.tensor_tensor(pos_i[:, j, 0, :], pos[:, j, :], beyond[:, j, :], ALU.add).then_inc(m.step, 1)
                        v.wait_ge(m.step, i * 4 + 2)
                        v.tensor_single_scalar(pos_i[:, j, 1, :], pos_i[:, j, 0, :], P - 1, ALU.bitwise_and)
                        v.tensor_single_scalar(pos_i[:, j, 2, :], pos_i[:, j, 0, :], 7,
                                               ALU.logical_shift_right).then_inc(m.step, 1)
                        v.wait_ge(m.step, i * 4 + 3)
                        v.wait_ge(m.written[j], it * (16 * GR))
                        v.scalar_tensor_tensor(idx[:, j, :], pos_i[:, j, 1, :], float(TILES), pos_i[:, j, 2, :],
                                               ALU.mult, ALU.add).then_inc(m.step, 1)
                        v.tensor_copy(rec_c[:, j, :, :], rec[:, bass.ds(i * GR, GR), :]).then_inc(m.idx_ready[j], 1)
                        v.wait_ge(m.step, i * 4 + 4)

            @block.tensor
            def _(pe):
                pe.wait_ge(m.bank_free, 1)
                with pe.Fori(0, TURNS // 2) as it:
                    for j in range(2):
                        i = it * 2 + j
                        pe.wait_ge(m.hot[j], it + 1)
                        pe.wait_ge(m.given_ready, i + 1)
                        pe.matmul(total[:, j, 0:BLOCKS], ones_f[0:1, :], given[0:1, j, :], start=True, stop=False)
                        for e in range(GR):
                            last = pe.matmul(total[:, j, 0:BLOCKS], ones_b[:, :], onehot[:, j, e, :],
                                             start=False, stop=e == GR - 1)
                        last.then_inc(m.totaled, 1)
                        for k in range(GR):
                            if k == 0:
                                pe.wait_ge(m.ranked, i * GR)
                            pe.matmul(taken[:, k, 0:BLOCKS], ones_f[0:1, :], given[0:1, j, :], start=True, stop=False)
                            for e in range(k):
                                pe.matmul(taken[:, k, 0:BLOCKS], ones_b[:, :], onehot[:, j, e, :],
                                          start=False, stop=False)
                            pe.matmul(taken[:, k, 0:BLOCKS], before_b[:, :], onehot[:, j, k, :],
                                             start=False, stop=True).then_inc(m.prior[k], 1)

            @block.gpsimd
            def _(pool):
                with pool.Fori(0, TURNS // 2) as it:
                    for j in range(2):
                        pool.wait_ge(m.idx_ready[j], it + 1)
                        pool.sem_inc(m.turn, 1)
                        for k in range(GR):
                            pool.indirect_dma_start(
                                slot_d, bass.IndirectOffsetOnAxis(ap=idx[:, j, k:k + 1], axis=0), rec_c[:, j, k, :], None,
                                bounds_check=P * TILES - 1, oob_is_err=False).then_inc(m.written[j], 16)
                for j in range(2):
                    pool.wait_ge(m.written[j], (TURNS // 2) * 16 * GR)

        with phase(nc, "slots", "loaded") as (block, m):
            @block.sync
            def _(sp):
                sp.dma_start(g["slots"][:, 0:TILES, :], slot_d.rearrange("(p t) f -> p t f", p=P)).then_inc(m.loaded, 16)
                sp.wait_ge(m.loaded, 16)

            @block.vector
            def _(v):
                v.memset(g["slots"][:, TILES:TILES + BT, :], 99.0)
                v.memset(g["kv"][:, :, :, :], 0.0)


def transposed(pe, src, banks, ident, signal):
    for u in range(CT):
        for k in range(2):
            last = pe.transpose(banks[:, u // 2, (u % 2) * D + k * P:(u % 2) * D + (k + 1) * P],
                                src[:, u, k * P:(k + 1) * P], ident[:, :])
        if u % 2 or u == CT - 1:
            last.then_inc(signal, 1)


def copy_transposed(act, c, banks, dst, ready, copied):
    for b in range(3):
        n = min(2, CT - 2 * b)
        act.wait_ge(ready, c * 3 + (b + 1))
        act.activation(dst[:, :, 2 * b * P:(2 * b + n) * P].rearrange("p k (u n) -> p u k n", u=n),
                       banks[:, b, 0:n * D].rearrange("p (u k n) -> p u k n", u=n, k=2), ACT.Copy).then_inc(copied, 1)


def normalize(v, act, c, src, dst, stats, mv, std, rstd, eps, m):
    for u in range(CT):
        last = v.bn_stats(stats[:, u, :], src(u))
    last.then_inc(m.ln_step, 1)
    v.wait_ge(m.ln_step, c * 4 + 1)
    v.sem_inc(m.turn, 1)
    for u in range(CT):
        last = v.bn_aggr(mv[:, u, :], stats[:, u, :])
    last.then_inc(m.ln_step, 1)
    v.wait_ge(m.std_ready, c + 1)
    v.reciprocal(rstd[:, :], std[:, :]).then_inc(m.ln_step, 1)
    v.wait_ge(m.ln_step, c * 4 + 3)
    for u in range(CT):
        last = v.tensor_scalar(dst[:, u, :], src(u), mv[:, u, 0:1], rstd[:, u:u + 1], ALU.subtract, ALU.mult)
    last.then_inc(m.ln_step, 1)


def deviations(act, c, mv, std, eps, m):
    act.wait_ge(m.ln_step, c * 4 + 2)
    act.activation(std[:, :], mv[:, :, 1], ACT.Sqrt, bias=eps[:, 0:1]).then_inc(m.std_ready, 1)


def ln_buffers(s):
    return s("stats", (P, CT, 6)), s("mv", (P, CT, 2)), s("std", (P, CT)), s("rstd", (P, CT))


def hidden_in(nc, t, sb, pb, g):
    x, hid, ident, eps = g["x"], g["hid"], g["ident"], g["eps"]
    with ExitStack() as st:
        def s(name, shape, dt=F32):
            return sb("hi_" + name, shape, dt, st)
        win, b_in = s("win", (P, 2, D)), s("b_in", (P, D))
        stats, mv, std, rstd = ln_buffers(s)
        xn, xnT = s("xn", (P, CT, D)), s("xnT", (P, 2, CN))
        banks, prod = pb(st, "hi_banks", (P, 3, 512)), pb(st, "hi_prod", (P, 3, 512))
        with phase(nc, "hid", "loaded", "turn", "ln_step", "std_ready", "banks_ready", "copied", "prod_ready", "stored",
                   "x_added") as (block, m):
            @block.sync
            def _(sp):
                sp.dma_start(win[:, :, :], t["Win"]).then_inc(m.loaded, 16)
                sp.dma_start(b_in[:, :], t["b_in"]).then_inc(m.loaded, 16)

            @block.vector
            def _(v):
                v.wait_ge(m.loaded, 32)
                with v.Fori(0, CHUNKS) as c:
                    normalize(v, None, c, lambda u: x[:, bass.ds(c * CT + u, 1), :].rearrange("p a d -> p (a d)"),
                              xn, stats, mv, std, rstd, eps, m)
                    v.wait_ge(m.ln_step, c * 4 + 4)
                    v.tensor_tensor(x[:, bass.ds(c * CT, CT), :], x[:, bass.ds(c * CT, CT), :], xn[:, :, :],
                                    ALU.add).then_inc(m.x_added, 1)
                    for b in range(3):
                        n = min(2, CT - 2 * b)
                        v.wait_ge(m.prod_ready, c * 3 + (b + 1))
                        v.tensor_tensor(hid[:, bass.ds(c * CT + 2 * b, n), :],
                                        prod[:, b, 0:n * D].rearrange("p (u d) -> p u d", u=n),
                                        bc(b_in[:, :], 1, n), ALU.add).then_inc(m.stored, 1)
                    v.wait_ge(m.x_added, c + 1)

            @block.scalar
            def _(act):
                with act.Fori(0, CHUNKS) as c:
                    deviations(act, c, mv, std, eps, m)
                    copy_transposed(act, c, banks, xnT, m.banks_ready, m.copied)

            @block.tensor
            def _(pe):
                pe.wait_ge(m.loaded, 32)
                with pe.Fori(0, CHUNKS) as c:
                    pe.wait_ge(m.ln_step, c * 4 + 4)
                    transposed(pe, xn, banks, ident, m.banks_ready)
                    pe.wait_ge(m.stored, c * 3)
                    for u in range(CT):
                        pe.wait_ge(m.copied, c * 3 + (u // 2 + 1))
                        for k in range(2):
                            last = pe.matmul(prod[:, u // 2, (u % 2) * D:(u % 2 + 1) * D],
                                             xnT[:, k, u * P:(u + 1) * P], win[:, k, :], start=k == 0, stop=k == 1)
                        if u % 2 or u == CT - 1:
                            last.then_inc(m.prod_ready, 1)


def qkv(nc, t, sb, pb, g, layer):
    hid, ident, kv_d, q_d = g["hid"], g["ident"], g["kv_d"], g["q_d"]
    with ExitStack() as st:
        def s(name, shape, dt=F32):
            return sb("qkv_" + name, shape, dt, st)
        wq, wkv = s("wq", (P, 2, 2 * D)), s("wkv", (P, 2, 2 * D))
        bq, bqs, bkv = s("bq", (P, H)), s("bqs", (P, H)), s("bkv", (P, 2 * D))
        hb, hT = s("hb", (P, CT, D)), s("hT", (P, 2, CN))
        kv_row, qs = s("kv_row", (P, CT, 2 * D)), s("qs", (P, CB, 2, HW))
        banks = pb(st, "qkv_banks", (P, 3, 512))
        kv_ps, q_ps = pb(st, "kv_ps", (P, 2, 512)), pb(st, "q_ps", (P, 2, 512))
        with phase(nc, "qkv", "loaded", "hb_ready", "banks_ready", "copied", "kv_ready", "kv_rows", "q_ready", "q_rows",
                   "kv_stored", "q_stored", "bias_ready", "zeroed", "turn") as (block, m):
            @block.sync
            def _(sp):
                sp.dma_start(wkv[:, :, :], t["Wkv"][bass.ds(layer, 1)].rearrange("a p k n -> p (a k) n")).then_inc(m.loaded, 16)
                sp.dma_start(bkv[:, :], t["bkv"][bass.ds(layer, 1)].rearrange("a p n -> p (a n)")).then_inc(m.loaded, 16)
                sp.dma_start(wq[:, :, :], t["Wq"][bass.ds(layer, 1)].rearrange("a p k n -> p (a k) n")).then_inc(m.loaded, 16)
                sp.dma_start(bq[:, :], t["bq"][bass.ds(layer, 1)].rearrange("a p n -> p (a n)")).then_inc(m.loaded, 16)
                kv_rows = kv_d.rearrange("(u p) d -> p u d", p=P)
                q_rows = q_d.rearrange("(b p) c -> p b c", p=P)
                with sp.Fori(0, CHUNKS) as c:
                    sp.wait_ge(m.kv_rows, c * CT + CT)
                    sp.dma_start(kv_rows[:, bass.ds(c * CT, CT), :], kv_row[:, :, :]).then_inc(m.kv_stored, 16)
                    sp.wait_ge(m.q_rows, c * (2 * H) + 2 * H)
                    sp.dma_start(q_rows[:, bass.ds(c * CB, CB), :],
                                 qs[:, :, :, :].rearrange("p b a c -> p b (a c)")).then_inc(m.q_stored, 16)
                sp.wait_ge(m.kv_stored, CHUNKS * 16)
                sp.wait_ge(m.q_stored, CHUNKS * 16)

            @block.gpsimd
            def _(pool):
                pool.memset(qs[0:DH, :, 1, :], 0.0)
                pool.memset(qs[DH:P, :, 0, :], 0.0).then_inc(m.zeroed, 1)
                pool.wait_ge(m.zeroed, 1)
                with pool.Fori(0, CHUNKS) as c:
                    pool.wait_ge(m.copied, c * 3)
                    pool.sem_inc(m.turn, 1)
                    pool.tensor_copy(hb[:, :, :], hid[:, bass.ds(c * CT, CT), :]).then_inc(m.hb_ready, 1)

            @block.vector
            def _(v):
                v.wait_ge(m.loaded, 64)
                with v.Fori(0, CHUNKS) as c:
                    v.wait_ge(m.kv_stored, c * 16)
                    for u in range(CT):
                        v.wait_ge(m.kv_ready, c * CT + (u + 1))
                        v.tensor_tensor(kv_row[:, u, :], kv_ps[:, u % 2, :], bkv[:, :], ALU.add).then_inc(m.kv_rows, 1)

            @block.scalar
            def _(act):
                act.wait_ge(m.loaded, 64)
                act.activation(bqs[:, :], bq[:, :], ACT.Copy, scale=DH ** -0.5).then_inc(m.bias_ready, 1)
                act.wait_ge(m.bias_ready, 1)
                act.wait_ge(m.zeroed, 1)
                with act.Fori(0, CHUNKS) as c:
                    copy_transposed(act, c, banks, hT, m.banks_ready, m.copied)
                    act.wait_ge(m.q_stored, c * 16)
                    for h in range(H):
                        for f in range(2):
                            r = h * 2 + f
                            act.wait_ge(m.q_ready, c * (2 * H) + (r + 1))
                            for a in range(2):
                                last = act.activation(
                                    qs[a * DH:(a + 1) * DH, f * (CB // 2):(f + 1) * (CB // 2), a, h * W:(h + 1) * W],
                                    q_ps[a * DH:(a + 1) * DH, r % 2, 0:HALF].rearrange("p (b w) -> p b w", w=W),
                                    ACT.Identity, bias=bqs[a * DH:(a + 1) * DH, h:h + 1], scale=DH ** -0.5)
                            last.then_inc(m.q_rows, 1)

            @block.tensor
            def _(pe):
                pe.wait_ge(m.loaded, 64)
                with pe.Fori(0, CHUNKS) as c:
                    pe.wait_ge(m.hb_ready, c + 1)
                    transposed(pe, hb, banks, ident, m.banks_ready)
                    pe.wait_ge(m.copied, c * 3 + 3)
                    for u in range(CT):
                        if u < 2:
                            pe.wait_ge(m.kv_rows, c * CT)
                        else:
                            pe.wait_ge(m.kv_rows, c * CT + (u - 1))
                        for k in range(2):
                            last = pe.matmul(kv_ps[:, u % 2, :], hT[:, k, u * P:(u + 1) * P], wkv[:, k, :],
                                             start=k == 0, stop=k == 1)
                        last.then_inc(m.kv_ready, 1)
                    for h in range(H):
                        for f in range(2):
                            r = h * 2 + f
                            if r < 2:
                                pe.wait_ge(m.q_rows, c * (2 * H))
                            else:
                                pe.wait_ge(m.q_rows, c * (2 * H) + (r - 1))
                            for k in range(2):
                                last = pe.matmul(q_ps[:, r % 2, 0:HALF], wq[:, k, h * P:(h + 1) * P],
                                                 hT[:, k, f * HALF:(f + 1) * HALF], start=k == 0, stop=k == 1)
                            last.then_inc(m.q_ready, 1)


def attention_edges(nc, t, sb, pb, g):
    ident, ident_b, iota_w, slots, kv = g["ident"], g["ident_b"], g["iota_w"], g["slots"], g["kv"]
    keep, tile_blk, tile_out, kv_d, q_d, m_d = (g[k] for k in ("keep", "tile_blk", "tile_out", "kv_d", "q_d", "m_d"))
    GH = H * H
    with ExitStack() as st:
        def s(name, shape, dt=F32):
            return sb("ae_" + name, shape, dt, st)
        idx = s("idx", (P, SETS, BT), I32)
        q = s("q", (P, SETS, BT, P))
        sel = s("sel", (P, SETS, BT, W), BF16)
        off = s("off", (P, SETS, BT, W), BF16)
        typ = s("typ", (P, SETS, BT, TYPES), BF16)
        kT = s("kT", (P, BT, 2, P))
        own = s("own", (P, 2, BT, H, H))
        top = s("top", (P, 2, BT, H))
        low = s("low", (P, 2, BT, H, H))
        ex = s("ex", (P, 2, BT, H, H))
        z = s("z", (P, 2, BT, H))
        rz = s("rz", (P, 2, BT, H))
        att = s("att", (P, 2, BT, H, H))
        wgt = s("wgt", (P, 2, BT, GH, W))
        acc = s("acc", (MR, SETS, BT, HW))
        kT_ps = pb(st, "kT_ps", (P, BT, 2, P))
        sc_ps = pb(st, "sc_ps", (P, 2, BT, GH * W))
        out_ps = pb(st, "out_ps", (P, 2, 512))
        with phase(nc, "ae", "idx_ready", "turn", "kv_loaded*4", "q_loaded*4", "sel_step", "sel_ready", "kT_ready", "kT_copied",
                   "scores_ready", "own_ready", "top_ready", "low_ready", "exp_ready", "z_ready", "rz_ready",
                   "att_ready", "weights_ready", "sums_ready", "acc_ready", "sums_stored*4") as (block, m):

            @block.gpsimd
            def _(pool):
                def step(b, n, k):
                    if after(b, SETS):
                        pool.wait_ge(m.sums_ready, b - SETS + 1)
                        pool.sem_inc(m.turn, 1)
                    pool.tensor_copy(idx[:, k, :], slots[:, bass.ds(b * BT, BT), 0]).then_inc(m.idx_ready, 1)
                    pool.wait_ge(m.idx_ready, b + 1)
                    pool.sem_inc(m.turn, 1)
                    for u in range(BT):
                        pool.indirect_dma_start(
                            kv[:, k, u, :], None, kv_d, bass.IndirectOffsetOnAxis(ap=idx[:, k, u:u + 1], axis=0),
                            bounds_check=NP_ - 1, oob_is_err=False).then_inc(m.kv_loaded[k], 16)
                batches(pool, 0, BATCHES, SETS, step)

            @block.sync
            def _(sp):
                def load(b, n, k):
                    rows = [sp.value_load(tile_blk[0:1, bass.ds(b * BT + u, 1)], min_val=0, max_val=BLOCKS - 1)
                            for u in range(BT)]
                    if after(b, SETS):
                        sp.wait_ge(m.scores_ready, (b - SETS) * 2 + 2)
                    for u in range(BT):
                        sp.dma_start(q[:, k, u, :], q_d[bass.ds(rows[u] * P, P), :]).then_inc(m.q_loaded[k], 16)

                def store(b, n, k):
                    rows = [sp.value_load(tile_out[0:1, bass.ds(b * BT + u, 1)], min_val=0, max_val=BLOCKS + TILES - 1)
                            for u in range(BT)]
                    sp.wait_ge(m.acc_ready, (b + 1) * BT)
                    for u in range(BT):
                        sp.dma_start(m_d[bass.ds(rows[u] * MR, MR), :], acc[:, k, u, :]).then_inc(m.sums_stored[k], 16)

                LAG = SETS + 2

                def step(b, n, k):
                    load(b, n, k)
                    if after(b, LAG):
                        store(b - LAG, None, (k - LAG) % SETS)
                batches(sp, 0, BATCHES, LAG, step)
                for b in range(BATCHES - LAG, BATCHES):
                    store(b, None, b % SETS)
                for k in range(SETS):
                    sp.wait_ge(m.sums_stored[k], 16 * BT * len(range(k, BATCHES, SETS)))

            @block.scalar
            def _(act):
                def copies(b):
                    for f in range(2):
                        act.wait_ge(m.kT_ready, b * 2 + (f + 1))
                        act.activation(kT[:, 2 * f:2 * f + 2, :, :], kT_ps[:, 2 * f:2 * f + 2, :, :],
                                       ACT.Copy).then_inc(m.kT_copied, 1)

                def step(b, n, k):
                    if not isinstance(b, int) or b + 1 < BATCHES:
                        copies(b + 1)
                    act.wait_ge(m.low_ready, b + 1)
                    act.activation(ex[:, k % 2, :, :, :], low[:, k % 2, :, :, :], ACT.Exp).then_inc(m.exp_ready, 1)
                copies(0)
                batches(act, 0, BATCHES - 1, 1, step)
                step(BATCHES - 1, None, (BATCHES - 1) % SETS)

            @block.vector
            def _(v):
                def select(b, k):
                    v.tensor_tensor(sel[:, k, :, :], bc(iota_w[:, :], 1, BT),
                                    bc(slots[:, bass.ds(b * BT, BT), 1], 2, W), ALU.is_equal).then_inc(m.sel_step, 1)
                    v.tensor_tensor(typ[:, k, :, :], bc(iota_w[:, 0:TYPES], 1, BT),
                                    bc(slots[:, bass.ds(b * BT, BT), 2], 2, TYPES), ALU.is_equal)
                    v.wait_ge(m.sel_step, b + 1)
                    v.tensor_scalar(off[:, k, :, :], sel[:, k, :, :], BIG, -BIG, ALU.mult, ALU.add).then_inc(m.sel_ready, 1)

                def accumulate(b, k, u):
                    prev = acc[:, k, u - 1, :] if u else acc[:, (k - 1) % SETS, BT - 1, :]
                    v.scalar_tensor_tensor(acc[:, k, u, :], prev, keep[0:MR, bass.ds(b * BT + u, 1)],
                                           out_ps[0:MR, k % 2, u * HW:(u + 1) * HW], ALU.mult, ALU.add).then_inc(m.acc_ready, 1)

                def acc_waits(b, n, k):
                    v.wait_ge(m.sums_ready, b + 1)
                    if after(b, SETS):
                        v.wait_ge(m.sums_stored[k], n * (16 * BT))

                def step(b, n, k):
                    j = k % 2
                    for f in range(2):
                        v.wait_ge(m.scores_ready, b * 2 + (f + 1))
                        v.tensor_reduce(own[:, j, 2 * f:2 * f + 2, :, :].rearrange("p u g h -> p (u g h)"),
                                        sc_ps[:, j, 2 * f:2 * f + 2, :].rearrange("p u (x w) -> p (u x) w", w=W),
                                        axis=AX.X, op=ALU.max).then_inc(m.own_ready, 1)
                    v.wait_ge(m.own_ready, b * 2 + 2)
                    v.tensor_reduce(top[:, j, :, :], own[:, j, :, :, :].rearrange("p u g h -> p u h g"),
                                    axis=AX.X, op=ALU.max).then_inc(m.top_ready, 1)
                    v.wait_ge(m.top_ready, b + 1)
                    v.tensor_tensor(low[:, j, :, :, :], own[:, j, :, :, :], bc(top[:, j, :, :], 2, H),
                                    ALU.subtract).then_inc(m.low_ready, 1)
                    select(b + 1, (k + 1) % SETS)
                    old = after(b, 2)
                    if old:
                        bo, no, ko = b - 2, n if k >= 2 else n - 1, (k - 2) % SETS
                        acc_waits(bo, no, ko)
                        v.wait_ge(m.acc_ready, bo * BT)
                        accumulate(bo, ko, 0)
                    v.wait_ge(m.exp_ready, b + 1)
                    v.tensor_reduce(z[:, j, :, :], ex[:, j, :, :, :].rearrange("p u g h -> p u h g"),
                                    axis=AX.X, op=ALU.add).then_inc(m.z_ready, 1)
                    if old:
                        v.wait_ge(m.acc_ready, bo * BT + 1)
                        accumulate(bo, ko, 1)
                    v.wait_ge(m.z_ready, b + 1)
                    v.reciprocal(rz[:, j, :, :], z[:, j, :, :]).then_inc(m.rz_ready, 1)
                    if old:
                        v.wait_ge(m.acc_ready, bo * BT + 2)
                        accumulate(bo, ko, 2)
                    v.wait_ge(m.rz_ready, b + 1)
                    v.tensor_tensor(att[:, j, :, :, :], ex[:, j, :, :, :], bc(rz[:, j, :, :], 2, H),
                                    ALU.mult).then_inc(m.att_ready, 1)
                    if old:
                        v.wait_ge(m.acc_ready, bo * BT + 3)
                        accumulate(bo, ko, 3)
                    v.wait_ge(m.att_ready, b + 1)
                    for f in range(2):
                        v.tensor_tensor(wgt[:, j, 2 * f:2 * f + 2, :, :],
                                        bc(att[:, j, 2 * f:2 * f + 2, :, :].rearrange("p u g h -> p u (g h)"), 3, W),
                                        bc(sel[:, k, 2 * f:2 * f + 2, :], 2, GH), ALU.mult).then_inc(m.weights_ready, 1)

                v.memset(acc[:, SETS - 1, BT - 1, :], 0.0)
                select(0, 0)
                batches(v, 0, BATCHES, 2, step)
                for b in (BATCHES - 2, BATCHES - 1):
                    acc_waits(b, b // SETS, b % SETS)
                    for u in range(BT):
                        v.wait_ge(m.acc_ready, b * BT + u)
                        accumulate(b, b % SETS, u)

            @block.tensor
            def _(pe):
                def transposes(b, n, k):
                    pe.wait_ge(m.kv_loaded[k], n * (16 * BT) + 16 * BT)
                    for u in range(BT):
                        for i in range(2):
                            last = pe.transpose(kT_ps[:, u, i, :], kv[:, k, u, i * P:(i + 1) * P], ident[:, :])
                        if u % 2:
                            last.then_inc(m.kT_ready, 1)

                def scores(b, n, k):
                    pe.wait_ge(m.sel_ready, b + 1)
                    pe.wait_ge(m.q_loaded[k], n * (16 * BT) + 16 * BT)
                    for u in range(BT):
                        pe.matmul(sc_ps[:, k % 2, u, :], ident_b[:, :], bc(off[:, k, u, :], 1, GH), start=True, stop=False)
                        if u % 2 == 0:
                            pe.wait_ge(m.kT_copied, b * 2 + (u // 2 + 1))
                        for i in range(2):
                            last = pe.matmul(sc_ps[:, k % 2, u, i * P:(i + 1) * P], kT[:, u, i, :], q[:, k, u, :],
                                             start=False, stop=i == 1)
                        if u % 2:
                            last.then_inc(m.scores_ready, 1)

                def sums(b, n, k):
                    for u in range(BT):
                        if u % 2 == 0:
                            pe.wait_ge(m.weights_ready, b * 2 + (u // 2 + 1))
                        for i in range(H):
                            pe.matmul(out_ps[0:DH, k % 2, u * HW:(u + 1) * HW], kv[:, k, u, D + i * DH:D + (i + 1) * DH],
                                      wgt[:, k % 2, u, i * H:(i + 1) * H, :].rearrange("p h w -> p (h w)"),
                                      start=i == 0, stop=i == H - 1)
                        last = pe.matmul(out_ps[DH:MR, k % 2, u * HW:(u + 1) * HW], typ[:, k, u, :],
                                         bc(sel[:, k, u, :], 1, H), start=True, stop=True)
                    last.then_inc(m.sums_ready, 1)

                def step(b, n, k):
                    scores(b, n, k)
                    if not isinstance(b, int) or b + 1 < BATCHES:
                        transposes(b + 1, n + 1 if k == SETS - 1 else n, (k + 1) % SETS)
                    if after(b, 1):
                        sums(b - 1, None, (k - 1) % SETS)

                transposes(0, 0, 0)
                batches(pe, 0, BATCHES - 1, 1, step)
                step(BATCHES - 1, (BATCHES - 1) // SETS, (BATCHES - 1) % SETS)
                sums(BATCHES - 1, None, (BATCHES - 1) % SETS)


def node_update(nc, t, sb, pb, g, layer):
    hid, eps, m_d = g["hid"], g["eps"], g["m_d"]
    with ExitStack() as st:
        def s(name, shape, dt=F32):
            return sb("nu_" + name, shape, dt, st)
        wo, ee, ew, bo = s("wo", (DH, H, D)), s("ee", (DH, H, 3)), s("ew", (DH + 3, D)), s("bo", (DH + 3, D))
        gam, bet = s("gam", (P, D)), s("bet", (P, D))
        sums, sumsT = s("sums", (MR, CB, H, W)), s("sumsT", (MR, H, CN))
        stats, mv, std, rstd = ln_buffers(s)
        y, yn = s("y", (P, CT, D)), s("yn", (P, CT, D))
        ew_ps, prod = pb(st, "ew_ps", (P, 512)), pb(st, "nu_prod", (P, 3, 512))
        with phase(nc, "nu", "loaded", "ew_ready", "ew_done", "sums_loaded", "sums_laid", "prod_ready", "added", "turn", "ln_step", "std_ready",
                   "scaled", "shifted", "done") as (block, m):
            @block.sync
            def _(sp):
                one = bass.ds(layer, 1)
                sp.dma_start(wo[:, :, :], t["Wo"][one].rearrange("a p h n -> p (a h) n")).then_inc(m.loaded, 16)
                sp.dma_start(ee[:, :, :], t["Ee"][one].rearrange("a p h n -> p (a h) n")).then_inc(m.loaded, 16)
                sp.dma_start(bo[DH:DH + 3, :], t["bo"][one].rearrange("a p n -> p (a n)")).then_inc(m.loaded, 16)
                sp.dma_start(gam[:, :], t["ln_g"][one].rearrange("a p n -> p (a n)")).then_inc(m.loaded, 16)
                sp.dma_start(bet[:, :], t["ln_b"][one].rearrange("a p n -> p (a n)")).then_inc(m.loaded, 16)
                rows = m_d.rearrange("(b r) c -> r b c", r=MR)
                with sp.Fori(0, CHUNKS) as c:
                    sp.wait_ge(m.sums_laid, c)
                    sp.dma_start(sums[:, :, :, :].rearrange("r b h w -> r b (h w)"), rows[:, bass.ds(c * CB, CB), :]).then_inc(m.sums_loaded, 16)

            @block.tensor
            def _(pe):
                pe.wait_ge(m.loaded, 80)
                for h in range(H):
                    last = pe.matmul(ew_ps[DH:DH + 3, 0:D], ee[:, h, :], wo[:, h, :], start=h == 0, stop=h == H - 1)
                last.then_inc(m.ew_ready, 1)
                pe.wait_ge(m.ew_done, 1)
                with pe.Fori(0, CHUNKS) as c:
                    pe.wait_ge(m.sums_laid, c + 1)
                    pe.wait_ge(m.added, c * 3)
                    for u in range(CT):
                        o = prod[:, u // 2, (u % 2) * D:(u % 2 + 1) * D]
                        for h in range(H):
                            pe.matmul(o, sumsT[0:DH, h, u * P:(u + 1) * P], wo[:, h, :],
                                      start=h == 0, stop=False)
                        last = pe.matmul(o, sumsT[DH:DH + 3, 0, u * P:(u + 1) * P], ew[DH:DH + 3, :],
                                         start=False, stop=True)
                        if u % 2 or u == CT - 1:
                            last.then_inc(m.prod_ready, 1)

            @block.vector
            def _(v):
                v.wait_ge(m.loaded, 80)
                v.wait_ge(m.ew_ready, 1)
                v.tensor_tensor(ew[DH:DH + 3, :], ew_ps[DH:DH + 3, 0:D], bo[DH:DH + 3, :], ALU.add).then_inc(m.ew_done, 1)
                with v.Fori(0, CHUNKS) as c:
                    for b in range(3):
                        n = min(2, CT - 2 * b)
                        v.wait_ge(m.prod_ready, c * 3 + (b + 1))
                        v.tensor_tensor(y[:, 2 * b:2 * b + n, :], prod[:, b, 0:n * D].rearrange("p (u d) -> p u d", u=n),
                                        hid[:, bass.ds(c * CT + 2 * b, n), :], ALU.add).then_inc(m.added, 1)
                    v.wait_ge(m.added, c * 3 + 3)
                    normalize(v, None, c, lambda u: y[:, u, :], yn, stats, mv, std, rstd, eps, m)
                    v.wait_ge(m.ln_step, c * 4 + 4)
                    v.tensor_tensor(y[:, :, :], yn[:, :, :], bc(gam[:, :], 1, CT), ALU.mult).then_inc(m.scaled, 1)
                    v.wait_ge(m.scaled, c + 1)
                    v.wait_ge(m.done, c)
                    v.tensor_tensor(yn[:, :, :], y[:, :, :], bc(bet[:, :], 1, CT), ALU.add).then_inc(m.shifted, 1)
                    v.wait_ge(m.done, c + 1)

            @block.scalar
            def _(act):
                with act.Fori(0, CHUNKS) as c:
                    act.wait_ge(m.sums_loaded, c * 16 + 16)
                    act.wait_ge(m.prod_ready, c * 3)
                    act.activation(sumsT[:, :, :].rearrange("r h (b w) -> r b h w", w=W), sums[:, :, :, :],
                                   ACT.Copy).then_inc(m.sums_laid, 1)
                    deviations(act, c, mv, std, eps, m)
                    act.wait_ge(m.shifted, c + 1)
                    act.activation(hid[:, bass.ds(c * CT, CT), :], yn[:, :, :], ACT.Relu).then_inc(m.done, 1)


def adjustment(nc, t, sb, pb, g):
    x, hid, ident = g["x"], g["hid"], g["ident"]
    with ExitStack() as st:
        def s(name, shape, dt=F32):
            return sb("ad_" + name, shape, dt, st)
        a1w, a2w, a1, a2 = s("w1", (P, 2, D)), s("w2", (P, 2, D)), s("b1", (P, 2)), s("b2", (P, D))
        hb, hT, u1T, y = s("hb", (P, CT, D)), s("hT", (P, 2, CN)), s("u1T", (P, 2, CN)), s("y", (P, CT, D))
        banks, u_ps, prod = pb(st, "ad_banks", (P, 3, 512)), pb(st, "ad_u", (P, 2, 512)), pb(st, "ad_prod", (P, 3, 512))
        with phase(nc, "ad", "loaded", "hb_ready", "turn", "banks_ready", "copied", "u_ready", "relu_ready", "prod_ready",
                   "biased", "added") as (block, m):
            @block.sync
            def _(sp):
                for a, b in ((a1w[:, :, :], "A1"), (a2w[:, :, :], "A2"), (a1[:, :], "a1"), (a2[:, :], "a2")):
                    sp.dma_start(a, t[b]).then_inc(m.loaded, 16)

            @block.gpsimd
            def _(pool):
                with pool.Fori(0, CHUNKS) as c:
                    pool.wait_ge(m.copied, c * 3)
                    pool.sem_inc(m.turn, 1)
                    pool.tensor_copy(hb[:, :, :], hid[:, bass.ds(c * CT, CT), :]).then_inc(m.hb_ready, 1)

            @block.scalar
            def _(act):
                act.wait_ge(m.loaded, 64)
                with act.Fori(0, CHUNKS) as c:
                    copy_transposed(act, c, banks, hT, m.banks_ready, m.copied)
                    act.wait_ge(m.prod_ready, c * 3)
                    for r in range(4):
                        act.wait_ge(m.u_ready, c * 4 + (r + 1))
                        act.activation(u1T[:, r // 2, (r % 2) * HALF:(r % 2 + 1) * HALF], u_ps[:, r % 2, 0:HALF], ACT.Relu,
                                       bias=a1[:, r // 2:r // 2 + 1]).then_inc(m.relu_ready, 1)

            @block.vector
            def _(v):
                v.wait_ge(m.loaded, 64)
                with v.Fori(0, CHUNKS) as c:
                    v.wait_ge(m.added, c)
                    for b in range(3):
                        n = min(2, CT - 2 * b)
                        v.wait_ge(m.prod_ready, c * 3 + (b + 1))
                        v.tensor_tensor(y[:, 2 * b:2 * b + n, :], prod[:, b, 0:n * D].rearrange("p (u d) -> p u d", u=n),
                                        bc(a2[:, :], 1, n), ALU.add).then_inc(m.biased, 1)
                    v.wait_ge(m.biased, c * 3 + 3)
                    v.tensor_tensor(x[:, bass.ds(c * CT, CT), :], x[:, bass.ds(c * CT, CT), :], y[:, :, :],
                                    ALU.add).then_inc(m.added, 1)
                v.wait_ge(m.added, CHUNKS)

            @block.tensor
            def _(pe):
                pe.wait_ge(m.loaded, 64)
                with pe.Fori(0, CHUNKS) as c:
                    pe.wait_ge(m.hb_ready, c + 1)
                    transposed(pe, hb, banks, ident, m.banks_ready)
                    pe.wait_ge(m.copied, c * 3 + 3)
                    for r in range(4):
                        pe.wait_ge(m.relu_ready, c * 4 if r < 2 else c * 4 + (r - 1))
                        for k in range(2):
                            last = pe.matmul(u_ps[:, r % 2, 0:HALF], a1w[:, k, (r // 2) * P:(r // 2 + 1) * P],
                                             hT[:, k, (r % 2) * HALF:(r % 2 + 1) * HALF], start=k == 0, stop=k == 1)
                        last.then_inc(m.u_ready, 1)
                    pe.wait_ge(m.relu_ready, c * 4 + 4)
                    pe.wait_ge(m.biased, c * 3)
                    for u in range(CT):
                        for k in range(2):
                            last = pe.matmul(prod[:, u // 2, (u % 2) * D:(u % 2 + 1) * D], u1T[:, k, u * P:(u + 1) * P],
                                             a2w[:, k, :], start=k == 0, stop=k == 1)
                        if u % 2 or u == CT - 1:
                            last.then_inc(m.prod_ready, 1)


def expert_ffn(nc, t, sb, pb, g):
    x, ident, ident_b, eps = g["x"], g["ident"], g["ident_b"], g["eps"]
    with ExitStack() as st:
        def s(name, shape, dt=F32):
            return sb("ex_" + name, shape, dt, st)
        e1w, e2w, e1, e2 = s("w1", (P, 2, EX0 * H0)), s("w2", (P, HC, D)), s("b1", (P, HC)), s("b2", (EX0, D))
        rw, rb, iota = s("rw", (P, 2, EX0)), s("rb", (P, EX0)), s("iota", (P, EX0))
        owner, owner_b = s("owner", (EX0, HC, P)), s("owner_b", (EX0, HC, P), BF16)
        stats, mv, std, rstd = ln_buffers(s)
        xn, xnT = s("xn", (P, CT, D)), s("xnT", (P, 2, CN))
        lg, eq, best, first = s("lg", (P, CT, EX0)), s("eq", (P, CT, EX0)), s("best", (P, CT)), s("first", (P, CT))
        hot = s("hot", (P, CT, EX0), BF16)
        hotT, offT = s("hotT", (EX0, CN)), s("offT", (EX0, CN), BF16)
        hs = s("hs", (P, 2, CN))
        out_ps = pb(st, "ex_out", (P, CT, 512))
        h_ps, lg_ps = pb(st, "ex_h", (P, 2, 512)), pb(st, "ex_lgp", (P, 512))
        SPLIT = (range(0, 3), range(3, CT))
        with phase(nc, "ex", "loaded", "turn", "ln_step", "std_ready", "banks_ready", "copied", "logits_ready", "pick",
                   "hot_ready", "hotT_ready", "off_ready", "h_ready", "relu_ready", "out_step", "added") as (block, m):
            @block.sync
            def _(sp):
                for a, b in ((rw[:, :, :], "router_w"), (rb[:, :], "router_b"), (iota[:, :], "c_iota_e"), (e1w[:, :, :], "E1"),
                             (e1[:, :], "e1"), (owner[:, :, :], "c_owner"), (e2w[:, :, :], "E2"), (e2[:, :], "e2")):
                    sp.dma_start(a, t[b]).then_inc(m.loaded, 16)

            @block.vector
            def _(v):
                v.wait_ge(m.loaded, 128)
                v.tensor_single_scalar(iota[:, :], iota[:, :], -float(EX0), ALU.add).then_inc(m.turn, 1)
                v.wait_ge(m.turn, 1)
                with v.Fori(0, CHUNKS) as c:
                    normalize(v, None, c, lambda u: x[:, bass.ds(c * CT + u, 1), :].rearrange("p a d -> p (a d)"),
                              xn, stats, mv, std, rstd, eps, m)
                    v.wait_ge(m.logits_ready, c + 1)
                    v.tensor_tensor(lg[:, :, :], lg_ps[:, 0:CT * EX0].rearrange("p (u e) -> p u e", u=CT),
                                    bc(rb[:, :], 1, CT), ALU.add).then_inc(m.pick, 1)
                    v.wait_ge(m.pick, c * 5 + 1)
                    v.tensor_reduce(best[:, :], lg[:, :, :], axis=AX.X, op=ALU.max).then_inc(m.pick, 1)
                    v.wait_ge(m.pick, c * 5 + 2)
                    v.tensor_tensor(eq[:, :, :], lg[:, :, :], bc(best[:, :], 2, EX0), ALU.is_equal).then_inc(m.pick, 1)
                    v.wait_ge(m.pick, c * 5 + 3)
                    v.tensor_tensor(lg[:, :, :], eq[:, :, :], bc(iota[:, :], 1, CT), ALU.mult).then_inc(m.pick, 1)
                    v.wait_ge(m.pick, c * 5 + 4)
                    v.tensor_reduce(first[:, :], lg[:, :, :], axis=AX.X, op=ALU.min).then_inc(m.pick, 1)
                    v.wait_ge(m.pick, c * 5 + 5)
                    v.tensor_tensor(hot[:, :, :], bc(first[:, :], 2, EX0), bc(iota[:, :], 1, CT),
                                    ALU.is_equal).then_inc(m.hot_ready, 1)
                    v.wait_ge(m.out_step, c * HC + HC)
                    for u in range(CT):
                        xu = x[:, bass.ds(c * CT + u, 1), :].rearrange("p a d -> p (a d)")
                        v.scalar_tensor_tensor(xu, out_ps[:, u, 0:D], 0.0, xu, ALU.max, ALU.add).then_inc(m.added, 1)
                v.wait_ge(m.added, CHUNKS * CT)

            @block.scalar
            def _(act):
                act.wait_ge(m.loaded, 128)
                act.activation(owner_b[:, :, :], owner[:, :, :], ACT.Copy, scale=BIG).then_inc(m.off_ready, 1)
                with act.Fori(0, CHUNKS) as c:
                    deviations(act, c, mv, std, eps, m)
                    copy_transposed(act, c, out_ps, xnT, m.banks_ready, m.copied)
                    for f, us in enumerate(SPLIT):
                        act.wait_ge(m.hotT_ready, c * 2 + (f + 1))
                        cols = slice(us[0] * P, (us[-1] + 1) * P)
                        act.activation(hotT[:, cols], h_ps[0:EX0, f, 0:len(us) * P], ACT.Copy)
                        act.activation(offT[:, cols], h_ps[0:EX0, f, 0:len(us) * P], ACT.Copy, bias=-1.0).then_inc(m.off_ready, 1)
                    for j in range(HC):
                        act.wait_ge(m.out_step, c * HC if j < 2 else c * HC + (j - 1))
                        for f in range(2):
                            act.wait_ge(m.h_ready, c * (2 * HC) + (2 * j + f + 1))
                            act.activation(hs[:, j % 2, f * HALF:(f + 1) * HALF], h_ps[:, f, 0:HALF], ACT.Relu,
                                           bias=e1[:, j:j + 1]).then_inc(m.relu_ready, 1)

            @block.tensor
            def _(pe):
                pe.wait_ge(m.loaded, 128)
                with pe.Fori(0, CHUNKS) as c:
                    pe.wait_ge(m.ln_step, c * 4 + 4)
                    pe.wait_ge(m.added, c * CT)
                    transposed(pe, xn, out_ps, ident, m.banks_ready)
                    pe.wait_ge(m.copied, c * 3 + 3)
                    for u in range(CT):
                        for k in range(2):
                            last = pe.matmul(lg_ps[:, u * EX0:(u + 1) * EX0], xnT[:, k, u * P:(u + 1) * P], rw[:, k, :],
                                             start=k == 0, stop=k == 1)
                    last.then_inc(m.logits_ready, 1)
                    pe.wait_ge(m.hot_ready, c + 1)
                    pe.wait_ge(m.relu_ready, c * (2 * HC))
                    for f, us in enumerate(SPLIT):
                        for n, u in enumerate(us):
                            last = pe.matmul(h_ps[0:EX0, f, n * P:(n + 1) * P], hot[:, u, :], ident_b[:, :], start=True, stop=True)
                        last.then_inc(m.hotT_ready, 1)
                    pe.wait_ge(m.off_ready, c * 2 + 3)

                    def second(j):
                        pe.wait_ge(m.relu_ready, c * (2 * HC) + (2 * j + 2))
                        for u in range(CT):
                            last = pe.matmul(out_ps[:, u, 0:D], hs[:, j % 2, u * P:(u + 1) * P], e2w[:, j, :],
                                             start=False, stop=j == HC - 1)
                        last.then_inc(m.out_step, 1)

                    for u in range(CT):
                        pe.matmul(out_ps[:, u, 0:D], hotT[:, u * P:(u + 1) * P], e2[:, :], start=True, stop=False)
                    for j in range(HC):
                        for f in range(2):
                            if j:
                                pe.wait_ge(m.relu_ready, c * (2 * HC) + (2 * j + f - 1))
                            cols = slice(f * HALF, (f + 1) * HALF)
                            pe.matmul(h_ps[:, f, 0:HALF], owner_b[:, j, :], offT[:, cols], start=True, stop=False)
                            for k in range(2):
                                last = pe.matmul(h_ps[:, f, 0:HALF], e1w[:, k, j * P:(j + 1) * P], xnT[:, k, cols],
                                                 start=False, stop=k == 1)
                            last.then_inc(m.h_ready, 1)
                        if j:
                            second(j - 1)
                    second(HC - 1)


def features(nc, t, sb, pb, g):
    x, ident, eps, f_d, as_d = g["x"], g["ident"], g["eps"], g["f_d"], g["as_d"]
    with ExitStack() as st:
        def s(name, shape, dt=F32):
            return sb("fe_" + name, shape, dt, st)
        ws, bs = s("ws", (P, 2, D)), s("bs", (P, D))
        aws, awd = s("aws", (P, D)), s("awd", (P, D))
        stats, mv, std, rstd = ln_buffers(s)
        xn, xnT = s("xn", (P, CT, D)), s("xnT", (P, 2, CN))
        row, tmp, a_src = s("row", (P, CT, FROW)), s("tmp", (P, 2, CT * H, DH)), s("a_src", (P, CT * H))
        banks, prod = pb(st, "fe_banks", (P, 3, 512)), pb(st, "fe_prod", (P, 3, 512))
        heads = row[:, :, 0:H * FR].rearrange("p u (h c) -> p u h c", c=FR)
        with phase(nc, "fe", "loaded", "turn", "ln_step", "std_ready", "banks_ready", "copied", "prod_ready", "biased", "weighted",
                   "rows_ready", "rows_stored", "ones_ready") as (block, m):
            @block.sync
            def _(sp):
                for a, b in ((ws[:, :, :], "Ws"), (bs[:, :], "bs"), (aws[:, :], "aw_s"), (awd[:, :], "aw_d")):
                    sp.dma_start(a, t[b]).then_inc(m.loaded, 16)
                f_rows = f_d.rearrange("(u p) c -> p u c", p=P)
                as_rows = as_d.rearrange("b (w h) -> (b w) h", h=H).rearrange("(u p) h -> p u h", p=P)
                with sp.Fori(0, CHUNKS) as c:
                    sp.wait_ge(m.rows_ready, c * 2 + 2)
                    sp.dma_start(f_rows[:, bass.ds(c * CT, CT), :], row[:, :, :]).then_inc(m.rows_stored, 16)
                    sp.dma_start(as_rows[:, bass.ds(c * CT, CT), :],
                                 a_src[:, :].rearrange("p (u h) -> p u h", h=H)).then_inc(m.rows_stored, 16)
                sp.wait_ge(m.rows_stored, CHUNKS * 32)

            @block.gpsimd
            def _(pool):
                pool.memset(heads[:, :, :, DH], 1.0).then_inc(m.ones_ready, 1)

            @block.vector
            def _(v):
                v.wait_ge(m.loaded, 64)
                v.wait_ge(m.ones_ready, 1)
                with v.Fori(0, CHUNKS) as c:
                    normalize(v, None, c, lambda u: x[:, bass.ds(c * CT + u, 1), :].rearrange("p a d -> p (a d)"),
                              xn, stats, mv, std, rstd, eps, m)
                    v.wait_ge(m.rows_stored, c * 32)
                    for b in range(3):
                        n = min(2, CT - 2 * b)
                        v.wait_ge(m.prod_ready, c * 3 + (b + 1))
                        for u in range(2 * b, 2 * b + n):
                            last = v.tensor_tensor(heads[:, u, :, 0:DH],
                                                   prod[:, b, (u % 2) * D:(u % 2 + 1) * D].rearrange("p (h d) -> p h d", h=H),
                                                   bs[:, :].rearrange("p (h d) -> p h d", h=H), ALU.add)
                        last.then_inc(m.biased, 1)
                    v.wait_ge(m.biased, c * 3 + 3)
                    for a, aw in enumerate((aws, awd)):
                        for u in range(CT):
                            last = v.tensor_tensor(tmp[:, a, u * H:(u + 1) * H, :], heads[:, u, :, 0:DH],
                                                   aw[:, :].rearrange("p (h d) -> p h d", h=H), ALU.mult)
                        last.then_inc(m.weighted, 1)
                    v.wait_ge(m.weighted, c * 2 + 1)
                    v.tensor_reduce(a_src[:, :], tmp[:, 0, :, :], axis=AX.X, op=ALU.add).then_inc(m.rows_ready, 1)
                    v.wait_ge(m.weighted, c * 2 + 2)
                    v.tensor_reduce(row[:, :, H * FR:FROW], tmp[:, 1, :, :].rearrange("p (u h) d -> p u h d", h=H),
                                    axis=AX.X, op=ALU.add).then_inc(m.rows_ready, 1)
                    v.wait_ge(m.rows_ready, c * 2 + 2)

            @block.scalar
            def _(act):
                with act.Fori(0, CHUNKS) as c:
                    deviations(act, c, mv, std, eps, m)
                    copy_transposed(act, c, banks, xnT, m.banks_ready, m.copied)

            @block.tensor
            def _(pe):
                pe.wait_ge(m.loaded, 64)
                with pe.Fori(0, CHUNKS) as c:
                    pe.wait_ge(m.ln_step, c * 4 + 4)
                    transposed(pe, xn, banks, ident, m.banks_ready)
                    pe.wait_ge(m.biased, c * 3)
                    for u in range(CT):
                        pe.wait_ge(m.copied, c * 3 + (u // 2 + 1))
                        for k in range(2):
                            last = pe.matmul(prod[:, u // 2, (u % 2) * D:(u % 2 + 1) * D],
                                             xnT[:, k, u * P:(u + 1) * P], ws[:, k, :], start=k == 0, stop=k == 1)
                        if u % 2 or u == CT - 1:
                            last.then_inc(m.prod_ready, 1)


def pooling_edges(nc, t, sb, pb, g):
    ident_b, iota_w, slots = g["ident_b"], g["iota_w"], g["slots"]
    keep, tile_blk, tile_out, f_d, as_d, p_d = (g[k] for k in ("keep", "tile_blk", "tile_out", "f_d", "as_d", "p_d"))
    feat = g["kv"][:, :, :, 0:FROW]
    with ExitStack() as st:
        def s(name, shape, dt=F32):
            return sb("pe_" + name, shape, dt, st)
        idx = s("idx", (P, SETS, BT), I32)
        a_src = s("a_src", (1, SETS, BT, HW))
        ones = s("ones", (1, P))
        awe, ab = s("awe", (P, H)), s("ab", (P, H))
        sel = s("sel", (P, SETS, BT, W), BF16)
        off = s("off", (P, SETS, BT, W), BF16)
        edge = s("edge", (P, SETS, BT, H))
        own = s("own", (P, 2, BT, H))
        part = s("part", (P, 2, BT, H))
        low = s("low", (P, 2, BT, H))
        ex = s("ex", (P, 2, BT, H))
        wgt = s("wgt", (P, 2, BT, H, W))
        acc = s("acc", (PR, SETS, BT, HW))
        sc_ps, out_ps = pb(st, "pe_sc", (P, 2, 512)), pb(st, "pe_out", (P, 2, 512))
        with phase(nc, "pe", "loaded", "const_ready", "turn", "idx_ready", "feat_loaded*4", "src_loaded*4", "sel_step", "edge_step",
                   "sel_ready", "scores_ready", "own_ready", "part_ready", "sum_ready", "low_ready", "exp_ready", "weights_ready",
                   "sums_ready", "acc_ready", "sums_stored*4") as (block, m):

            @block.gpsimd
            def _(pool):
                def step(b, n, k):
                    if after(b, SETS):
                        pool.wait_ge(m.sums_ready, b - SETS + 1)
                        pool.sem_inc(m.turn, 1)
                    pool.tensor_copy(idx[:, k, :], slots[:, bass.ds(b * BT, BT), 0]).then_inc(m.idx_ready, 1)
                    pool.wait_ge(m.idx_ready, b + 1)
                    pool.sem_inc(m.turn, 1)
                    for u in range(BT):
                        pool.indirect_dma_start(
                            feat[:, k, u, :], None, f_d, bass.IndirectOffsetOnAxis(ap=idx[:, k, u:u + 1], axis=0),
                            bounds_check=NP_ - 1, oob_is_err=False).then_inc(m.feat_loaded[k], 16)
                batches(pool, 0, BATCHES, SETS, step)

            @block.sync
            def _(sp):
                sp.dma_start(awe[:, :], t["aw_e"]).then_inc(m.loaded, 16)
                sp.dma_start(ab[:, :], t["ab"]).then_inc(m.loaded, 16)

                def load(b, n, k):
                    rows = [sp.value_load(tile_blk[0:1, bass.ds(b * BT + u, 1)], min_val=0, max_val=BLOCKS - 1)
                            for u in range(BT)]
                    if after(b, SETS):
                        sp.wait_ge(m.scores_ready, b - SETS + 1)
                    for u in range(BT):
                        sp.dma_start(a_src[0:1, k, u, :], as_d[bass.ds(rows[u], 1), :]).then_inc(m.src_loaded[k], 16)

                def store(b, n, k):
                    rows = [sp.value_load(tile_out[0:1, bass.ds(b * BT + u, 1)], min_val=0, max_val=BLOCKS + TILES - 1)
                            for u in range(BT)]
                    sp.wait_ge(m.acc_ready, (b + 1) * BT)
                    for u in range(BT):
                        sp.dma_start(p_d[bass.ds(rows[u] * PR, PR), :], acc[:, k, u, :]).then_inc(m.sums_stored[k], 16)

                LAG = SETS + 2

                def step(b, n, k):
                    load(b, n, k)
                    if after(b, LAG):
                        store(b - LAG, None, (k - LAG) % SETS)
                batches(sp, 0, BATCHES, LAG, step)
                for b in range(BATCHES - LAG, BATCHES):
                    store(b, None, b % SETS)
                for k in range(SETS):
                    sp.wait_ge(m.sums_stored[k], 16 * BT * len(range(k, BATCHES, SETS)))

            @block.scalar
            def _(act):
                def step(b, n, k):
                    act.wait_ge(m.low_ready, b + 1)
                    act.activation(ex[:, k % 2, :, :], low[:, k % 2, :, :], ACT.Exp, scale=-1.0).then_inc(m.exp_ready, 1)
                batches(act, 0, BATCHES, 0, step)

            @block.vector
            def _(v):
                def select(b, k):
                    v.tensor_tensor(sel[:, k, :, :], bc(iota_w[:, :], 1, BT),
                                    bc(slots[:, bass.ds(b * BT, BT), 1], 2, W), ALU.is_equal).then_inc(m.sel_step, 1)
                    v.tensor_tensor(part[:, k % 2, :, :], bc(slots[:, bass.ds(b * BT, BT), 3], 2, H),
                                    bc(awe[:, :], 1, BT), ALU.mult).then_inc(m.edge_step, 1)
                    v.wait_ge(m.sel_step, b + 1)
                    v.tensor_scalar(off[:, k, :, :], sel[:, k, :, :], BIG, -BIG, ALU.mult, ALU.add).then_inc(m.sel_ready, 1)
                    v.wait_ge(m.edge_step, b * 2 + 1)
                    v.tensor_tensor(edge[:, k, :, :], part[:, k % 2, :, :], bc(ab[:, :], 1, BT), ALU.add).then_inc(m.edge_step, 1)

                def accumulate(b, k, u):
                    prev = acc[0:FR, k, u - 1, :] if u else acc[0:FR, (k - 1) % SETS, BT - 1, :]
                    v.scalar_tensor_tensor(acc[0:FR, k, u, :], prev, keep[0:FR, bass.ds(b * BT + u, 1)],
                                           out_ps[0:FR, k % 2, u * HW:(u + 1) * HW], ALU.mult, ALU.add).then_inc(m.acc_ready, 1)

                def acc_waits(b, n, k):
                    v.wait_ge(m.sums_ready, b + 1)
                    if after(b, SETS):
                        v.wait_ge(m.sums_stored[k], n * (16 * BT))

                def step(b, n, k):
                    j = k % 2
                    v.wait_ge(m.scores_ready, b + 1)
                    v.tensor_reduce(own[:, j, :, :].rearrange("p u h -> p (u h)"),
                                    sc_ps[:, j, 0:BT * HW].rearrange("p (x w) -> p x w", w=W),
                                    axis=AX.X, op=ALU.max).then_inc(m.own_ready, 1)
                    select(b + 1, (k + 1) % SETS)
                    v.wait_ge(m.own_ready, b + 1)
                    v.wait_ge(m.feat_loaded[k], n * (16 * BT) + 16 * BT)
                    v.tensor_tensor(part[:, j, :, :], own[:, j, :, :], feat[:, k, :, H * FR:FROW], ALU.add).then_inc(m.part_ready, 1)
                    old = after(b, 2)
                    if old:
                        bo, no, ko = b - 2, n if k >= 2 else n - 1, (k - 2) % SETS
                        acc_waits(bo, no, ko)
                        v.wait_ge(m.acc_ready, bo * BT)
                        accumulate(bo, ko, 0)
                    v.wait_ge(m.part_ready, b + 1)
                    v.wait_ge(m.edge_step, b * 2 + 2)
                    v.tensor_tensor(own[:, j, :, :], part[:, j, :, :], edge[:, k, :, :], ALU.add).then_inc(m.sum_ready, 1)
                    if old:
                        v.wait_ge(m.acc_ready, bo * BT + 1)
                        accumulate(bo, ko, 1)
                    v.wait_ge(m.sum_ready, b + 1)
                    v.tensor_scalar(low[:, j, :, :], own[:, j, :, :], 1.0 / 20.0, 0.0, ALU.mult, ALU.max).then_inc(m.low_ready, 1)
                    for u in (2, 3):
                        if old:
                            v.wait_ge(m.acc_ready, bo * BT + u)
                            accumulate(bo, ko, u)
                    v.wait_ge(m.exp_ready, b + 1)
                    v.tensor_tensor(wgt[:, j, :, :, :], bc(ex[:, j, :, :], 3, W), bc(sel[:, k, :, :], 2, H),
                                    ALU.mult).then_inc(m.weights_ready, 1)

                v.memset(acc[:, :, :, :], 0.0).then_inc(m.const_ready, 1)
                v.memset(ones[:, :], 1.0).then_inc(m.const_ready, 1)
                v.wait_ge(m.const_ready, 2)
                v.wait_ge(m.loaded, 32)
                select(0, 0)
                batches(v, 0, BATCHES, 2, step)
                for b in (BATCHES - 2, BATCHES - 1):
                    acc_waits(b, b // SETS, b % SETS)
                    for u in range(BT):
                        v.wait_ge(m.acc_ready, b * BT + u)
                        accumulate(b, b % SETS, u)

            @block.tensor
            def _(pe):
                def scores(b, n, k):
                    pe.wait_ge(m.sel_ready, b + 1)
                    pe.wait_ge(m.src_loaded[k], n * (16 * BT) + 16 * BT)
                    for u in range(BT):
                        o = sc_ps[:, k % 2, u * HW:(u + 1) * HW]
                        pe.matmul(o, ident_b[:, :], bc(off[:, k, u, :], 1, H), start=True, stop=False)
                        last = pe.matmul(o, ones[0:1, :], a_src[0:1, k, u, :].rearrange("a (w h) -> a h w", h=H),
                                         start=False, stop=True)
                    last.then_inc(m.scores_ready, 1)

                def sums(b, n, k):
                    pe.wait_ge(m.weights_ready, b + 1)
                    pe.wait_ge(m.feat_loaded[k], n * (16 * BT) + 16 * BT)
                    for u in range(BT):
                        for h in range(H):
                            last = pe.matmul(out_ps[0:FR, k % 2, u * HW + h * W:u * HW + (h + 1) * W],
                                             feat[:, k, u, h * FR:(h + 1) * FR], wgt[:, k % 2, u, h, :], start=True, stop=True)
                    last.then_inc(m.sums_ready, 1)

                def step(b, n, k):
                    scores(b, n, k)
                    if after(b, 1):
                        sums(b - 1, n if k else n - 1, (k - 1) % SETS)

                pe.wait_ge(m.const_ready, 2)
                batches(pe, 0, BATCHES, 1, step)
                sums(BATCHES - 1, (BATCHES - 1) // SETS, (BATCHES - 1) % SETS)


def pooled_nodes(nc, t, sb, pb, g):
    x, hid, ident, eps, p_d, valid, node_sum = (g[k] for k in ("x", "hid", "ident", "eps", "p_d", "valid", "node_sum"))
    with ExitStack() as st:
        def s(name, shape, dt=F32):
            return sb("pn_" + name, shape, dt, st)
        sums, sumsT = s("sums", (PR, CB, H, W)), s("sumsT", (FR, H, CN))
        stats, mv, std, rstd = ln_buffers(s)
        padding, total, inv = s("padding", (P, NODE_TILES)), s("total", (P, CT, H)), s("inv", (P, CT, H))
        y, xn = s("y", (P, CT, D)), s("xn", (P, CT, D))
        nodes, col_ps = pb(st, "pn_nodes", (P, CT, 512)), pb(st, "pn_col", (P, 512))
        heads = nodes[:, :, 0:H * FR].rearrange("p u (h c) -> p u h c", c=FR)
        with phase(nc, "pn", "sums_loaded", "sums_laid", "turn", "padding_ready", "nodes_ready", "step", "added", "ln_step",
                   "std_ready", "kept", "cols_ready", "cols_added") as (block, m):
            @block.sync
            def _(sp):
                rows = p_d.rearrange("(b r) c -> r b c", r=PR)
                with sp.Fori(0, CHUNKS) as c:
                    sp.wait_ge(m.sums_laid, c)
                    sp.dma_start(sums[:, :, :, :].rearrange("r b h w -> r b (h w)"),
                                 rows[:, bass.ds(c * CB, CB), :]).then_inc(m.sums_loaded, 16)

            @block.scalar
            def _(act):
                with act.Fori(0, CHUNKS) as c:
                    act.wait_ge(m.sums_loaded, c * 16 + 16)
                    act.wait_ge(m.nodes_ready, c)
                    act.activation(sumsT[:, :, :].rearrange("r h (b w) -> r b h w", w=W), sums[0:FR, :, :, :],
                                   ACT.Copy).then_inc(m.sums_laid, 1)
                    deviations(act, c, mv, std, eps, m)
                    act.wait_ge(m.ln_step, c * 4 + 4)
                    act.activation(hid[:, bass.ds(c * CT, CT), :], xn[:, :, :], ACT.Copy).then_inc(m.kept, 1)

            @block.vector
            def _(v):
                v.memset(node_sum[:, :], 0.0).then_inc(m.padding_ready, 1)
                v.tensor_scalar(padding[:, :], valid[:, :], -1.0, 1.0, ALU.mult, ALU.add).then_inc(m.padding_ready, 1)
                v.wait_ge(m.padding_ready, 2)
                with v.Fori(0, CHUNKS) as c:
                    v.wait_ge(m.nodes_ready, c + 1)
                    v.tensor_tensor(total[:, :, :], heads[:, :, :, DH], bc(padding[:, bass.ds(c * CT, CT)], 2, H),
                                    ALU.add).then_inc(m.step, 1)
                    v.wait_ge(m.step, c * 3 + 1)
                    v.reciprocal(inv[:, :, :], total[:, :, :]).then_inc(m.step, 1)
                    v.wait_ge(m.step, c * 3 + 2)
                    for u in range(CT):
                        last = v.tensor_tensor(y[:, u, :].rearrange("p (h d) -> p h d", h=H), heads[:, u, :, 0:DH],
                                               bc(inv[:, u, :], 2, DH), ALU.mult)
                    last.then_inc(m.step, 1)
                    v.wait_ge(m.step, c * 3 + 3)
                    xc = x[:, bass.ds(c * CT, CT), :]
                    v.tensor_tensor(xc, xc, y[:, :, :], ALU.add).then_inc(m.added, 1)
                    v.wait_ge(m.added, c + 1)
                    v.wait_ge(m.kept, c)
                    v.wait_ge(m.cols_ready, c)
                    v.sem_inc(m.turn, 1)
                    normalize(v, None, c, lambda u: x[:, bass.ds(c * CT + u, 1), :].rearrange("p a d -> p (a d)"),
                              xn, stats, mv, std, rstd, eps, m)
                    v.wait_ge(m.cols_ready, c + 1)
                    v.tensor_tensor(node_sum[:, :], node_sum[:, :], col_ps[:, 0:2], ALU.add).then_inc(m.cols_added, 1)
                    v.wait_ge(m.cols_added, c + 1)

            @block.tensor
            def _(pe):
                with pe.Fori(0, CHUNKS) as c:
                    pe.wait_ge(m.sums_laid, c + 1)
                    pe.wait_ge(m.added, c)
                    for u in range(CT):
                        for h in range(H):
                            last = pe.transpose(nodes[:, u, h * FR:(h + 1) * FR], sumsT[:, h, u * P:(u + 1) * P], ident[0:FR, 0:FR])
                    last.then_inc(m.nodes_ready, 1)
                    pe.wait_ge(m.ln_step, c * 4 + 4)
                    pe.wait_ge(m.cols_added, c)
                    for k in range(2):
                        for u in range(CT):
                            last = pe.matmul(col_ps[:, k:k + 1], xn[:, u, k * P:(k + 1) * P], valid[:, bass.ds(c * CT + u, 1)],
                                             start=u == 0, stop=u == CT - 1)
                    last.then_inc(m.cols_ready, 1)


def routed_ffn(nc, t, sb, pb, g, out):
    x, hid, ident, eps, node_sum = (g[k] for k in ("x", "hid", "ident", "eps", "node_sum"))
    with ExitStack() as st:
        def s(name, shape, dt=F32):
            return sb("rf_" + name, shape, dt, st)
        wr, br, iota = s("wr", (P, 2, EX1)), s("br", (1, EX1)), s("iota", (1, EX1))
        r = s("r", (1, 14, EX1))
        c1 = s("c1", (1, 14))
        pick = s("pick", (1, 2), I32)
        ones = s("ones", (1, P))
        wts, ws = s("wts", (1, 2)), s("ws", (P, 2))
        f1w, f2w, f1, f2 = s("f1w", (P, 2, 2, FF)), s("f2w", (P, 2, FC, D)), s("f1", (P, 2, FC)), s("f2", (P, 2, D))
        f2s, bias = s("f2s", (P, 2, FC, D)), s("bias", (P, 2, D))
        with ExitStack() as ps_st, phase(nc, "ro", "loaded", "ones_ready", "logits_ready", "step", "exp_ready", "picked", "weights_ready",
                                         "experts_loaded", "spread_ready", "ws_ready", "scaled") as (block, m):
            lg_ps, ws_ps = pb(ps_st, "ro_lg", (P, 512)), pb(ps_st, "ro_ws", (P, 512))

            @block.sync
            def _(sp):
                sp.dma_start(wr[:, :, :], t["Wr"]).then_inc(m.loaded, 16)
                sp.dma_start(br[:, :], t["br"]).then_inc(m.loaded, 16)
                sp.dma_start(iota[:, :], t["c_iota_e"][0:1, 0:EX1]).then_inc(m.loaded, 16)
                sp.wait_ge(m.picked, 2)
                for e in range(2):
                    w = sp.value_load(pick[0:1, e:e + 1], min_val=0, max_val=EX1 - 1)
                    one = bass.ds(w, 1)
                    sp.dma_start(f1w[:, e, :, :], t["F1"][one].rearrange("a p k n -> p (a k) n")).then_inc(m.experts_loaded, 16)
                    sp.dma_start(f2w[:, e, :, :], t["F2"][one].rearrange("a p k n -> p (a k) n")).then_inc(m.experts_loaded, 16)
                    sp.dma_start(f1[:, e, :], t["f1"][one].rearrange("a p k -> p (a k)")).then_inc(m.experts_loaded, 16)
                    sp.dma_start(f2[:, e, :], t["f2"][one].rearrange("a p k -> p (a k)")).then_inc(m.experts_loaded, 16)
                sp.wait_ge(m.experts_loaded, 128)

            @block.tensor
            def _(pe):
                pe.wait_ge(m.loaded, 48)
                for k in range(2):
                    last = pe.matmul(lg_ps[0:1, 0:EX1], node_sum[:, k:k + 1], wr[:, k, :], start=k == 0, stop=k == 1)
                last.then_inc(m.logits_ready, 1)
                pe.wait_ge(m.ones_ready, 1)
                pe.wait_ge(m.weights_ready, 2)
                pe.matmul(ws_ps[:, 0:2], ones[0:1, :], wts[0:1, :], start=True, stop=True).then_inc(m.spread_ready, 1)

            @block.scalar
            def _(act):
                for n, (src, dst, neg, tot) in enumerate(((0, 1, 0, 1), (4, 5, 2, 3))):
                    act.wait_ge(m.step, 2 if n == 0 else 9)
                    act.activation(r[0:1, dst, :], r[0:1, src, :], ACT.Exp, bias=c1[0:1, neg:neg + 1],
                                   accum_out=c1[0:1, tot:tot + 1]).then_inc(m.exp_ready, 1)
                act.wait_ge(m.step, 21)
                act.activation(c1[0:1, 10:11], c1[0:1, 9:10], ACT.Exp).then_inc(m.exp_ready, 1)
                act.wait_ge(m.ws_ready, 1)
                act.wait_ge(m.experts_loaded, 128)
                for e in range(2):
                    act.activation(f2s[:, e, :, :], f2w[:, e, :, :], ACT.Copy, scale=ws[:, e:e + 1])

            @block.vector
            def _(v):
                done = [0]

                def then(ins):
                    done[0] += 1
                    ins.then_inc(m.step, 1)
                    v.wait_ge(m.step, done[0])

                def row(i):
                    return r[0:1, i, :]

                def one(i):
                    return c1[0:1, i:i + 1]
                v.memset(ones[:, :], 1.0).then_inc(m.ones_ready, 1)
                v.wait_ge(m.loaded, 48)
                v.wait_ge(m.logits_ready, 1)
                then(v.scalar_tensor_tensor(row(0), lg_ps[0:1, 0:EX1], 1.0 / N, br[0:1, :], ALU.mult, ALU.add))
                then(v.tensor_reduce(one(0), row(0), axis=AX.X, op=ALU.max, negate=True))
                v.wait_ge(m.exp_ready, 1)
                then(v.reciprocal(one(4), one(1)))
                then(v.tensor_scalar(row(2), row(1), one(4), None, ALU.mult))
                then(v.tensor_single_scalar(row(3), row(2), float(N), ALU.mult))
                then(v.reciprocal(row(6), row(3)))
                then(v.tensor_scalar(row(7), row(6), CAPACITY, 1.0, ALU.mult, ALU.min))
                then(v.tensor_tensor(row(4), row(2), row(7), ALU.mult))
                then(v.tensor_reduce(one(2), row(4), axis=AX.X, op=ALU.max, negate=True))
                then(v.tensor_single_scalar(iota[0:1, :], iota[0:1, :], -float(EX1), ALU.add))
                v.wait_ge(m.exp_ready, 2)
                then(v.reciprocal(one(5), one(3)))
                then(v.tensor_scalar(row(8), row(5), one(5), None, ALU.mult))
                for n in range(2):
                    then(v.tensor_reduce(one(6 + n), row(8), axis=AX.X, op=ALU.max))
                    then(v.scalar_tensor_tensor(row(9), row(8), one(6 + n), iota[0:1, :], ALU.is_equal, ALU.mult))
                    then(v.tensor_reduce(one(8), row(9), axis=AX.X, op=ALU.min))
                    v.tensor_single_scalar(pick[0:1, n:n + 1], one(8), float(EX1), ALU.add).then_inc(m.picked, 1)
                    if n == 0:
                        then(v.tensor_scalar(row(10), iota[0:1, :], one(8), -4.0, ALU.is_equal, ALU.mult))
                        then(v.tensor_tensor(row(8), row(8), row(10), ALU.add))
                then(v.tensor_tensor(one(9), one(7), one(6), ALU.subtract))
                assert done[0] == 21, done
                v.wait_ge(m.exp_ready, 3)
                then(v.tensor_single_scalar(one(11), one(10), 1.0, ALU.add))
                then(v.reciprocal(one(12), one(11)))
                v.tensor_copy(wts[0:1, 0:1], one(12)).then_inc(m.weights_ready, 1)
                v.tensor_tensor(wts[0:1, 1:2], one(12), one(10), ALU.mult).then_inc(m.weights_ready, 1)
                v.wait_ge(m.spread_ready, 1)
                v.tensor_copy(ws[:, :], ws_ps[:, 0:2]).then_inc(m.ws_ready, 1)
                v.wait_ge(m.ws_ready, 1)
                v.wait_ge(m.experts_loaded, 128)
                then(v.tensor_scalar(bias[:, 1, :], f2[:, 0, :], ws[:, 0:1], None, ALU.mult))
                then(v.scalar_tensor_tensor(bias[:, 0, :], f2[:, 1, :], ws[:, 1:2], bias[:, 1, :], ALU.mult, ALU.add))

        gam, bet = s("gam", (P, D)), s("bet", (P, D))
        hb, hT, hs = s("hb", (P, CT, D)), s("hT", (P, 2, CN)), s("hs", (P, 2, FC, CN))
        stats, mv, std, rstd = ln_buffers(s)
        y, z = s("y", (P, CT, D)), s("z", (P, CT, D))
        banks, h_ps, prod = pb(st, "rf_banks", (P, 3, 512)), pb(st, "rf_h", (P, 2, 512)), pb(st, "rf_prod", (P, 3, 512))
        R = 2 * FC * 2
        with phase(nc, "rf", "loaded", "hb_ready", "turn", "banks_ready", "copied", "h_ready", "gelu_ready", "prod_ready",
                   "biased", "with_hid", "ln_step", "std_ready", "scaled", "shifted", "summed", "stored") as (block, m):
            @block.sync
            def _(sp):
                sp.dma_start(gam[:, :], t["gamma"]).then_inc(m.loaded, 16)
                sp.dma_start(bet[:, :], t["beta"]).then_inc(m.loaded, 16)
                with sp.Fori(0, CHUNKS) as c:
                    sp.wait_ge(m.summed, c + 1)
                    sp.dma_start(out[:, bass.ds(c * CT, CT), :], z[:, :, :]).then_inc(m.stored, 16)
                sp.wait_ge(m.stored, CHUNKS * 16)

            @block.gpsimd
            def _(pool):
                with pool.Fori(0, CHUNKS) as c:
                    pool.wait_ge(m.copied, c * 3)
                    pool.wait_ge(m.with_hid, c)
                    pool.sem_inc(m.turn, 1)
                    pool.tensor_copy(hb[:, :, :], hid[:, bass.ds(c * CT, CT), :]).then_inc(m.hb_ready, 1)

            @block.scalar
            def _(act):
                with act.Fori(0, CHUNKS) as c:
                    copy_transposed(act, c, banks, hT, m.banks_ready, m.copied)
                    act.wait_ge(m.prod_ready, c * 3)
                    for n in range(R):
                        e, j, f = n // (2 * FC), n // 2 % FC, n % 2
                        act.wait_ge(m.h_ready, c * R + (n + 1))
                        act.activation(hs[:, e, j, f * HALF:(f + 1) * HALF], h_ps[:, f, 0:HALF], ACT.Gelu,
                                       bias=f1[:, e, j:j + 1]).then_inc(m.gelu_ready, 1)
                    deviations(act, c, mv, std, eps, m)

            @block.tensor
            def _(pe):
                with pe.Fori(0, CHUNKS) as c:
                    pe.wait_ge(m.hb_ready, c + 1)
                    transposed(pe, hb, banks, ident, m.banks_ready)
                    pe.wait_ge(m.copied, c * 3 + 3)
                    for n in range(R):
                        e, j, f = n // (2 * FC), n // 2 % FC, n % 2
                        pe.wait_ge(m.gelu_ready, c * R if n < 2 else c * R + (n - 1))
                        for k in range(2):
                            last = pe.matmul(h_ps[:, f, 0:HALF], f1w[:, e, k, j * P:(j + 1) * P],
                                             hT[:, k, f * HALF:(f + 1) * HALF], start=k == 0, stop=k == 1)
                        last.then_inc(m.h_ready, 1)
                    pe.wait_ge(m.gelu_ready, c * R + R)
                    pe.wait_ge(m.biased, c * 3)
                    for u in range(CT):
                        for n in range(2 * FC):
                            last = pe.matmul(prod[:, u // 2, (u % 2) * D:(u % 2 + 1) * D], hs[:, n // FC, n % FC, u * P:(u + 1) * P],
                                             f2s[:, n // FC, n % FC, :], start=n == 0, stop=n == 2 * FC - 1)
                        if u % 2 or u == CT - 1:
                            last.then_inc(m.prod_ready, 1)

            @block.vector
            def _(v):
                v.wait_ge(m.loaded, 32)
                with v.Fori(0, CHUNKS) as c:
                    for b in range(3):
                        n = min(2, CT - 2 * b)
                        v.wait_ge(m.prod_ready, c * 3 + (b + 1))
                        v.tensor_tensor(y[:, 2 * b:2 * b + n, :], prod[:, b, 0:n * D].rearrange("p (u d) -> p u d", u=n),
                                        bc(bias[:, 0, :], 1, n), ALU.add).then_inc(m.biased, 1)
                    v.wait_ge(m.biased, c * 3 + 3)
                    v.wait_ge(m.stored, c * 16)
                    v.tensor_tensor(z[:, :, :], y[:, :, :], hb[:, :, :], ALU.add).then_inc(m.with_hid, 1)
                    v.wait_ge(m.with_hid, c + 1)
                    normalize(v, None, c, lambda u: z[:, u, :], y, stats, mv, std, rstd, eps, m)
                    v.wait_ge(m.ln_step, c * 4 + 4)
                    v.tensor_tensor(z[:, :, :], y[:, :, :], bc(gam[:, :], 1, CT), ALU.mult).then_inc(m.scaled, 1)
                    v.wait_ge(m.scaled, c + 1)
                    v.tensor_tensor(y[:, :, :], z[:, :, :], bc(bet[:, :], 1, CT), ALU.add).then_inc(m.shifted, 1)
                    v.wait_ge(m.shifted, c + 1)
                    v.tensor_tensor(z[:, :, :], y[:, :, :], x[:, bass.ds(c * CT, CT), :], ALU.add).then_inc(m.summed, 1)
                    v.wait_ge(m.summed, c + 1)


def host_layout(i):
    f = {k: np.ascontiguousarray(v) for k, v in i.items()}

    def edges(a, pad):
        out = np.full(P * EC, pad, a.dtype)
        out[:E] = a
        return out.reshape(P, EC)

    def rows(a):
        return np.ascontiguousarray(a.reshape(-1, P, a.shape[-1]).transpose(1, 0, 2))

    def spread(a):
        return np.ascontiguousarray(np.broadcast_to(a.reshape(1, -1), (P, a.size)))

    x = np.zeros((NP_, D), np.float32)
    x[:N] = f["x"]
    p = np.arange(P)
    t = {
        "x": x.reshape(NODE_TILES, P, D).transpose(1, 0, 2),
        "src": edges(f["src"], SRC_PAD), "dst": edges(f["dst"], 0), "edge_type": edges(f["edge_type_3"], 0),
        "edge_weight": edges(f["edge_weight"], 0),
        "c_ident": np.eye(P, dtype=np.float32),
        "c_before": np.triu(np.ones((P, P), np.float32), 1),
        "c_iota_b": spread(np.arange(BLOCKS, dtype=np.float32)),
        "c_iota_w": spread(np.arange(W, dtype=np.float32)),
        "c_iota_e": spread(np.arange(EX0, dtype=np.float32)),
        "c_tcol": (p[:, None] + P * np.arange(TG)[None]).astype(np.float32),
        "c_valid": (p[:, None] + P * np.arange(NODE_TILES)[None] < N).astype(np.float32),
        "c_owner": (np.arange(EX0)[:, None, None] == (2 * np.arange(HC)[:, None] + p[None] // H0)[None]).astype(np.float32),
        "Win": rows(f["L0_gnn_Win"].T), "b_in": spread(f["L0_gnn_b_in"]),
        "Wq": np.stack([rows(np.repeat(w.T.reshape(D, H, 1, DH), 2, 2).reshape(D, 2 * D)) for w in f["L0_gnn_Wq"]]),
        "bq": np.stack([np.concatenate([b.reshape(H, DH).T] * 2) for b in f["L0_gnn_bq"]]),
        "Wkv": np.stack([rows(np.concatenate([k.T, v.T], 1)) for k, v in zip(f["L0_gnn_Wk"], f["L0_gnn_Wv"])]),
        "bkv": np.stack([spread(np.concatenate([k, v])) for k, v in zip(f["L0_gnn_bk"], f["L0_gnn_bv"])]),
        "Wo": np.stack([w.T.reshape(H, DH, D).transpose(1, 0, 2) for w in f["L0_gnn_Wo"]]),
        "Ee": np.stack([e.reshape(3, H, DH).transpose(2, 1, 0) for e in f["L0_gnn_Eemb"]]),
        "bo": np.stack([spread(b)[:3] for b in f["L0_gnn_bo"]]),
        "ln_g": np.stack([spread(b) for b in f["L0_gnn_ln_g"]]),
        "ln_b": np.stack([spread(b) for b in f["L0_gnn_ln_b"]]),
        "A1": rows(f["L0_gnn_W1"].T), "a1": f["L0_gnn_b1"].reshape(2, P).T,
        "A2": rows(f["L0_gnn_W2"].T), "a2": spread(f["L0_gnn_b2"]),
        "router_w": rows(f["L0_ffn_router_w"].T), "router_b": spread(f["L0_ffn_router_b"]),
        "E1": rows(f["L0_ffn_W1"].transpose(1, 0, 2).reshape(D, EX0 * H0)),
        "e1": f["L0_ffn_b1"].reshape(HC, P).T,
        "E2": rows(f["L0_ffn_W2"].reshape(EX0 * H0, D)), "e2": f["L0_ffn_b2"],
        "Ws": rows(f["L1_gnn_Ws"].transpose(1, 0, 2).reshape(D, H * DH)), "bs": spread(f["L1_gnn_bs"]),
        "aw_s": spread(f["L1_gnn_aw"][:, :DH]), "aw_d": spread(f["L1_gnn_aw"][:, DH:2 * DH]),
        "aw_e": spread(f["L1_gnn_aw"][:, 2 * DH]), "ab": spread(f["L1_gnn_ab"]),
        "Wr": rows(f["L1_ffn_Wr"]), "br": f["L1_ffn_br"].reshape(1, EX1),
        "F1": np.stack([rows(w) for w in f["L1_ffn_W1"]]),
        "f1": np.stack([b.reshape(FC, P).T for b in f["L1_ffn_b1"]]),
        "F2": np.stack([rows(w) for w in f["L1_ffn_W2"]]),
        "f2": np.stack([spread(b) for b in f["L1_ffn_b2"]]),
        "gamma": spread(f["L1_ffn_gamma"]), "beta": spread(f["L1_ffn_beta"]),
    }
    return {k: np.ascontiguousarray(v) for k, v in t.items()}


def kernel(**inputs):
    import concourse.bacc as bacc
    from concourse.bass_utils import run_bass_kernel_spmd

    nc = bacc.Bacc("TRN2", target_bir_lowering=False, num_devices=1)
    arrays = {f"in_{k}": v for k, v in host_layout(inputs).items()}
    t = {k[3:]: nc.dram_tensor(k, list(a.shape), mybir.dt.from_np(a.dtype), kind="ExternalInput").ap()
         for k, a in arrays.items()}
    out = nc.dram_tensor("out_x", [P, NODE_TILES, D], F32, kind="ExternalOutput").ap()
    build(nc, t, out)
    got = run_bass_kernel_spmd(nc, [arrays], core_ids=[0]).results[0]["out_x"]
    return np.asarray(got).transpose(1, 0, 2).reshape(NP_, D)[:N]
```

```python
from contextlib import ExitStack, contextmanager

import numpy as np

import concourse.bass as bass
from concourse import mybir

F32, BF16, I32 = mybir.dt.float32, mybir.dt.bfloat16, mybir.dt.int32
ALU = mybir.AluOpType
ACT = mybir.ActivationFunctionType
AX = mybir.AxisListType

P = 128
N, D, E = 3125, 256, 53125
H, DH, LAYERS = 4, 64, 3
W = 16
HW = H * W
NODE_TILES = -(-N // P)
NP_ = NODE_TILES * P
BLOCKS = NP_ // W
CT = 5
CHUNKS = NODE_TILES // CT
CN = CT * P
CB = CN // W
HALF = CN // 2
EC = -(-E // P)
BT = 4
TILES = -(-(E // P + BLOCKS) // BT) * BT
BATCHES = TILES // BT
TG = -(-(TILES + BT) // P)
SETS = 4
TYPES = 4
MARKS = W + TYPES
MC = HW + W
FR = DH + 1
FROW = H * FR + H
BIG = 1e30
FREE = 1
EPS = 1e-5
EX0, H0 = 32, 64
HC = EX0 * H0 // P
EX1, FF = 8, 512
FC = FF // P
CAPACITY = float(-(-N * 5 // (4 * EX1)))
SRC_PAD = 4000
NOBODY = 4095
assert SRC_PAD // W >= BLOCKS and NOBODY >= NP_ and CHUNKS * CT == NODE_TILES and EC % 8 == 0


@contextmanager
def phase(nc, title, *names):
    sems = {}
    for name in names:
        name, _, many = name.partition("*")
        name, _, producer = name.partition("+")
        made = [nc.alloc_semaphore(f"{title}_{name}{i}") for i in range(int(many or 1))]
        sems[name] = made if many else made[0]
        if producer:
            engine = {"pe": nc.tensor, "act": nc.scalar, "dve": nc.vector, "pool": nc.gpsimd, "sp": nc.sync}[producer]
            for sem in made:
                engine.sem_inc(sem, FREE)
    flat = [s for x in sems.values() for s in (x if isinstance(x, list) else [x])]
    with nc.Block() as block:
        yield block, type("Sems", (), sems)
    nc.clear_and_free_semaphores(flat)
    nc.all_engine_barrier()


def batches(eng, first, last, peel, step):
    mid = (last - first - peel) // SETS
    for b in range(first, first + peel):
        step(b, b // SETS, b % SETS)
    b0 = first + peel
    if mid:
        with eng.Fori(0, mid) as i:
            for j in range(SETS):
                step(i * SETS + (b0 + j), i + (b0 + j) // SETS, (b0 + j) % SETS)
    for b in range(b0 + mid * SETS, last):
        step(b, b // SETS, b % SETS)


def after(b, k):
    return not isinstance(b, int) or b >= k


def bc(ap, axis, count):
    a = ap.unsqueeze(axis)
    shape = list(a.shape)
    shape[axis] = count
    return a.broadcast_to(shape)


def build(nc, t, out):
    ctx = ExitStack()

    def dram(name, shape, dt=F32):
        return nc.dram_tensor(name, list(shape), dt, kind="Internal").ap()

    slot_d = dram("slot_table", (P * TILES, 4))
    blk_d = dram("tile_block", (TG * P,), I32)
    keep_d = dram("tile_keep", (TG * P,))
    kv_d = dram("kv_table", (NP_, 2 * D))
    q_d = dram("q_blocks", (BLOCKS * P, P))
    x_d = dram("x_kept", (P, NODE_TILES, D))
    f_d = dram("feature_table", (NP_, FROW))
    as_d = dram("a_src", (BLOCKS, W * H))

    with ctx:
        def sb(name, shape, dt=F32, stack=ctx):
            return stack.enter_context(nc.sbuf_tensor(name, list(shape), dt))

        def pb(stack, name, shape, dt=F32):
            return stack.enter_context(nc.psum_tensor(name, list(shape), dt))

        hid = sb("hid", (P, NODE_TILES, D))
        ident = sb("ident", (P, P))
        ident_b = sb("ident_b", (P, P), BF16)
        ident_big = sb("ident_big", (P, P), BF16)
        iota_w = sb("iota_w", (P, W))
        valid = sb("valid", (P, NODE_TILES))
        eps = sb("eps", (P, 1))
        keep = sb("keep", (P, TG * P))
        tile_blk = sb("tile_blk", (1, TG * P), I32)
        slots = sb("slots", (P, TILES, 4))
        marks = sb("marks", (P, TILES, MARKS), BF16)
        kv = sb("kv", (P, SETS, BT, 2 * D))
        node_sum = sb("node_sum", (P, 2))

        with ExitStack() as st:
            x = sb("x_in", (P, NODE_TILES, D), F32, st)
            edge_sort(nc, t, sb, pb, locals())
            hidden_in(nc, t, sb, pb, locals())
        with nc.Fori(0, LAYERS) as layer:
            qkv(nc, t, sb, pb, locals(), layer)
            with ExitStack() as st:
                sums = sb("sums", (P, BLOCKS, MC), F32, st)
                attention_edges(nc, t, sb, pb, locals())
                node_update(nc, t, sb, pb, locals(), layer)
        x = sb("x", (P, NODE_TILES, D))
        adjustment(nc, t, sb, pb, locals())
        expert_ffn(nc, t, sb, pb, locals())
        features(nc, t, sb, pb, locals())
        with ExitStack() as st:
            sums = sb("pooled", (FR, BLOCKS, HW), F32, st)
            pooling_edges(nc, t, sb, pb, locals())
            pooled_nodes(nc, t, sb, pb, locals())
        routed_ffn(nc, t, sb, pb, locals(), out)


def tile_blocks(nc, engine, table, b):
    return nc.values_load_multi_w_load_instructions(
        table[0:1, bass.ds(b * BT, BT)], engines=(engine,), min_val=0, max_val=BLOCKS - 1,
        skip_runtime_bounds_check_because="the table is clamped to the blocks where it is made")[1]


def edge_sort(nc, t, sb, pb, g):
    slot_d, blk_d, keep_d, slots, marks = (g[k] for k in ("slot_d", "blk_d", "keep_d", "slots", "marks"))
    x, ident, ident_b, iota_w, valid, eps = (g[k] for k in ("x", "ident", "ident_b", "iota_w", "valid", "eps"))
    G8 = 8
    with ExitStack() as st:
        def s(name, shape, dt=F32):
            return sb(name, shape, dt, st)
        src = s("src_i", (P, EC), I32)
        dst = s("dst_i", (P, EC), I32)
        ety = s("ety_i", (P, EC), I32)
        ewt = s("edge_w", (P, EC))
        blk = s("edge_blk", (P, EC), I32)
        loc = s("edge_loc", (P, EC), I32)
        blk_f = s("edge_blk_f", (P, EC + 4))
        rec = s("rec", (P, EC, 4))
        iota_b = s("iota_b", (P, BLOCKS))
        onehot = s("onehot", (P, 2, G8, BLOCKS), BF16)
        before = s("before", (P, P))
        before_b = s("before_b", (P, P), BF16)
        ones_b = s("ones_b", (P, P), BF16)
        zeros = s("zeros", (P, BLOCKS))
        zeros_b = s("zeros_b", (P, 2 * BLOCKS), BF16)
        empty = s("empty", (P, TILES, 4))
        count = s("count", (P, BLOCKS))
        count_i = s("count_i", (P, BLOCKS), I32)
        tiles = s("tiles", (P, BLOCKS))
        t_end = s("t_end", (P, BLOCKS))
        t_base = s("t_base", (P, BLOCKS))
        s_base = s("s_base", (P, BLOCKS))
        tcol = s("tcol", (P, TG))
        cmp = s("cmp", (P, 2, TG, BLOCKS))
        cols = s("cols", (P, 3, TG))
        cols_i = s("cols_i", (P, TG), I32)

        with ExitStack() as ps_st, phase(
                nc, "count", "loaded", "x_loaded", "const_ready", "filled", "empty_ready", "split", "parts", "hot*2",
                "counted+pe*2", "sum_ready") as (block, m):
            hist = pb(ps_st, "hist", (P, 2 * BLOCKS))

            @block.sync
            def _(sp):
                for a, b in ((src, t["src"]), (dst, t["dst"]), (ety, t["edge_type"]), (ewt, t["edge_weight"]), (iota_b, t["c_iota_b"]),
                             (before, t["c_before"]), (tcol, t["c_tcol"]), (ident, t["c_ident"]),
                             (iota_w, t["c_iota_w"]), (valid, t["c_valid"])):
                    sp.dma_start(a[:, :], b).then_inc(m.loaded, 16)
                sp.dma_start(x[:, :, :], t["x"]).then_inc(m.x_loaded, 16)
                sp.wait_ge(m.empty_ready, 1)
                sp.dma_start(slot_d.rearrange("(p t) f -> p t f", p=P), empty[:, :, :]).then_inc(m.filled, 16)
                sp.wait_ge(m.x_loaded, 16)
                sp.wait_ge(m.filled, 16)

            @block.gpsimd
            def _(pool):
                pool.memset(ones_b[:, :], 1.0)
                pool.memset(zeros[:, :], 0.0)
                pool.memset(eps[:, :], EPS)
                pool.memset(zeros_b[:, :], 0.0).then_inc(m.const_ready, 1)
                pool.memset(blk_f[:, EC:EC + 4], float(BLOCKS))
                pool.memset(empty[:, :, 0], float(NOBODY))
                pool.memset(empty[:, :, 1], 99.0)
                pool.memset(empty[:, :, 2], 99.0)
                pool.memset(empty[:, :, 3], 0.0).then_inc(m.empty_ready, 1)

            @block.scalar
            def _(act):
                act.wait_ge(m.loaded, 160)
                act.activation(ident_b[:, :], ident[:, :], ACT.Copy)
                act.activation(before_b[:, :], before[:, :], ACT.Copy)
                act.activation(rec[:, :, 2], ety[:, :], ACT.Copy)
                act.activation(rec[:, :, 0], dst[:, :], ACT.Copy)
                act.activation(rec[:, :, 3], ewt[:, :], ACT.Copy)

            @block.vector
            def _(v):
                v.wait_ge(m.loaded, 160)
                v.tensor_single_scalar(blk[:, :], src[:, :], 4, ALU.logical_shift_right).then_inc(m.split, 1)
                v.tensor_single_scalar(loc[:, :], src[:, :], W - 1, ALU.bitwise_and).then_inc(m.split, 1)
                v.wait_ge(m.split, 2)
                v.tensor_copy(blk_f[:, 0:EC], blk[:, :]).then_inc(m.parts, 1)
                v.tensor_copy(rec[:, :, 1], loc[:, :]).then_inc(m.parts, 1)
                v.wait_ge(m.parts, 1)
                with v.Fori(0, EC // (2 * G8)) as i:
                    for j in range(2):
                        v.wait_ge(m.counted[j], i + FREE)
                        v.tensor_tensor(onehot[:, j, :, :], bc(iota_b[:, :], 1, G8),
                                        bc(blk_f[:, bass.ds((i * 2 + j) * G8, G8)], 2, BLOCKS),
                                        ALU.is_equal).then_inc(m.hot[j], 1)

                v.wait_ge(m.sum_ready, 1)
                v.tensor_copy(count[:, :], hist[:, 0:BLOCKS]).then_inc(m.split, 1)
                v.wait_ge(m.split, 3)
                v.scalar_tensor_tensor(tiles[:, :], count[:, :], float(P - 1), hist[:, BLOCKS:2 * BLOCKS], ALU.add,
                                       ALU.add).then_inc(m.split, 1)
                v.wait_ge(m.split, 4)
                v.tensor_copy(count_i[:, :], tiles[:, :]).then_inc(m.split, 1)
                v.wait_ge(m.split, 5)
                v.tensor_single_scalar(count_i[:, :], count_i[:, :], 7, ALU.logical_shift_right).then_inc(m.split, 1)
                v.wait_ge(m.split, 6)
                v.tensor_single_scalar(tiles[:, :], count_i[:, :], 1.0, ALU.max).then_inc(m.split, 1)
                v.wait_ge(m.split, 7)
                v.wait_ge(m.const_ready, 1)
                v.tensor_tensor_scan(t_end[:, :], tiles[:, :], zeros[:, :], 0.0, ALU.add, ALU.add).then_inc(m.split, 1)
                v.wait_ge(m.split, 8)
                v.tensor_tensor(t_base[:, :], t_end[:, :], tiles[:, :], ALU.subtract).then_inc(m.split, 1)
                v.wait_ge(m.split, 9)
                v.tensor_single_scalar(s_base[:, :], t_base[:, :], float(P), ALU.mult).then_inc(m.split, 1)

            @block.tensor
            def _(pe):
                pe.wait_ge(m.const_ready, 1)
                pe.matmul(hist[:, :], ones_b[:, :], zeros_b[:, :], start=True, stop=False)
                with pe.Fori(0, EC // (2 * G8)) as i:
                    for j in range(2):
                        pe.wait_ge(m.hot[j], i + 1)
                        for c in range(0, G8, 2):
                            last = pe.matmul(hist[:, :], ones_b[:, :],
                                             onehot[:, j, c:c + 2, :].rearrange("p a b -> p (a b)"),
                                             start=False, stop=False)
                        last.then_inc(m.counted[j], 1)
                pe.matmul(hist[:, :], ones_b[:, :], zeros_b[:, :], start=False, stop=True).then_inc(m.sum_ready, 1)

        with phase(nc, "tables", "step", "stored", "loaded") as (block, m):
            tb = bc(tcol[:, :], 2, BLOCKS)

            @block.vector
            def _(v):
                v.tensor_tensor(cmp[:, 0, :, :], bc(t_end[:, :], 1, TG), tb, ALU.is_le).then_inc(m.step, 1)
                v.tensor_tensor(cmp[:, 1, :, :], bc(t_base[:, :], 1, TG), tb, ALU.is_equal).then_inc(m.step, 1)
                v.wait_ge(m.step, 2)
                v.tensor_reduce(cols[:, 0:2, :], cmp[:, :, :, :], axis=AX.X, op=ALU.add).then_inc(m.step, 1)
                v.wait_ge(m.step, 3)
                v.tensor_single_scalar(cols_i[:, :], cols[:, 0, :], float(BLOCKS - 1), ALU.min).then_inc(m.step, 1)
                v.tensor_scalar(cols[:, 2, :], cols[:, 1, :], -1.0, 1.0, ALU.mult, ALU.add).then_inc(m.step, 1)

            @block.sync
            def _(sp):
                sp.wait_ge(m.step, 5)
                with nc.allow_non_contiguous_dma("tile tables, once"):
                    sp.dma_start(blk_d.rearrange("(g p) -> p g", p=P), cols_i[:, :]).then_inc(m.stored, 16)
                    sp.dma_start(keep_d.rearrange("(g p) -> p g", p=P), cols[:, 2, :]).then_inc(m.stored, 16)
                sp.wait_ge(m.stored, 32)
                sp.dma_start(g["tile_blk"][0:1, :], blk_d.unsqueeze(0)).then_inc(m.loaded, 16)
                sp.dma_start(g["keep"][:, :], keep_d.unsqueeze(0).broadcast_to([P, TG * P])).then_inc(m.loaded, 16)
                sp.wait_ge(m.loaded, 32)

        GR = 4
        TURNS = EC // GR
        pos = s("pos", (P, 2, GR))
        pos_i = s("pos_i", (P, 2, 3, GR), I32)
        beyond = s("beyond", (P, 2, GR))
        idx = s("idx", (P, 2, GR), I32)
        rec_c = s("rec_c", (P, 2, GR, 4))
        prod = s("prod", (P, GR, BLOCKS))
        given = s("given", (64, 2, BLOCKS), BF16)
        pick = s("pick", (64, P), BF16)
        with ExitStack() as ps_st, phase(
                nc, "place", "hot*2", "pick_ready", "ranked+dve", "prior*4", "totaled+pe", "high_ready", "given_ready", "turn", "step",
                "idx_ready*2", "written*2") as (block, m):
            taken = pb(ps_st, "taken", (P, GR, 512))
            total = pb(ps_st, "total", (P, 2, 512))

            @block.scalar
            def _(act):
                act.activation(given[:, 0, :], s_base[0:64, :], ACT.Copy).then_inc(m.high_ready, 1)
                with act.Fori(0, TURNS // 2) as it:
                    for j in range(2):
                        act.wait_ge(m.totaled, it * 2 + (j + 1 + FREE))
                        act.activation(given[:, 1 - j, :], total[0:64, j, 0:BLOCKS], ACT.Copy).then_inc(m.high_ready, 1)

            @block.vector
            def _(v):
                def hot(i, j):
                    v.tensor_tensor(onehot[:, j, 0:GR, :], bc(iota_b[:, :], 1, GR),
                                    bc(blk_f[:, bass.ds(i * GR, GR)], 2, BLOCKS), ALU.is_equal).then_inc(m.hot[j], 1)
                v.memset(pick[:, :], 0.0).then_inc(m.pick_ready, 1)
                v.wait_ge(m.pick_ready, 1)
                v.memset(pick[0:1, :], 1.0)
                v.memset(pick[32:33, :], 1.0).then_inc(m.pick_ready, 1)
                v.wait_ge(m.high_ready, 1)
                v.tensor_tensor(given[32:64, 0, :], s_base[32:64, :], given[32:64, 0, :], ALU.subtract).then_inc(m.given_ready, 1)
                hot(0, 0)
                def turn(it, j):
                    i = it * 2 + j
                    v.wait_ge(m.totaled, i + FREE)
                    hot(i + 1, 1 - j)
                    v.wait_ge(m.high_ready, i + 2)
                    v.tensor_tensor(given[32:64, 1 - j, :], total[32:64, j, 0:BLOCKS], given[32:64, 1 - j, :],
                                    ALU.subtract).then_inc(m.given_ready, 1)
                    v.wait_ge(m.hot[j], it + 1)
                    for k in range(GR):
                        v.wait_ge(m.prior[k], i + 1)
                        v.tensor_tensor_reduce(out=prod[:, k, :], in0=onehot[:, j, k, :],
                                               in1=taken[:, k, 0:BLOCKS], scale=1.0, scalar=0.0, op0=ALU.mult,
                                               op1=ALU.add, accum_out=pos[:, j, k:k + 1]).then_inc(m.ranked, 1)
                    v.tensor_scalar(beyond[:, j, :], blk_f[:, bass.ds(i * GR, GR)], float(BLOCKS) - 0.5,
                                    float(1 << 24), ALU.is_ge, ALU.mult).then_inc(m.step, 1)
                    v.wait_ge(m.step, i * 4 + 1)
                    v.wait_ge(m.ranked, i * GR + (GR + FREE))
                    v.tensor_tensor(pos_i[:, j, 0, :], pos[:, j, :], beyond[:, j, :], ALU.add).then_inc(m.step, 1)
                    v.wait_ge(m.step, i * 4 + 2)
                    v.tensor_single_scalar(pos_i[:, j, 1, :], pos_i[:, j, 0, :], P - 1, ALU.bitwise_and)
                    v.tensor_single_scalar(pos_i[:, j, 2, :], pos_i[:, j, 0, :], 7,
                                           ALU.logical_shift_right).then_inc(m.step, 1)
                    v.wait_ge(m.step, i * 4 + 3)
                    if after(it, 1):
                        v.wait_ge(m.written[j], it * (16 * GR))
                    v.scalar_tensor_tensor(idx[:, j, :], pos_i[:, j, 1, :], float(TILES), pos_i[:, j, 2, :],
                                           ALU.mult, ALU.add).then_inc(m.step, 1)
                    v.tensor_copy(rec_c[:, j, :, :], rec[:, bass.ds(i * GR, GR), :]).then_inc(m.idx_ready[j], 1)
                    v.wait_ge(m.step, i * 4 + 4)

                for j in range(2):
                    turn(0, j)
                with v.Fori(0, TURNS // 2 - 1) as it:
                    for j in range(2):
                        turn(it + 1, j)

            @block.tensor
            def _(pe):
                pe.wait_ge(m.pick_ready, 2)
                with pe.Fori(0, TURNS // 2) as it:
                    for j in range(2):
                        i = it * 2 + j
                        pe.wait_ge(m.hot[j], it + 1)
                        pe.wait_ge(m.given_ready, i + 1)
                        pe.matmul(total[:, j, 0:BLOCKS], pick[:, :], given[:, j, :], start=True, stop=False)
                        for e in range(GR):
                            last = pe.matmul(total[:, j, 0:BLOCKS], ones_b[:, :], onehot[:, j, e, :],
                                             start=False, stop=e == GR - 1)
                        last.then_inc(m.totaled, 1)
                        for k in range(GR):
                            if k == 0:
                                pe.wait_ge(m.ranked, i * GR + FREE)
                            pe.matmul(taken[:, k, 0:BLOCKS], pick[:, :], given[:, j, :], start=True, stop=False)
                            for e in range(k):
                                pe.matmul(taken[:, k, 0:BLOCKS], ones_b[:, :], onehot[:, j, e, :],
                                          start=False, stop=False)
                            pe.matmul(taken[:, k, 0:BLOCKS], before_b[:, :], onehot[:, j, k, :],
                                             start=False, stop=True).then_inc(m.prior[k], 1)

            @block.gpsimd
            def _(pool):
                with pool.Fori(0, TURNS // 2) as it:
                    for j in range(2):
                        pool.wait_ge(m.idx_ready[j], it + 1)
                        pool.sem_inc(m.turn, 1)
                        for k in range(GR):
                            pool.indirect_dma_start(
                                slot_d, bass.IndirectOffsetOnAxis(ap=idx[:, j, k:k + 1], axis=0), rec_c[:, j, k, :], None,
                                bounds_check=P * TILES - 1, oob_is_err=False).then_inc(m.written[j], 16)
                for j in range(2):
                    pool.wait_ge(m.written[j], (TURNS // 2) * 16 * GR)

        with phase(nc, "slots", "loaded", "own_ready") as (block, m):
            @block.sync
            def _(sp):
                sp.dma_start(slots[:, :, :], slot_d.rearrange("(p t) f -> p t f", p=P)).then_inc(m.loaded, 16)
                sp.wait_ge(m.loaded, 16)

            @block.scalar
            def _(act):
                act.activation(g["ident_big"][:, :], ident[:, :], ACT.Copy, scale=BIG)

            @block.vector
            def _(v):
                v.memset(g["kv"][:, :, :, :], 0.0)
                v.wait_ge(m.loaded, 16)
                own = marks[:, :, 0:W]
                v.tensor_tensor(own, bc(iota_w[:, :], 1, TILES), bc(slots[:, :, 1], 2, W), ALU.is_equal).then_inc(m.own_ready, 1)
                v.tensor_tensor(marks[:, :, W:MARKS], bc(iota_w[:, 0:TYPES], 1, TILES), bc(slots[:, :, 2], 2, TYPES), ALU.is_equal)
                v.wait_ge(m.own_ready, 1)
                v.tensor_single_scalar(own, own, -1.0, ALU.add)


def transposed(pe, src, banks, ident, signal):
    for u in range(CT):
        for k in range(2):
            last = pe.transpose(banks[:, u // 2, (u % 2) * D + k * P:(u % 2) * D + (k + 1) * P],
                                src[:, u, k * P:(k + 1) * P], ident[:, :])
        if u % 2 or u == CT - 1:
            last.then_inc(signal, 1)


def copy_transposed(act, c, banks, dst, ready, copied):
    for b in range(3):
        n = min(2, CT - 2 * b)
        act.wait_ge(ready, c * 3 + (b + 1))
        act.activation(dst[:, :, 2 * b * P:(2 * b + n) * P].rearrange("p k (u n) -> p u k n", u=n),
                       banks[:, b, 0:n * D].rearrange("p (u k n) -> p u k n", u=n, k=2), ACT.Copy).then_inc(copied, 1)


def normalize(v, c, src, dst, stats, mv, std, rstd, eps, m):
    for u in range(CT):
        last = v.bn_stats(stats[:, u, :], src(u))
    last.then_inc(m.ln_step, 1)
    v.wait_ge(m.ln_step, c * 4 + 1)
    v.sem_inc(m.turn, 1)
    for u in range(CT):
        last = v.bn_aggr(mv[:, u, :], stats[:, u, :])
    last.then_inc(m.ln_step, 1)
    v.wait_ge(m.std_ready, c + 1)
    v.reciprocal(rstd[:, :], std[:, :]).then_inc(m.ln_step, 1)
    v.wait_ge(m.ln_step, c * 4 + 3)
    for u in range(CT):
        last = v.tensor_scalar(dst[:, u, :], src(u), mv[:, u, 0:1], rstd[:, u:u + 1], ALU.subtract, ALU.mult)
    last.then_inc(m.ln_step, 1)


def deviations(act, c, mv, std, eps, m):
    act.wait_ge(m.ln_step, c * 4 + 2)
    act.activation(std[:, :], mv[:, :, 1], ACT.Sqrt, bias=eps[:, 0:1]).then_inc(m.std_ready, 1)


def ln_buffers(s):
    return s("stats", (P, CT, 6)), s("mv", (P, CT, 2)), s("std", (P, CT)), s("rstd", (P, CT))


def hidden_in(nc, t, sb, pb, g):
    x, hid, ident, eps, x_d = g["x"], g["hid"], g["ident"], g["eps"], g["x_d"]
    with ExitStack() as st:
        def s(name, shape, dt=F32):
            return sb("hi_" + name, shape, dt, st)
        win, b_in = s("win", (P, 2, D)), s("b_in", (P, D))
        stats, mv, std, rstd = ln_buffers(s)
        xn, xnT = s("xn", (P, CT, D)), s("xnT", (P, 2, CN))
        banks, prod = pb(st, "hi_banks", (P, 3, 512)), pb(st, "hi_prod", (P, 3, 512))
        with phase(nc, "hid", "loaded", "turn", "ln_step", "std_ready", "banks_ready", "copied", "prod_ready", "stored+dve",
                   "x_added", "x_stored") as (block, m):
            @block.sync
            def _(sp):
                sp.dma_start(win[:, :, :], t["Win"]).then_inc(m.loaded, 16)
                sp.dma_start(b_in[:, :], t["b_in"]).then_inc(m.loaded, 16)
                with sp.Fori(0, CHUNKS) as c:
                    sp.wait_ge(m.x_added, c + 1)
                    sp.dma_start(x_d[:, bass.ds(c * CT, CT), :], x[:, bass.ds(c * CT, CT), :]).then_inc(m.x_stored, 16)
                sp.wait_ge(m.x_stored, CHUNKS * 16)

            @block.vector
            def _(v):
                v.wait_ge(m.loaded, 32)
                with v.Fori(0, CHUNKS) as c:
                    normalize(v, c, lambda u: x[:, bass.ds(c * CT + u, 1), :].rearrange("p a d -> p (a d)"),
                              xn, stats, mv, std, rstd, eps, m)
                    v.wait_ge(m.ln_step, c * 4 + 4)
                    v.tensor_tensor(x[:, bass.ds(c * CT, CT), :], x[:, bass.ds(c * CT, CT), :], xn[:, :, :],
                                    ALU.add).then_inc(m.x_added, 1)
                    for b in range(3):
                        n = min(2, CT - 2 * b)
                        v.wait_ge(m.prod_ready, c * 3 + (b + 1))
                        v.tensor_tensor(hid[:, bass.ds(c * CT + 2 * b, n), :],
                                        prod[:, b, 0:n * D].rearrange("p (u d) -> p u d", u=n),
                                        bc(b_in[:, :], 1, n), ALU.add).then_inc(m.stored, 1)
                    v.wait_ge(m.x_added, c + 1)

            @block.scalar
            def _(act):
                with act.Fori(0, CHUNKS) as c:
                    deviations(act, c, mv, std, eps, m)
                    copy_transposed(act, c, banks, xnT, m.banks_ready, m.copied)

            @block.tensor
            def _(pe):
                pe.wait_ge(m.loaded, 32)
                with pe.Fori(0, CHUNKS) as c:
                    pe.wait_ge(m.ln_step, c * 4 + 4)
                    transposed(pe, xn, banks, ident, m.banks_ready)
                    pe.wait_ge(m.stored, c * 3 + FREE)
                    for u in range(CT):
                        pe.wait_ge(m.copied, c * 3 + (u // 2 + 1))
                        for k in range(2):
                            last = pe.matmul(prod[:, u // 2, (u % 2) * D:(u % 2 + 1) * D],
                                             xnT[:, k, u * P:(u + 1) * P], win[:, k, :], start=k == 0, stop=k == 1)
                        if u % 2 or u == CT - 1:
                            last.then_inc(m.prod_ready, 1)


def qkv(nc, t, sb, pb, g, layer):
    hid, ident, kv_d, q_d = g["hid"], g["ident"], g["kv_d"], g["q_d"]
    with ExitStack() as st:
        def s(name, shape, dt=F32):
            return sb("qkv_" + name, shape, dt, st)
        wq, wkv = s("wq", (P, 2, 2 * D)), s("wkv", (P, 2, 2 * D))
        bq, bqs, bkv = s("bq", (P, H)), s("bqs", (P, H)), s("bkv", (P, 2 * D))
        hb, hT = s("hb", (P, CT, D)), s("hT", (P, 2, CN))
        kv_row, qs = s("kv_row", (P, CT, 2 * D)), s("qs", (P, CB, 2, HW))
        banks = pb(st, "qkv_banks", (P, 3, 512))
        kv_ps, q_ps = pb(st, "kv_ps", (P, 2, 512)), pb(st, "q_ps", (P, 2, 512))
        with phase(nc, "qkv", "loaded", "hb_ready", "banks_ready", "copied+act", "kv_ready", "kv_rows+dve", "q_ready", "q_rows+act",
                   "kv_stored+sp", "q_stored+sp", "bias_ready", "zeroed", "turn") as (block, m):
            @block.sync
            def _(sp):
                sp.dma_start(wkv[:, :, :], t["Wkv"][bass.ds(layer, 1)].rearrange("a p k n -> p (a k) n")).then_inc(m.loaded, 16)
                sp.dma_start(bkv[:, :], t["bkv"][bass.ds(layer, 1)].rearrange("a p n -> p (a n)")).then_inc(m.loaded, 16)
                sp.dma_start(wq[:, :, :], t["Wq"][bass.ds(layer, 1)].rearrange("a p k n -> p (a k) n")).then_inc(m.loaded, 16)
                sp.dma_start(bq[:, :], t["bq"][bass.ds(layer, 1)].rearrange("a p n -> p (a n)")).then_inc(m.loaded, 16)
                kv_rows = kv_d.rearrange("(u p) d -> p u d", p=P)
                q_rows = q_d.rearrange("(b p) c -> p b c", p=P)
                with sp.Fori(0, CHUNKS) as c:
                    sp.wait_ge(m.kv_rows, c * CT + (CT + FREE))
                    sp.dma_start(kv_rows[:, bass.ds(c * CT, CT), :], kv_row[:, :, :]).then_inc(m.kv_stored, 16)
                    sp.wait_ge(m.q_rows, c * (2 * H) + (2 * H + FREE))
                    sp.dma_start(q_rows[:, bass.ds(c * CB, CB), :],
                                 qs[:, :, :, :].rearrange("p b a c -> p b (a c)")).then_inc(m.q_stored, 16)
                sp.wait_ge(m.kv_stored, CHUNKS * 16 + FREE)
                sp.wait_ge(m.q_stored, CHUNKS * 16 + FREE)

            @block.gpsimd
            def _(pool):
                pool.memset(qs[0:DH, :, 1, :], 0.0)
                pool.memset(qs[DH:P, :, 0, :], 0.0).then_inc(m.zeroed, 1)
                pool.wait_ge(m.zeroed, 1)
                with pool.Fori(0, CHUNKS) as c:
                    pool.wait_ge(m.copied, c * 3 + FREE)
                    pool.sem_inc(m.turn, 1)
                    pool.tensor_copy(hb[:, :, :], hid[:, bass.ds(c * CT, CT), :]).then_inc(m.hb_ready, 1)

            @block.vector
            def _(v):
                v.wait_ge(m.loaded, 64)
                with v.Fori(0, CHUNKS) as c:
                    v.wait_ge(m.kv_stored, c * 16 + FREE)
                    for u in range(CT):
                        v.wait_ge(m.kv_ready, c * CT + (u + 1))
                        v.tensor_tensor(kv_row[:, u, :], kv_ps[:, u % 2, :], bkv[:, :], ALU.add).then_inc(m.kv_rows, 1)

            @block.scalar
            def _(act):
                act.wait_ge(m.loaded, 64)
                act.activation(bqs[:, :], bq[:, :], ACT.Copy, scale=DH ** -0.5).then_inc(m.bias_ready, 1)
                act.wait_ge(m.bias_ready, 1)
                act.wait_ge(m.zeroed, 1)
                with act.Fori(0, CHUNKS) as c:
                    copy_transposed(act, c, banks, hT, m.banks_ready, m.copied)
                    act.wait_ge(m.q_stored, c * 16 + FREE)
                    for h in range(H):
                        for f in range(2):
                            r = h * 2 + f
                            act.wait_ge(m.q_ready, c * (2 * H) + (r + 1))
                            for a in range(2):
                                last = act.activation(
                                    qs[a * DH:(a + 1) * DH, f * (CB // 2):(f + 1) * (CB // 2), a, h * W:(h + 1) * W],
                                    q_ps[a * DH:(a + 1) * DH, r % 2, 0:HALF].rearrange("p (b w) -> p b w", w=W),
                                    ACT.Identity, bias=bqs[a * DH:(a + 1) * DH, h:h + 1], scale=DH ** -0.5)
                            last.then_inc(m.q_rows, 1)

            @block.tensor
            def _(pe):
                pe.wait_ge(m.loaded, 64)
                with pe.Fori(0, CHUNKS) as c:
                    pe.wait_ge(m.hb_ready, c + 1)
                    transposed(pe, hb, banks, ident, m.banks_ready)
                    pe.wait_ge(m.copied, c * 3 + (3 + FREE))
                    for u in range(CT):
                        if u < 2:
                            pe.wait_ge(m.kv_rows, c * CT + FREE)
                        else:
                            pe.wait_ge(m.kv_rows, c * CT + (u - 1 + FREE))
                        for k in range(2):
                            last = pe.matmul(kv_ps[:, u % 2, :], hT[:, k, u * P:(u + 1) * P], wkv[:, k, :],
                                             start=k == 0, stop=k == 1)
                        last.then_inc(m.kv_ready, 1)
                    for h in range(H):
                        for f in range(2):
                            r = h * 2 + f
                            if r < 2:
                                pe.wait_ge(m.q_rows, c * (2 * H) + FREE)
                            else:
                                pe.wait_ge(m.q_rows, c * (2 * H) + (r - 1 + FREE))
                            for k in range(2):
                                last = pe.matmul(q_ps[:, r % 2, 0:HALF], wq[:, k, h * P:(h + 1) * P],
                                                 hT[:, k, f * HALF:(f + 1) * HALF], start=k == 0, stop=k == 1)
                            last.then_inc(m.q_ready, 1)


def attention_edges(nc, t, sb, pb, g):
    ident, ident_big, slots, marks, kv = g["ident"], g["ident_big"], g["slots"], g["marks"], g["kv"]
    keep, tile_blk, kv_d, q_d, totals = (g[k] for k in ("keep", "tile_blk", "kv_d", "q_d", "sums"))
    GH = H * H
    with ExitStack() as st:
        def s(name, shape, dt=F32):
            return sb("ae_" + name, shape, dt, st)
        idx = s("idx", (P, SETS, BT), I32)
        q = s("q", (P, SETS, BT, P))
        typ = s("typ", (P, SETS, BT, P), BF16)
        sel = s("sel", (P, SETS, BT, W), BF16)
        kT = s("kT", (P, BT, 2, P))
        own = s("own", (P, 2, BT, H, H))
        top = s("top", (P, 2, BT, H))
        low = s("low", (P, 2, BT, H, H))
        ex = s("ex", (P, 2, BT, H, H))
        z = s("z", (P, 2, BT, H))
        rz = s("rz", (P, 2, BT, H))
        att = s("att", (P, 2, BT, H, H))
        wgt = s("wgt", (P, 2, BT, GH, W))
        acc = s("acc", (P, SETS, BT, MC))
        kT_ps = pb(st, "kT_ps", (P, BT, 2, P))
        sc_ps = pb(st, "sc_ps", (P, 2, BT, GH * W))
        out_ps = pb(st, "out_ps", (P, 2, 512))
        with phase(nc, "ae", "idx_ready", "turn", "kv_loaded*4", "q_loaded*4", "const_ready", "sel_ready", "kT_ready", "kT_copied",
                   "scores_ready", "own_ready", "top_ready", "low_ready", "exp_ready", "z_ready", "rz_ready",
                   "att_ready", "weights_ready", "sums_ready", "acc_ready", "kept") as (block, m):

            @block.gpsimd
            def _(pool):
                def step(b, n, k):
                    if after(b, SETS):
                        pool.wait_ge(m.sums_ready, b - SETS + 1)
                        pool.sem_inc(m.turn, 1)
                    pool.tensor_copy(idx[:, k, :], slots[:, bass.ds(b * BT, BT), 0]).then_inc(m.idx_ready, 1)
                    pool.wait_ge(m.idx_ready, b + 1)
                    pool.sem_inc(m.turn, 1)
                    for u in range(BT):
                        pool.indirect_dma_start(
                            kv[:, k, u, :], None, kv_d, bass.IndirectOffsetOnAxis(ap=idx[:, k, u:u + 1], axis=0),
                            bounds_check=NP_ - 1, oob_is_err=False).then_inc(m.kv_loaded[k], 16)
                batches(pool, 0, BATCHES, SETS, step)

            @block.sync
            def _(sp):
                def step(b, n, k):
                    blocks = tile_blocks(nc, mybir.EngineType.SP, tile_blk, b)
                    if after(b, SETS):
                        sp.wait_ge(m.scores_ready, (b - SETS) * 2 + 2)
                    for u in range(BT):
                        sp.dma_start(q[:, k, u, :], q_d[bass.ds(blocks[u] * P, P), :]).then_inc(m.q_loaded[k], 16)
                batches(sp, 0, BATCHES, SETS, step)

            @block.scalar
            def _(act):
                def copies(b):
                    for f in range(2):
                        act.wait_ge(m.kT_ready, b * 2 + (f + 1))
                        act.activation(kT[:, 2 * f:2 * f + 2, :, :], kT_ps[:, 2 * f:2 * f + 2, :, :],
                                       ACT.Copy).then_inc(m.kT_copied, 1)

                def select(b, k):
                    if after(b, SETS):
                        act.wait_ge(m.sums_ready, b - SETS + 1)
                        act.sem_inc(m.turn, 1)
                    act.activation(typ[:, k, :, 0:TYPES], marks[:, bass.ds(b * BT, BT), W:MARKS], ACT.Copy).then_inc(m.sel_ready, 1)
                    act.activation(sel[:, k, :, :], marks[:, bass.ds(b * BT, BT), 0:W], ACT.Copy, bias=1.0).then_inc(m.sel_ready, 1)

                def keep_sums(b, k):
                    blocks = tile_blocks(nc, mybir.EngineType.Activation, tile_blk, b)
                    for u in range(BT):
                        if u == 0:
                            act.wait_ge(m.acc_ready, b * BT + BT)
                        act.wait_ge(m.kept, b * BT + u)
                        act.sem_inc(m.turn, 1)
                        act.activation(totals[:, bass.ds(blocks[u], 1), :], acc[:, k, u:u + 1, :], ACT.Copy).then_inc(m.kept, 1)

                LATE = 3

                def step(b, n, k):
                    if not isinstance(b, int) or b + 1 < BATCHES:
                        copies(b + 1)
                        select(b + 1, (k + 1) % SETS)
                    act.wait_ge(m.low_ready, b + 1)
                    act.activation(ex[:, k % 2, :, :, :], low[:, k % 2, :, :, :], ACT.Exp).then_inc(m.exp_ready, 1)
                    if after(b, LATE):
                        keep_sums(b - LATE, (k - LATE) % SETS)
                act.wait_ge(m.const_ready, 1)
                copies(0)
                select(0, 0)
                batches(act, 0, BATCHES - 1, SETS, step)
                step(BATCHES - 1, None, (BATCHES - 1) % SETS)
                for b in range(BATCHES - LATE, BATCHES):
                    keep_sums(b, b % SETS)

            @block.vector
            def _(v):
                def accumulate(b, k, u):
                    prev = acc[:, k, u - 1, :] if u else acc[:, (k - 1) % SETS, BT - 1, :]
                    v.scalar_tensor_tensor(acc[:, k, u, :], prev, keep[:, bass.ds(b * BT + u, 1)],
                                           out_ps[:, k % 2, u * MC:(u + 1) * MC], ALU.mult, ALU.add).then_inc(m.acc_ready, 1)

                def acc_waits(b, k):
                    v.wait_ge(m.sums_ready, b + 1)
                    if after(b, SETS):
                        v.wait_ge(m.kept, (b - SETS) * BT + BT)

                def step(b, n, k):
                    j = k % 2
                    for f in range(2):
                        v.wait_ge(m.scores_ready, b * 2 + (f + 1))
                        v.tensor_reduce(own[:, j, 2 * f:2 * f + 2, :, :].rearrange("p u g h -> p (u g h)"),
                                        sc_ps[:, j, 2 * f:2 * f + 2, :].rearrange("p u (x w) -> p (u x) w", w=W),
                                        axis=AX.X, op=ALU.max).then_inc(m.own_ready, 1)
                    v.wait_ge(m.own_ready, b * 2 + 2)
                    v.tensor_reduce(top[:, j, :, :], own[:, j, :, :, :].rearrange("p u g h -> p u h g"),
                                    axis=AX.X, op=ALU.max).then_inc(m.top_ready, 1)
                    v.wait_ge(m.top_ready, b + 1)
                    v.tensor_tensor(low[:, j, :, :, :], own[:, j, :, :, :], bc(top[:, j, :, :], 2, H),
                                    ALU.subtract).then_inc(m.low_ready, 1)
                    old = after(b, 2)
                    if old:
                        bo, ko = b - 2, (k - 2) % SETS
                        acc_waits(bo, ko)
                        v.wait_ge(m.acc_ready, bo * BT)
                        accumulate(bo, ko, 0)
                    v.wait_ge(m.exp_ready, b + 1)
                    v.tensor_reduce(z[:, j, :, :], ex[:, j, :, :, :].rearrange("p u g h -> p u h g"),
                                    axis=AX.X, op=ALU.add).then_inc(m.z_ready, 1)
                    if old:
                        v.wait_ge(m.acc_ready, bo * BT + 1)
                        accumulate(bo, ko, 1)
                    v.wait_ge(m.z_ready, b + 1)
                    v.reciprocal(rz[:, j, :, :], z[:, j, :, :]).then_inc(m.rz_ready, 1)
                    if old:
                        v.wait_ge(m.acc_ready, bo * BT + 2)
                        accumulate(bo, ko, 2)
                    v.wait_ge(m.rz_ready, b + 1)
                    v.tensor_tensor(att[:, j, :, :, :], ex[:, j, :, :, :], bc(rz[:, j, :, :], 2, H),
                                    ALU.mult).then_inc(m.att_ready, 1)
                    if old:
                        v.wait_ge(m.acc_ready, bo * BT + 3)
                        accumulate(bo, ko, 3)
                    v.wait_ge(m.att_ready, b + 1)
                    v.wait_ge(m.sel_ready, b * 2 + 2)
                    for f in range(2):
                        v.tensor_tensor(wgt[:, j, 2 * f:2 * f + 2, :, :],
                                        bc(att[:, j, 2 * f:2 * f + 2, :, :].rearrange("p u g h -> p u (g h)"), 3, W),
                                        bc(sel[:, k, 2 * f:2 * f + 2, :], 2, GH), ALU.mult).then_inc(m.weights_ready, 1)

                v.memset(acc[:, SETS - 1, BT - 1, :], 0.0)
                v.memset(typ[:, :, :, :], 0.0).then_inc(m.const_ready, 1)
                batches(v, 0, BATCHES, SETS + 2, step)
                for b in (BATCHES - 2, BATCHES - 1):
                    acc_waits(b, b % SETS)
                    for u in range(BT):
                        v.wait_ge(m.acc_ready, b * BT + u)
                        accumulate(b, b % SETS, u)

            @block.tensor
            def _(pe):
                def transposes(b, n, k):
                    pe.wait_ge(m.kv_loaded[k], n * (16 * BT) + 16 * BT)
                    for u in range(BT):
                        for i in range(2):
                            last = pe.transpose(kT_ps[:, u, i, :], kv[:, k, u, i * P:(i + 1) * P], ident[:, :])
                        if u % 2:
                            last.then_inc(m.kT_ready, 1)

                def scores(b, n, k):
                    pe.wait_ge(m.q_loaded[k], n * (16 * BT) + 16 * BT)
                    for u in range(BT):
                        pe.matmul(sc_ps[:, k % 2, u, :], ident_big[:, :], bc(marks[:, bass.ds(b * BT + u, 1), 0:W].rearrange("p a w -> p (a w)"), 1, GH), start=True, stop=False)
                        if u % 2 == 0:
                            pe.wait_ge(m.kT_copied, b * 2 + (u // 2 + 1))
                        for i in range(2):
                            last = pe.matmul(sc_ps[:, k % 2, u, i * P:(i + 1) * P], kT[:, u, i, :], q[:, k, u, :],
                                             start=False, stop=i == 1)
                        if u % 2:
                            last.then_inc(m.scores_ready, 1)

                def sums(b, n, k):
                    for u in range(BT):
                        if u % 2 == 0:
                            pe.wait_ge(m.weights_ready, b * 2 + (u // 2 + 1))
                        o = out_ps[:, k % 2, u * MC:(u + 1) * MC]
                        for i in range(H):
                            pe.matmul(o[i % 2 * DH:(i % 2 + 1) * DH, 0:HW], kv[:, k, u, D + i * DH:D + (i + 1) * DH],
                                      wgt[:, k % 2, u, i * H:(i + 1) * H, :].rearrange("p h w -> p (h w)"),
                                      start=i < 2, stop=i >= 2)
                        if u == 0:
                            pe.wait_ge(m.sel_ready, b * 2 + 2)
                        last = pe.matmul(o[:, HW:MC], typ[:, k, u, :], sel[:, k, u, :], start=True, stop=True)
                    last.then_inc(m.sums_ready, 1)

                def step(b, n, k):
                    scores(b, n, k)
                    if not isinstance(b, int) or b + 1 < BATCHES:
                        transposes(b + 1, n + 1 if k == SETS - 1 else n, (k + 1) % SETS)
                    if after(b, 1):
                        sums(b - 1, None, (k - 1) % SETS)

                pe.wait_ge(m.const_ready, 1)
                transposes(0, 0, 0)
                batches(pe, 0, BATCHES - 1, 1, step)
                step(BATCHES - 1, (BATCHES - 1) // SETS, (BATCHES - 1) % SETS)
                sums(BATCHES - 1, None, (BATCHES - 1) % SETS)


def node_update(nc, t, sb, pb, g, layer):
    hid, eps, totals = g["hid"], g["eps"], g["sums"]
    with ExitStack() as st:
        def s(name, shape, dt=F32):
            return sb("nu_" + name, shape, dt, st)
        wo, ee, ew, bo = s("wo", (P, H, D)), s("ee", (DH, H, 3)), s("ew", (3, D)), s("bo", (3, D))
        gam, bet = s("gam", (P, D)), s("bet", (P, D))
        sums, types = s("sums", (P, H, CN)), s("types", (3, CN))
        stats, mv, std, rstd = ln_buffers(s)
        y, yn = s("y", (P, CT, D)), s("yn", (P, CT, D))
        ew_ps, prod = pb(st, "ew_ps", (P, 512)), pb(st, "nu_prod", (P, 3, 512))
        with phase(nc, "nu", "loaded", "ew_ready", "ew_done", "sums_laid", "prod_ready+pe", "added+dve", "turn", "ln_step", "std_ready",
                   "scaled", "shifted", "done+act") as (block, m):
            @block.sync
            def _(sp):
                one = bass.ds(layer, 1)
                sp.dma_start(wo[:, :, :], t["Wo"][one].rearrange("a p h n -> p (a h) n")).then_inc(m.loaded, 16)
                sp.dma_start(ee[:, :, :], t["Ee"][one].rearrange("a p h n -> p (a h) n")).then_inc(m.loaded, 16)
                sp.dma_start(bo[:, :], t["bo"][one].rearrange("a p n -> p (a n)")).then_inc(m.loaded, 16)
                sp.dma_start(gam[:, :], t["ln_g"][one].rearrange("a p n -> p (a n)")).then_inc(m.loaded, 16)
                sp.dma_start(bet[:, :], t["ln_b"][one].rearrange("a p n -> p (a n)")).then_inc(m.loaded, 16)

            @block.tensor
            def _(pe):
                pe.wait_ge(m.loaded, 80)
                for h in range(H):
                    last = pe.matmul(ew_ps[0:3, 0:D], ee[:, h, :], wo[0:DH, h, :], start=h == 0, stop=h == H - 1)
                last.then_inc(m.ew_ready, 1)
                pe.wait_ge(m.ew_done, 1)
                with pe.Fori(0, CHUNKS) as c:
                    pe.wait_ge(m.sums_laid, c * 2 + 2)
                    pe.wait_ge(m.added, c * 3 + FREE)
                    for u in range(CT):
                        o = prod[:, u // 2, (u % 2) * D:(u % 2 + 1) * D]
                        for h in range(H):
                            pe.matmul(o, sums[:, h, u * P:(u + 1) * P], wo[:, h, :],
                                      start=h == 0, stop=False)
                        last = pe.matmul(o, types[:, u * P:(u + 1) * P], ew[:, :],
                                         start=False, stop=True)
                        if u % 2 or u == CT - 1:
                            last.then_inc(m.prod_ready, 1)

            @block.vector
            def _(v):
                v.wait_ge(m.loaded, 80)
                v.wait_ge(m.ew_ready, 1)
                v.tensor_tensor(ew[:, :], ew_ps[0:3, 0:D], bo[:, :], ALU.add).then_inc(m.ew_done, 1)
                with v.Fori(0, CHUNKS) as c:
                    for b in range(3):
                        n = min(2, CT - 2 * b)
                        v.wait_ge(m.prod_ready, c * 3 + (b + 1 + FREE))
                        v.tensor_tensor(y[:, 2 * b:2 * b + n, :], prod[:, b, 0:n * D].rearrange("p (u d) -> p u d", u=n),
                                        hid[:, bass.ds(c * CT + 2 * b, n), :], ALU.add).then_inc(m.added, 1)
                    v.wait_ge(m.added, c * 3 + (3 + FREE))
                    normalize(v, c, lambda u: y[:, u, :], yn, stats, mv, std, rstd, eps, m)
                    v.wait_ge(m.ln_step, c * 4 + 4)
                    v.tensor_tensor(y[:, :, :], yn[:, :, :], bc(gam[:, :], 1, CT), ALU.mult).then_inc(m.scaled, 1)
                    v.wait_ge(m.scaled, c + 1)
                    v.wait_ge(m.done, c + FREE)
                    v.tensor_tensor(yn[:, :, :], y[:, :, :], bc(bet[:, :], 1, CT), ALU.add).then_inc(m.shifted, 1)
                    v.wait_ge(m.done, c + (1 + FREE))

            @block.scalar
            def _(act):
                with act.Fori(0, CHUNKS) as c:
                    act.wait_ge(m.prod_ready, c * 3 + FREE)
                    act.sem_inc(m.turn, 1)
                    act.activation(sums[:, :, :].rearrange("r h (b w) -> r b h w", w=W),
                                   totals[:, bass.ds(c * CB, CB), 0:HW].rearrange("r b (h w) -> r b h w", w=W),
                                   ACT.Copy).then_inc(m.sums_laid, 1)
                    act.activation(types[:, :].rearrange("r (b w) -> r b w", w=W), totals[0:3, bass.ds(c * CB, CB), HW:MC],
                                   ACT.Copy).then_inc(m.sums_laid, 1)
                    deviations(act, c, mv, std, eps, m)
                    act.wait_ge(m.shifted, c + 1)
                    act.activation(hid[:, bass.ds(c * CT, CT), :], yn[:, :, :], ACT.Relu).then_inc(m.done, 1)


def adjustment(nc, t, sb, pb, g):
    x, hid, ident, x_d = g["x"], g["hid"], g["ident"], g["x_d"]
    with ExitStack() as st:
        def s(name, shape, dt=F32):
            return sb("ad_" + name, shape, dt, st)
        a1w, a2w, a1, a2 = s("w1", (P, 2, D)), s("w2", (P, 2, D)), s("b1", (P, 2)), s("b2", (P, D))
        hb, hT, u1T, y = s("hb", (P, CT, D)), s("hT", (P, 2, CN)), s("u1T", (P, 2, CN)), s("y", (P, CT, D))
        banks, u_ps, prod = pb(st, "ad_banks", (P, 3, 512)), pb(st, "ad_u", (P, 2, 512)), pb(st, "ad_prod", (P, 3, 512))
        with phase(nc, "ad", "loaded", "x_loaded", "hb_ready", "turn", "banks_ready", "copied+act", "u_ready", "relu_ready+act", "prod_ready+pe",
                   "biased+dve", "added+dve") as (block, m):
            @block.sync
            def _(sp):
                for a, b in ((a1w[:, :, :], "A1"), (a2w[:, :, :], "A2"), (a1[:, :], "a1"), (a2[:, :], "a2")):
                    sp.dma_start(a, t[b]).then_inc(m.loaded, 16)
                sp.dma_start(x[:, :, :], x_d).then_inc(m.x_loaded, 16)

            @block.gpsimd
            def _(pool):
                with pool.Fori(0, CHUNKS) as c:
                    pool.wait_ge(m.copied, c * 3 + FREE)
                    pool.sem_inc(m.turn, 1)
                    pool.tensor_copy(hb[:, :, :], hid[:, bass.ds(c * CT, CT), :]).then_inc(m.hb_ready, 1)

            @block.scalar
            def _(act):
                act.wait_ge(m.loaded, 64)
                with act.Fori(0, CHUNKS) as c:
                    copy_transposed(act, c, banks, hT, m.banks_ready, m.copied)
                    act.wait_ge(m.prod_ready, c * 3 + FREE)
                    for r in range(4):
                        act.wait_ge(m.u_ready, c * 4 + (r + 1))
                        act.activation(u1T[:, r // 2, (r % 2) * HALF:(r % 2 + 1) * HALF], u_ps[:, r % 2, 0:HALF], ACT.Relu,
                                       bias=a1[:, r // 2:r // 2 + 1]).then_inc(m.relu_ready, 1)

            @block.vector
            def _(v):
                v.wait_ge(m.loaded, 64)
                v.wait_ge(m.x_loaded, 16)
                with v.Fori(0, CHUNKS) as c:
                    v.wait_ge(m.added, c + FREE)
                    for b in range(3):
                        n = min(2, CT - 2 * b)
                        v.wait_ge(m.prod_ready, c * 3 + (b + 1 + FREE))
                        v.tensor_tensor(y[:, 2 * b:2 * b + n, :], prod[:, b, 0:n * D].rearrange("p (u d) -> p u d", u=n),
                                        bc(a2[:, :], 1, n), ALU.add).then_inc(m.biased, 1)
                    v.wait_ge(m.biased, c * 3 + (3 + FREE))
                    v.tensor_tensor(x[:, bass.ds(c * CT, CT), :], x[:, bass.ds(c * CT, CT), :], y[:, :, :],
                                    ALU.add).then_inc(m.added, 1)
                v.wait_ge(m.added, CHUNKS + FREE)

            @block.tensor
            def _(pe):
                pe.wait_ge(m.loaded, 64)
                with pe.Fori(0, CHUNKS) as c:
                    pe.wait_ge(m.hb_ready, c + 1)
                    transposed(pe, hb, banks, ident, m.banks_ready)
                    pe.wait_ge(m.copied, c * 3 + (3 + FREE))
                    for r in range(4):
                        pe.wait_ge(m.relu_ready, c * 4 + (max(r - 1, 0) + FREE))
                        for k in range(2):
                            last = pe.matmul(u_ps[:, r % 2, 0:HALF], a1w[:, k, (r // 2) * P:(r // 2 + 1) * P],
                                             hT[:, k, (r % 2) * HALF:(r % 2 + 1) * HALF], start=k == 0, stop=k == 1)
                        last.then_inc(m.u_ready, 1)
                    pe.wait_ge(m.relu_ready, c * 4 + (4 + FREE))
                    pe.wait_ge(m.biased, c * 3 + FREE)
                    for u in range(CT):
                        for k in range(2):
                            last = pe.matmul(prod[:, u // 2, (u % 2) * D:(u % 2 + 1) * D], u1T[:, k, u * P:(u + 1) * P],
                                             a2w[:, k, :], start=k == 0, stop=k == 1)
                        if u % 2 or u == CT - 1:
                            last.then_inc(m.prod_ready, 1)


def expert_ffn(nc, t, sb, pb, g):
    x, ident, ident_b, eps = g["x"], g["ident"], g["ident_b"], g["eps"]
    with ExitStack() as st:
        def s(name, shape, dt=F32):
            return sb("ex_" + name, shape, dt, st)
        e1w, e2w, e1, e2 = s("w1", (P, 2, EX0 * H0)), s("w2", (P, HC, D)), s("b1", (P, HC)), s("b2", (EX0, D))
        rw, rb, iota = s("rw", (P, 2, EX0)), s("rb", (P, EX0)), s("iota", (P, EX0))
        owner, owner_b = s("owner", (EX0, HC, P)), s("owner_b", (EX0, HC, P), BF16)
        stats, mv, std, rstd = ln_buffers(s)
        xn, xnT = s("xn", (P, CT, D)), s("xnT", (P, 2, CN))
        lg, eq, best, first = s("lg", (P, CT, EX0)), s("eq", (P, CT, EX0)), s("best", (P, CT)), s("first", (P, CT))
        hot = s("hot", (P, CT, EX0), BF16)
        hotT, offT = s("hotT", (EX0, CN)), s("offT", (EX0, CN), BF16)
        hs = s("hs", (P, 2, CN))
        out_ps = pb(st, "ex_out", (P, CT, 512))
        h_ps, lg_ps = pb(st, "ex_h", (P, 2, 512)), pb(st, "ex_lgp", (P, 512))
        SPLIT = (range(0, 3), range(3, CT))
        with phase(nc, "ex", "loaded", "turn", "ln_step", "std_ready", "banks_ready", "copied", "logits_ready", "pick",
                   "hot_ready", "hotT_ready", "off_ready", "h_ready", "relu_ready+act", "out_step+pe", "added+dve") as (block, m):
            @block.sync
            def _(sp):
                for a, b in ((rw[:, :, :], "router_w"), (rb[:, :], "router_b"), (iota[:, :], "c_iota_e"), (e1w[:, :, :], "E1"),
                             (e1[:, :], "e1"), (owner[:, :, :], "c_owner"), (e2w[:, :, :], "E2"), (e2[:, :], "e2")):
                    sp.dma_start(a, t[b]).then_inc(m.loaded, 16)

            @block.vector
            def _(v):
                v.wait_ge(m.loaded, 128)
                v.tensor_single_scalar(iota[:, :], iota[:, :], -float(EX0), ALU.add).then_inc(m.turn, 1)
                v.wait_ge(m.turn, 1)
                with v.Fori(0, CHUNKS) as c:
                    normalize(v, c, lambda u: x[:, bass.ds(c * CT + u, 1), :].rearrange("p a d -> p (a d)"),
                              xn, stats, mv, std, rstd, eps, m)
                    v.wait_ge(m.logits_ready, c + 1)
                    v.tensor_tensor(lg[:, :, :], lg_ps[:, 0:CT * EX0].rearrange("p (u e) -> p u e", u=CT),
                                    bc(rb[:, :], 1, CT), ALU.add).then_inc(m.pick, 1)
                    v.wait_ge(m.pick, c * 5 + 1)
                    v.tensor_reduce(best[:, :], lg[:, :, :], axis=AX.X, op=ALU.max).then_inc(m.pick, 1)
                    v.wait_ge(m.pick, c * 5 + 2)
                    v.tensor_tensor(eq[:, :, :], lg[:, :, :], bc(best[:, :], 2, EX0), ALU.is_equal).then_inc(m.pick, 1)
                    v.wait_ge(m.pick, c * 5 + 3)
                    v.tensor_tensor(lg[:, :, :], eq[:, :, :], bc(iota[:, :], 1, CT), ALU.mult).then_inc(m.pick, 1)
                    v.wait_ge(m.pick, c * 5 + 4)
                    v.tensor_reduce(first[:, :], lg[:, :, :], axis=AX.X, op=ALU.min).then_inc(m.pick, 1)
                    v.wait_ge(m.pick, c * 5 + 5)
                    v.tensor_tensor(hot[:, :, :], bc(first[:, :], 2, EX0), bc(iota[:, :], 1, CT),
                                    ALU.is_equal).then_inc(m.hot_ready, 1)
                    v.wait_ge(m.out_step, c * HC + (HC + FREE))
                    for u in range(CT):
                        xu = x[:, bass.ds(c * CT + u, 1), :].rearrange("p a d -> p (a d)")
                        v.scalar_tensor_tensor(xu, out_ps[:, u, 0:D], 0.0, xu, ALU.max, ALU.add).then_inc(m.added, 1)
                v.wait_ge(m.added, CHUNKS * CT + FREE)

            @block.scalar
            def _(act):
                act.wait_ge(m.loaded, 128)
                act.activation(owner_b[:, :, :], owner[:, :, :], ACT.Copy, scale=BIG).then_inc(m.off_ready, 1)
                with act.Fori(0, CHUNKS) as c:
                    deviations(act, c, mv, std, eps, m)
                    copy_transposed(act, c, out_ps, xnT, m.banks_ready, m.copied)
                    for f, us in enumerate(SPLIT):
                        act.wait_ge(m.hotT_ready, c * 2 + (f + 1))
                        cols = slice(us[0] * P, (us[-1] + 1) * P)
                        act.activation(hotT[:, cols], h_ps[0:EX0, f, 0:len(us) * P], ACT.Copy)
                        act.activation(offT[:, cols], h_ps[0:EX0, f, 0:len(us) * P], ACT.Copy, bias=-1.0).then_inc(m.off_ready, 1)
                    for j in range(HC):
                        act.wait_ge(m.out_step, c * HC + (max(j - 1, 0) + FREE))
                        for f in range(2):
                            act.wait_ge(m.h_ready, c * (2 * HC) + (2 * j + f + 1))
                            act.activation(hs[:, j % 2, f * HALF:(f + 1) * HALF], h_ps[:, f, 0:HALF], ACT.Relu,
                                           bias=e1[:, j:j + 1]).then_inc(m.relu_ready, 1)

            @block.tensor
            def _(pe):
                pe.wait_ge(m.loaded, 128)
                with pe.Fori(0, CHUNKS) as c:
                    pe.wait_ge(m.ln_step, c * 4 + 4)
                    pe.wait_ge(m.added, c * CT + FREE)
                    transposed(pe, xn, out_ps, ident, m.banks_ready)
                    pe.wait_ge(m.copied, c * 3 + 3)
                    for u in range(CT):
                        for k in range(2):
                            last = pe.matmul(lg_ps[:, u * EX0:(u + 1) * EX0], xnT[:, k, u * P:(u + 1) * P], rw[:, k, :],
                                             start=k == 0, stop=k == 1)
                    last.then_inc(m.logits_ready, 1)
                    pe.wait_ge(m.hot_ready, c + 1)
                    pe.wait_ge(m.relu_ready, c * (2 * HC) + FREE)
                    for f, us in enumerate(SPLIT):
                        for n, u in enumerate(us):
                            last = pe.matmul(h_ps[0:EX0, f, n * P:(n + 1) * P], hot[:, u, :], ident_b[:, :], start=True, stop=True)
                        last.then_inc(m.hotT_ready, 1)
                    pe.wait_ge(m.off_ready, c * 2 + 3)

                    def second(j):
                        pe.wait_ge(m.relu_ready, c * (2 * HC) + (2 * j + 2 + FREE))
                        for u in range(CT):
                            last = pe.matmul(out_ps[:, u, 0:D], hs[:, j % 2, u * P:(u + 1) * P], e2w[:, j, :],
                                             start=False, stop=j == HC - 1)
                        last.then_inc(m.out_step, 1)

                    for u in range(CT):
                        pe.matmul(out_ps[:, u, 0:D], hotT[:, u * P:(u + 1) * P], e2[:, :], start=True, stop=False)
                    for j in range(HC):
                        for f in range(2):
                            if j:
                                pe.wait_ge(m.relu_ready, c * (2 * HC) + (2 * j + f - 1 + FREE))
                            cols = slice(f * HALF, (f + 1) * HALF)
                            pe.matmul(h_ps[:, f, 0:HALF], owner_b[:, j, :], offT[:, cols], start=True, stop=False)
                            for k in range(2):
                                last = pe.matmul(h_ps[:, f, 0:HALF], e1w[:, k, j * P:(j + 1) * P], xnT[:, k, cols],
                                                 start=False, stop=k == 1)
                            last.then_inc(m.h_ready, 1)
                        if j:
                            second(j - 1)
                    second(HC - 1)


def features(nc, t, sb, pb, g):
    x, ident, eps, f_d, as_d = g["x"], g["ident"], g["eps"], g["f_d"], g["as_d"]
    with ExitStack() as st:
        def s(name, shape, dt=F32):
            return sb("fe_" + name, shape, dt, st)
        ws, bs = s("ws", (P, 2, D)), s("bs", (P, D))
        aws, awd = s("aws", (P, D)), s("awd", (P, D))
        stats, mv, std, rstd = ln_buffers(s)
        xn, xnT = s("xn", (P, CT, D)), s("xnT", (P, 2, CN))
        row, tmp, a_src = s("row", (P, CT, FROW)), s("tmp", (P, 2, CT * H, DH)), s("a_src", (P, CT * H))
        banks, prod = pb(st, "fe_banks", (P, 3, 512)), pb(st, "fe_prod", (P, 3, 512))
        heads = row[:, :, 0:H * FR].rearrange("p u (h c) -> p u h c", c=FR)
        with phase(nc, "fe", "loaded", "turn", "ln_step", "std_ready", "banks_ready", "copied", "prod_ready", "biased+dve", "weighted",
                   "rows_ready", "rows_stored+sp", "ones_ready") as (block, m):
            @block.sync
            def _(sp):
                for a, b in ((ws[:, :, :], "Ws"), (bs[:, :], "bs"), (aws[:, :], "aw_s"), (awd[:, :], "aw_d")):
                    sp.dma_start(a, t[b]).then_inc(m.loaded, 16)
                f_rows = f_d.rearrange("(u p) c -> p u c", p=P)
                as_rows = as_d.rearrange("b (w h) -> (b w) h", h=H).rearrange("(u p) h -> p u h", p=P)
                with sp.Fori(0, CHUNKS) as c:
                    sp.wait_ge(m.rows_ready, c * 2 + 2)
                    sp.dma_start(f_rows[:, bass.ds(c * CT, CT), :], row[:, :, :]).then_inc(m.rows_stored, 16)
                    sp.dma_start(as_rows[:, bass.ds(c * CT, CT), :],
                                 a_src[:, :].rearrange("p (u h) -> p u h", h=H)).then_inc(m.rows_stored, 16)
                sp.wait_ge(m.rows_stored, CHUNKS * 32 + FREE)

            @block.gpsimd
            def _(pool):
                pool.memset(heads[:, :, :, DH], 1.0).then_inc(m.ones_ready, 1)

            @block.vector
            def _(v):
                v.wait_ge(m.loaded, 64)
                v.wait_ge(m.ones_ready, 1)
                with v.Fori(0, CHUNKS) as c:
                    normalize(v, c, lambda u: x[:, bass.ds(c * CT + u, 1), :].rearrange("p a d -> p (a d)"),
                              xn, stats, mv, std, rstd, eps, m)
                    v.wait_ge(m.rows_stored, c * 32 + FREE)
                    for b in range(3):
                        n = min(2, CT - 2 * b)
                        v.wait_ge(m.prod_ready, c * 3 + (b + 1))
                        for u in range(2 * b, 2 * b + n):
                            last = v.tensor_tensor(heads[:, u, :, 0:DH],
                                                   prod[:, b, (u % 2) * D:(u % 2 + 1) * D].rearrange("p (h d) -> p h d", h=H),
                                                   bs[:, :].rearrange("p (h d) -> p h d", h=H), ALU.add)
                        last.then_inc(m.biased, 1)
                    v.wait_ge(m.biased, c * 3 + (3 + FREE))
                    for a, aw in enumerate((aws, awd)):
                        for u in range(CT):
                            last = v.tensor_tensor(tmp[:, a, u * H:(u + 1) * H, :], heads[:, u, :, 0:DH],
                                                   aw[:, :].rearrange("p (h d) -> p h d", h=H), ALU.mult)
                        last.then_inc(m.weighted, 1)
                    v.wait_ge(m.weighted, c * 2 + 1)
                    v.tensor_reduce(a_src[:, :], tmp[:, 0, :, :], axis=AX.X, op=ALU.add).then_inc(m.rows_ready, 1)
                    v.wait_ge(m.weighted, c * 2 + 2)
                    v.tensor_reduce(row[:, :, H * FR:FROW], tmp[:, 1, :, :].rearrange("p (u h) d -> p u h d", h=H),
                                    axis=AX.X, op=ALU.add).then_inc(m.rows_ready, 1)
                    v.wait_ge(m.rows_ready, c * 2 + 2)

            @block.scalar
            def _(act):
                with act.Fori(0, CHUNKS) as c:
                    deviations(act, c, mv, std, eps, m)
                    copy_transposed(act, c, banks, xnT, m.banks_ready, m.copied)

            @block.tensor
            def _(pe):
                pe.wait_ge(m.loaded, 64)
                with pe.Fori(0, CHUNKS) as c:
                    pe.wait_ge(m.ln_step, c * 4 + 4)
                    transposed(pe, xn, banks, ident, m.banks_ready)
                    pe.wait_ge(m.biased, c * 3 + FREE)
                    for u in range(CT):
                        pe.wait_ge(m.copied, c * 3 + (u // 2 + 1))
                        for k in range(2):
                            last = pe.matmul(prod[:, u // 2, (u % 2) * D:(u % 2 + 1) * D],
                                             xnT[:, k, u * P:(u + 1) * P], ws[:, k, :], start=k == 0, stop=k == 1)
                        if u % 2 or u == CT - 1:
                            last.then_inc(m.prod_ready, 1)


def pooling_edges(nc, t, sb, pb, g):
    ident_big, slots, marks = g["ident_big"], g["slots"], g["marks"]
    keep, tile_blk, f_d, as_d, totals = (g[k] for k in ("keep", "tile_blk", "f_d", "as_d", "sums"))
    feat = g["kv"][:, :, :, 0:FROW]
    with ExitStack() as st:
        def s(name, shape, dt=F32):
            return sb("pe_" + name, shape, dt, st)
        idx = s("idx", (P, SETS, BT), I32)
        a_src = s("a_src", (1, SETS, BT, HW))
        ones = s("ones", (1, P))
        awe, ab = s("awe", (P, H)), s("ab", (P, H))
        sel = s("sel", (P, SETS, BT, W), BF16)
        edge = s("edge", (P, SETS, BT, H))
        own = s("own", (P, 2, BT, H))
        part = s("part", (P, 2, BT, H))
        low = s("low", (P, 2, BT, H))
        ex = s("ex", (P, 2, BT, H))
        wgt = s("wgt", (P, 2, BT, H, W))
        acc = s("acc", (FR, SETS, BT, HW))
        sc_ps, out_ps = pb(st, "pe_sc", (P, 2, 512)), pb(st, "pe_out", (P, 2, 512))
        with phase(nc, "pe", "loaded", "const_ready", "turn", "idx_ready", "feat_loaded*4", "src_loaded*4", "edge_step",
                   "sel_ready", "scores_ready", "own_ready", "part_ready", "sum_ready", "low_ready", "exp_ready", "weights_ready",
                   "sums_ready", "acc_ready", "kept") as (block, m):

            @block.gpsimd
            def _(pool):
                def step(b, n, k):
                    if after(b, SETS):
                        pool.wait_ge(m.sums_ready, b - SETS + 1)
                        pool.sem_inc(m.turn, 1)
                    pool.tensor_copy(idx[:, k, :], slots[:, bass.ds(b * BT, BT), 0]).then_inc(m.idx_ready, 1)
                    pool.wait_ge(m.idx_ready, b + 1)
                    pool.sem_inc(m.turn, 1)
                    for u in range(BT):
                        pool.indirect_dma_start(
                            feat[:, k, u, :], None, f_d, bass.IndirectOffsetOnAxis(ap=idx[:, k, u:u + 1], axis=0),
                            bounds_check=NP_ - 1, oob_is_err=False).then_inc(m.feat_loaded[k], 16)
                batches(pool, 0, BATCHES, SETS, step)

            @block.sync
            def _(sp):
                sp.dma_start(awe[:, :], t["aw_e"]).then_inc(m.loaded, 16)
                sp.dma_start(ab[:, :], t["ab"]).then_inc(m.loaded, 16)

                def step(b, n, k):
                    blocks = tile_blocks(nc, mybir.EngineType.SP, tile_blk, b)
                    if after(b, SETS):
                        sp.wait_ge(m.scores_ready, b - SETS + 1)
                    for u in range(BT):
                        sp.dma_start(a_src[0:1, k, u, :], as_d[bass.ds(blocks[u], 1), :]).then_inc(m.src_loaded[k], 16)
                batches(sp, 0, BATCHES, SETS, step)

            @block.scalar
            def _(act):
                def select(b, k):
                    if after(b, SETS):
                        act.wait_ge(m.weights_ready, b - SETS + 1)
                        act.sem_inc(m.turn, 1)
                    act.activation(sel[:, k, :, :], marks[:, bass.ds(b * BT, BT), 0:W], ACT.Copy, bias=1.0).then_inc(m.sel_ready, 1)

                def keep_sums(b, k):
                    blocks = tile_blocks(nc, mybir.EngineType.Activation, tile_blk, b)
                    for u in range(BT):
                        if u == 0:
                            act.wait_ge(m.acc_ready, b * BT + BT)
                        act.wait_ge(m.kept, b * BT + u)
                        act.sem_inc(m.turn, 1)
                        act.activation(totals[:, bass.ds(blocks[u], 1), :], acc[:, k, u:u + 1, :], ACT.Copy).then_inc(m.kept, 1)

                LATE = 3

                def step(b, n, k):
                    if not isinstance(b, int) or b + 1 < BATCHES:
                        select(b + 1, (k + 1) % SETS)
                    act.wait_ge(m.low_ready, b + 1)
                    act.activation(ex[:, k % 2, :, :], low[:, k % 2, :, :], ACT.Exp, scale=-1.0).then_inc(m.exp_ready, 1)
                    if after(b, LATE):
                        keep_sums(b - LATE, (k - LATE) % SETS)
                select(0, 0)
                batches(act, 0, BATCHES - 1, SETS, step)
                step(BATCHES - 1, None, (BATCHES - 1) % SETS)
                for b in range(BATCHES - LATE, BATCHES):
                    keep_sums(b, b % SETS)

            @block.vector
            def _(v):
                def edges(b, k):
                    v.tensor_tensor(part[:, k % 2, :, :], bc(slots[:, bass.ds(b * BT, BT), 3], 2, H),
                                    bc(awe[:, :], 1, BT), ALU.mult).then_inc(m.edge_step, 1)
                    v.wait_ge(m.edge_step, b * 2 + 1)
                    v.tensor_tensor(edge[:, k, :, :], part[:, k % 2, :, :], bc(ab[:, :], 1, BT), ALU.add).then_inc(m.edge_step, 1)

                def accumulate(b, k, u):
                    prev = acc[:, k, u - 1, :] if u else acc[:, (k - 1) % SETS, BT - 1, :]
                    v.scalar_tensor_tensor(acc[:, k, u, :], prev, keep[0:FR, bass.ds(b * BT + u, 1)],
                                           out_ps[0:FR, k % 2, u * HW:(u + 1) * HW], ALU.mult, ALU.add).then_inc(m.acc_ready, 1)

                def acc_waits(b, k):
                    v.wait_ge(m.sums_ready, b + 1)
                    if after(b, SETS):
                        v.wait_ge(m.kept, (b - SETS) * BT + BT)

                def step(b, n, k):
                    j = k % 2
                    v.wait_ge(m.scores_ready, b + 1)
                    v.tensor_reduce(own[:, j, :, :].rearrange("p u h -> p (u h)"),
                                    sc_ps[:, j, 0:BT * HW].rearrange("p (x w) -> p x w", w=W),
                                    axis=AX.X, op=ALU.max).then_inc(m.own_ready, 1)
                    if not isinstance(b, int) or b + 1 < BATCHES:
                        edges(b + 1, (k + 1) % SETS)
                    v.wait_ge(m.own_ready, b + 1)
                    v.wait_ge(m.feat_loaded[k], n * (16 * BT) + 16 * BT)
                    v.tensor_tensor(part[:, j, :, :], own[:, j, :, :], feat[:, k, :, H * FR:FROW], ALU.add).then_inc(m.part_ready, 1)
                    old = after(b, 2)
                    if old:
                        bo, ko = b - 2, (k - 2) % SETS
                        acc_waits(bo, ko)
                        v.wait_ge(m.acc_ready, bo * BT)
                        accumulate(bo, ko, 0)
                    v.wait_ge(m.part_ready, b + 1)
                    v.wait_ge(m.edge_step, b * 2 + 2)
                    v.tensor_tensor(own[:, j, :, :], part[:, j, :, :], edge[:, k, :, :], ALU.add).then_inc(m.sum_ready, 1)
                    if old:
                        v.wait_ge(m.acc_ready, bo * BT + 1)
                        accumulate(bo, ko, 1)
                    v.wait_ge(m.sum_ready, b + 1)
                    v.tensor_scalar(low[:, j, :, :], own[:, j, :, :], 1.0 / 20.0, 0.0, ALU.mult, ALU.max).then_inc(m.low_ready, 1)
                    for u in (2, 3):
                        if old:
                            v.wait_ge(m.acc_ready, bo * BT + u)
                            accumulate(bo, ko, u)
                    v.wait_ge(m.exp_ready, b + 1)
                    v.wait_ge(m.sel_ready, b + 1)
                    v.tensor_tensor(wgt[:, j, :, :, :], bc(ex[:, j, :, :], 3, W), bc(sel[:, k, :, :], 2, H),
                                    ALU.mult).then_inc(m.weights_ready, 1)

                v.memset(acc[:, :, :, :], 0.0).then_inc(m.const_ready, 1)
                v.memset(ones[:, :], 1.0).then_inc(m.const_ready, 1)
                v.wait_ge(m.const_ready, 2)
                v.wait_ge(m.loaded, 32)
                edges(0, 0)
                batches(v, 0, BATCHES - 1, SETS + 2, step)
                step(BATCHES - 1, (BATCHES - 1) // SETS, (BATCHES - 1) % SETS)
                for b in (BATCHES - 2, BATCHES - 1):
                    acc_waits(b, b % SETS)
                    for u in range(BT):
                        v.wait_ge(m.acc_ready, b * BT + u)
                        accumulate(b, b % SETS, u)

            @block.tensor
            def _(pe):
                def scores(b, n, k):
                    pe.wait_ge(m.src_loaded[k], n * (16 * BT) + 16 * BT)
                    for u in range(BT):
                        o = sc_ps[:, k % 2, u * HW:(u + 1) * HW]
                        pe.matmul(o, ident_big[:, :], bc(marks[:, bass.ds(b * BT + u, 1), 0:W].rearrange("p a w -> p (a w)"), 1, H), start=True, stop=False)
                        last = pe.matmul(o, ones[0:1, :], a_src[0:1, k, u, :].rearrange("a (w h) -> a h w", h=H),
                                         start=False, stop=True)
                    last.then_inc(m.scores_ready, 1)

                def sums(b, n, k):
                    pe.wait_ge(m.weights_ready, b + 1)
                    pe.wait_ge(m.feat_loaded[k], n * (16 * BT) + 16 * BT)
                    for u in range(BT):
                        for h in range(H):
                            last = pe.matmul(out_ps[0:FR, k % 2, u * HW + h * W:u * HW + (h + 1) * W],
                                             feat[:, k, u, h * FR:(h + 1) * FR], wgt[:, k % 2, u, h, :], start=True, stop=True)
                    last.then_inc(m.sums_ready, 1)

                def step(b, n, k):
                    scores(b, n, k)
                    if after(b, 1):
                        sums(b - 1, n if k else n - 1, (k - 1) % SETS)

                pe.wait_ge(m.const_ready, 2)
                batches(pe, 0, BATCHES, 1, step)
                sums(BATCHES - 1, (BATCHES - 1) // SETS, (BATCHES - 1) % SETS)


def pooled_nodes(nc, t, sb, pb, g):
    x, hid, ident, eps, totals, valid, node_sum = (g[k] for k in ("x", "hid", "ident", "eps", "sums", "valid", "node_sum"))
    with ExitStack() as st:
        def s(name, shape, dt=F32):
            return sb("pn_" + name, shape, dt, st)
        sums = s("sums", (FR, H, CN))
        stats, mv, std, rstd = ln_buffers(s)
        padding, total, inv = s("padding", (P, NODE_TILES)), s("total", (P, CT, H)), s("inv", (P, CT, H))
        y, xn = s("y", (P, CT, D)), s("xn", (P, CT, D))
        nodes, col_ps = pb(st, "pn_nodes", (P, CT, 512)), pb(st, "pn_col", (P, 512))
        heads = nodes[:, :, 0:H * FR].rearrange("p u (h c) -> p u h c", c=FR)
        with phase(nc, "pn", "sums_laid", "turn", "padding_ready", "nodes_ready+pe", "step", "added+dve", "ln_step",
                   "std_ready", "kept+act", "cols_ready+pe", "cols_added+dve") as (block, m):
            @block.scalar
            def _(act):
                with act.Fori(0, CHUNKS) as c:
                    act.wait_ge(m.nodes_ready, c + FREE)
                    act.sem_inc(m.turn, 1)
                    act.activation(sums[:, :, :].rearrange("r h (b w) -> r b h w", w=W),
                                   totals[:, bass.ds(c * CB, CB), :].rearrange("r b (h w) -> r b h w", w=W),
                                   ACT.Copy).then_inc(m.sums_laid, 1)
                    deviations(act, c, mv, std, eps, m)
                    act.wait_ge(m.ln_step, c * 4 + 4)
                    act.activation(hid[:, bass.ds(c * CT, CT), :], xn[:, :, :], ACT.Copy).then_inc(m.kept, 1)

            @block.vector
            def _(v):
                v.memset(node_sum[:, :], 0.0).then_inc(m.padding_ready, 1)
                v.tensor_scalar(padding[:, :], valid[:, :], -1.0, 1.0, ALU.mult, ALU.add).then_inc(m.padding_ready, 1)
                v.wait_ge(m.padding_ready, 2)
                with v.Fori(0, CHUNKS) as c:
                    v.wait_ge(m.nodes_ready, c + (1 + FREE))
                    v.tensor_tensor(total[:, :, :], heads[:, :, :, DH], bc(padding[:, bass.ds(c * CT, CT)], 2, H),
                                    ALU.add).then_inc(m.step, 1)
                    v.wait_ge(m.step, c * 3 + 1)
                    v.reciprocal(inv[:, :, :], total[:, :, :]).then_inc(m.step, 1)
                    v.wait_ge(m.step, c * 3 + 2)
                    for u in range(CT):
                        last = v.tensor_tensor(y[:, u, :].rearrange("p (h d) -> p h d", h=H), heads[:, u, :, 0:DH],
                                               bc(inv[:, u, :], 2, DH), ALU.mult)
                    last.then_inc(m.step, 1)
                    v.wait_ge(m.step, c * 3 + 3)
                    xc = x[:, bass.ds(c * CT, CT), :]
                    v.tensor_tensor(xc, xc, y[:, :, :], ALU.add).then_inc(m.added, 1)
                    v.wait_ge(m.added, c + (1 + FREE))
                    v.wait_ge(m.kept, c + FREE)
                    v.wait_ge(m.cols_ready, c + FREE)
                    v.sem_inc(m.turn, 1)
                    normalize(v, c, lambda u: x[:, bass.ds(c * CT + u, 1), :].rearrange("p a d -> p (a d)"),
                              xn, stats, mv, std, rstd, eps, m)
                    v.wait_ge(m.cols_ready, c + (1 + FREE))
                    v.tensor_tensor(node_sum[:, :], node_sum[:, :], col_ps[:, 0:2], ALU.add).then_inc(m.cols_added, 1)
                    v.wait_ge(m.cols_added, c + (1 + FREE))

            @block.tensor
            def _(pe):
                with pe.Fori(0, CHUNKS) as c:
                    pe.wait_ge(m.sums_laid, c + 1)
                    pe.wait_ge(m.added, c + FREE)
                    for u in range(CT):
                        for h in range(H):
                            last = pe.transpose(nodes[:, u, h * FR:(h + 1) * FR], sums[:, h, u * P:(u + 1) * P], ident[0:FR, 0:FR])
                    last.then_inc(m.nodes_ready, 1)
                    pe.wait_ge(m.ln_step, c * 4 + 4)
                    pe.wait_ge(m.cols_added, c + FREE)
                    for k in range(2):
                        for u in range(CT):
                            last = pe.matmul(col_ps[:, k:k + 1], xn[:, u, k * P:(k + 1) * P], valid[:, bass.ds(c * CT + u, 1)],
                                             start=u == 0, stop=u == CT - 1)
                    last.then_inc(m.cols_ready, 1)


def routed_ffn(nc, t, sb, pb, g, out):
    x, hid, ident, eps, node_sum = (g[k] for k in ("x", "hid", "ident", "eps", "node_sum"))
    with ExitStack() as st:
        def s(name, shape, dt=F32):
            return sb("rf_" + name, shape, dt, st)
        wr, br, iota = s("wr", (P, 2, EX1)), s("br", (1, EX1)), s("iota", (1, EX1))
        r = s("r", (1, 14, EX1))
        c1 = s("c1", (1, 14))
        pick = s("pick", (1, 2), I32)
        ones = s("ones", (1, P))
        wts, ws = s("wts", (1, 2)), s("ws", (P, 2))
        f1w, f2w, f1, f2 = s("f1w", (P, 2, 2, FF)), s("f2w", (P, 2, FC, D)), s("f1", (P, 2, FC)), s("f2", (P, 2, D))
        f2s, bias = s("f2s", (P, 2, FC, D)), s("bias", (P, 2, D))
        with ExitStack() as ps_st, phase(nc, "ro", "loaded", "ones_ready", "logits_ready", "step", "exp_ready", "picked", "weights_ready",
                                         "experts_loaded", "spread_ready", "ws_ready", "scaled") as (block, m):
            lg_ps, ws_ps = pb(ps_st, "ro_lg", (P, 512)), pb(ps_st, "ro_ws", (P, 512))

            @block.sync
            def _(sp):
                sp.dma_start(wr[:, :, :], t["Wr"]).then_inc(m.loaded, 16)
                sp.dma_start(br[:, :], t["br"]).then_inc(m.loaded, 16)
                sp.dma_start(iota[:, :], t["c_iota_e"][0:1, 0:EX1]).then_inc(m.loaded, 16)
                sp.wait_ge(m.picked, 2)
                for e in range(2):
                    w = sp.value_load(pick[0:1, e:e + 1], min_val=0, max_val=EX1 - 1)
                    one = bass.ds(w, 1)
                    sp.dma_start(f1w[:, e, :, :], t["F1"][one].rearrange("a p k n -> p (a k) n")).then_inc(m.experts_loaded, 16)
                    sp.dma_start(f2w[:, e, :, :], t["F2"][one].rearrange("a p k n -> p (a k) n")).then_inc(m.experts_loaded, 16)
                    sp.dma_start(f1[:, e, :], t["f1"][one].rearrange("a p k -> p (a k)")).then_inc(m.experts_loaded, 16)
                    sp.dma_start(f2[:, e, :], t["f2"][one].rearrange("a p k -> p (a k)")).then_inc(m.experts_loaded, 16)
                sp.wait_ge(m.experts_loaded, 128)

            @block.tensor
            def _(pe):
                pe.wait_ge(m.loaded, 48)
                for k in range(2):
                    last = pe.matmul(lg_ps[0:1, 0:EX1], node_sum[:, k:k + 1], wr[:, k, :], start=k == 0, stop=k == 1)
                last.then_inc(m.logits_ready, 1)
                pe.wait_ge(m.ones_ready, 1)
                pe.wait_ge(m.weights_ready, 2)
                pe.matmul(ws_ps[:, 0:2], ones[0:1, :], wts[0:1, :], start=True, stop=True).then_inc(m.spread_ready, 1)

            @block.scalar
            def _(act):
                for n, (src, dst, neg, tot) in enumerate(((0, 1, 0, 1), (4, 5, 2, 3))):
                    act.wait_ge(m.step, 2 if n == 0 else 9)
                    act.activation(r[0:1, dst, :], r[0:1, src, :], ACT.Exp, bias=c1[0:1, neg:neg + 1],
                                   accum_out=c1[0:1, tot:tot + 1]).then_inc(m.exp_ready, 1)
                act.wait_ge(m.step, 21)
                act.activation(c1[0:1, 10:11], c1[0:1, 9:10], ACT.Exp).then_inc(m.exp_ready, 1)
                act.wait_ge(m.ws_ready, 1)
                act.wait_ge(m.experts_loaded, 128)
                for e in range(2):
                    act.activation(f2s[:, e, :, :], f2w[:, e, :, :], ACT.Copy, scale=ws[:, e:e + 1])

            @block.vector
            def _(v):
                done = [0]

                def then(ins):
                    done[0] += 1
                    ins.then_inc(m.step, 1)
                    v.wait_ge(m.step, done[0])

                def row(i):
                    return r[0:1, i, :]

                def one(i):
                    return c1[0:1, i:i + 1]
                v.memset(ones[:, :], 1.0).then_inc(m.ones_ready, 1)
                v.wait_ge(m.loaded, 48)
                v.wait_ge(m.logits_ready, 1)
                then(v.scalar_tensor_tensor(row(0), lg_ps[0:1, 0:EX1], 1.0 / N, br[0:1, :], ALU.mult, ALU.add))
                then(v.tensor_reduce(one(0), row(0), axis=AX.X, op=ALU.max, negate=True))
                v.wait_ge(m.exp_ready, 1)
                then(v.reciprocal(one(4), one(1)))
                then(v.tensor_scalar(row(2), row(1), one(4), None, ALU.mult))
                then(v.tensor_single_scalar(row(3), row(2), float(N), ALU.mult))
                then(v.reciprocal(row(6), row(3)))
                then(v.tensor_scalar(row(7), row(6), CAPACITY, 1.0, ALU.mult, ALU.min))
                then(v.tensor_tensor(row(4), row(2), row(7), ALU.mult))
                then(v.tensor_reduce(one(2), row(4), axis=AX.X, op=ALU.max, negate=True))
                then(v.tensor_single_scalar(iota[0:1, :], iota[0:1, :], -float(EX1), ALU.add))
                v.wait_ge(m.exp_ready, 2)
                then(v.reciprocal(one(5), one(3)))
                then(v.tensor_scalar(row(8), row(5), one(5), None, ALU.mult))
                for n in range(2):
                    then(v.tensor_reduce(one(6 + n), row(8), axis=AX.X, op=ALU.max))
                    then(v.scalar_tensor_tensor(row(9), row(8), one(6 + n), iota[0:1, :], ALU.is_equal, ALU.mult))
                    then(v.tensor_reduce(one(8), row(9), axis=AX.X, op=ALU.min))
                    v.tensor_single_scalar(pick[0:1, n:n + 1], one(8), float(EX1), ALU.add).then_inc(m.picked, 1)
                    if n == 0:
                        then(v.tensor_scalar(row(10), iota[0:1, :], one(8), -4.0, ALU.is_equal, ALU.mult))
                        then(v.tensor_tensor(row(8), row(8), row(10), ALU.add))
                then(v.tensor_tensor(one(9), one(7), one(6), ALU.subtract))
                assert done[0] == 21, done
                v.wait_ge(m.exp_ready, 3)
                then(v.tensor_single_scalar(one(11), one(10), 1.0, ALU.add))
                then(v.reciprocal(one(12), one(11)))
                v.tensor_copy(wts[0:1, 0:1], one(12)).then_inc(m.weights_ready, 1)
                v.tensor_tensor(wts[0:1, 1:2], one(12), one(10), ALU.mult).then_inc(m.weights_ready, 1)
                v.wait_ge(m.spread_ready, 1)
                v.tensor_copy(ws[:, :], ws_ps[:, 0:2]).then_inc(m.ws_ready, 1)
                v.wait_ge(m.ws_ready, 1)
                v.wait_ge(m.experts_loaded, 128)
                then(v.tensor_scalar(bias[:, 1, :], f2[:, 0, :], ws[:, 0:1], None, ALU.mult))
                then(v.scalar_tensor_tensor(bias[:, 0, :], f2[:, 1, :], ws[:, 1:2], bias[:, 1, :], ALU.mult, ALU.add))

        gam, bet = s("gam", (P, D)), s("bet", (P, D))
        hb, hT, hs = s("hb", (P, CT, D)), s("hT", (P, 2, CN)), s("hs", (P, 2, FC, CN))
        stats, mv, std, rstd = ln_buffers(s)
        y, z = s("y", (P, CT, D)), s("z", (P, CT, D))
        banks, h_ps, prod = pb(st, "rf_banks", (P, 3, 512)), pb(st, "rf_h", (P, 2, 512)), pb(st, "rf_prod", (P, 3, 512))
        R = 2 * FC * 2
        with phase(nc, "rf", "loaded", "hb_ready", "turn", "banks_ready", "copied+act", "h_ready", "gelu_ready+act", "prod_ready+pe",
                   "biased+dve", "with_hid+dve", "ln_step", "std_ready", "scaled", "shifted", "summed", "stored+sp") as (block, m):
            @block.sync
            def _(sp):
                sp.dma_start(gam[:, :], t["gamma"]).then_inc(m.loaded, 16)
                sp.dma_start(bet[:, :], t["beta"]).then_inc(m.loaded, 16)
                with sp.Fori(0, CHUNKS) as c:
                    sp.wait_ge(m.summed, c + 1)
                    sp.dma_start(out[:, bass.ds(c * CT, CT), :], z[:, :, :]).then_inc(m.stored, 16)
                sp.wait_ge(m.stored, CHUNKS * 16 + FREE)

            @block.gpsimd
            def _(pool):
                with pool.Fori(0, CHUNKS) as c:
                    pool.wait_ge(m.copied, c * 3 + FREE)
                    pool.wait_ge(m.with_hid, c + FREE)
                    pool.sem_inc(m.turn, 1)
                    pool.tensor_copy(hb[:, :, :], hid[:, bass.ds(c * CT, CT), :]).then_inc(m.hb_ready, 1)

            @block.scalar
            def _(act):
                with act.Fori(0, CHUNKS) as c:
                    copy_transposed(act, c, banks, hT, m.banks_ready, m.copied)
                    act.wait_ge(m.prod_ready, c * 3 + FREE)
                    for n in range(R):
                        e, j, f = n // (2 * FC), n // 2 % FC, n % 2
                        act.wait_ge(m.h_ready, c * R + (n + 1))
                        act.activation(hs[:, e, j, f * HALF:(f + 1) * HALF], h_ps[:, f, 0:HALF], ACT.Gelu,
                                       bias=f1[:, e, j:j + 1]).then_inc(m.gelu_ready, 1)
                    deviations(act, c, mv, std, eps, m)

            @block.tensor
            def _(pe):
                with pe.Fori(0, CHUNKS) as c:
                    pe.wait_ge(m.hb_ready, c + 1)
                    transposed(pe, hb, banks, ident, m.banks_ready)
                    pe.wait_ge(m.copied, c * 3 + (3 + FREE))
                    for n in range(R):
                        e, j, f = n // (2 * FC), n // 2 % FC, n % 2
                        pe.wait_ge(m.gelu_ready, c * R + (max(n - 1, 0) + FREE))
                        for k in range(2):
                            last = pe.matmul(h_ps[:, f, 0:HALF], f1w[:, e, k, j * P:(j + 1) * P],
                                             hT[:, k, f * HALF:(f + 1) * HALF], start=k == 0, stop=k == 1)
                        last.then_inc(m.h_ready, 1)
                    pe.wait_ge(m.gelu_ready, c * R + (R + FREE))
                    pe.wait_ge(m.biased, c * 3 + FREE)
                    for u in range(CT):
                        for n in range(2 * FC):
                            last = pe.matmul(prod[:, u // 2, (u % 2) * D:(u % 2 + 1) * D], hs[:, n // FC, n % FC, u * P:(u + 1) * P],
                                             f2s[:, n // FC, n % FC, :], start=n == 0, stop=n == 2 * FC - 1)
                        if u % 2 or u == CT - 1:
                            last.then_inc(m.prod_ready, 1)

            @block.vector
            def _(v):
                v.wait_ge(m.loaded, 32)
                with v.Fori(0, CHUNKS) as c:
                    for b in range(3):
                        n = min(2, CT - 2 * b)
                        v.wait_ge(m.prod_ready, c * 3 + (b + 1 + FREE))
                        v.tensor_tensor(y[:, 2 * b:2 * b + n, :], prod[:, b, 0:n * D].rearrange("p (u d) -> p u d", u=n),
                                        bc(bias[:, 0, :], 1, n), ALU.add).then_inc(m.biased, 1)
                    v.wait_ge(m.biased, c * 3 + (3 + FREE))
                    v.wait_ge(m.stored, c * 16 + FREE)
                    v.tensor_tensor(z[:, :, :], y[:, :, :], hb[:, :, :], ALU.add).then_inc(m.with_hid, 1)
                    v.wait_ge(m.with_hid, c + (1 + FREE))
                    normalize(v, c, lambda u: z[:, u, :], y, stats, mv, std, rstd, eps, m)
                    v.wait_ge(m.ln_step, c * 4 + 4)
                    v.tensor_tensor(z[:, :, :], y[:, :, :], bc(gam[:, :], 1, CT), ALU.mult).then_inc(m.scaled, 1)
                    v.wait_ge(m.scaled, c + 1)
                    v.tensor_tensor(y[:, :, :], z[:, :, :], bc(bet[:, :], 1, CT), ALU.add).then_inc(m.shifted, 1)
                    v.wait_ge(m.shifted, c + 1)
                    v.tensor_tensor(z[:, :, :], y[:, :, :], x[:, bass.ds(c * CT, CT), :], ALU.add).then_inc(m.summed, 1)
                    v.wait_ge(m.summed, c + 1)


def host_layout(i):
    f = {k: np.ascontiguousarray(v) for k, v in i.items()}

    def edges(a, pad):
        out = np.full(P * EC, pad, a.dtype)
        out[:E] = a
        return out.reshape(P, EC)

    def rows(a):
        return np.ascontiguousarray(a.reshape(-1, P, a.shape[-1]).transpose(1, 0, 2))

    def spread(a):
        return np.ascontiguousarray(np.broadcast_to(a.reshape(1, -1), (P, a.size)))

    x = np.zeros((NP_, D), np.float32)
    x[:N] = f["x"]
    p = np.arange(P)
    t = {
        "x": x.reshape(NODE_TILES, P, D).transpose(1, 0, 2),
        "src": edges(f["src"], SRC_PAD), "dst": edges(f["dst"], 0), "edge_type": edges(f["edge_type_3"], 0),
        "edge_weight": edges(f["edge_weight"], 0),
        "c_ident": np.eye(P, dtype=np.float32),
        "c_before": np.triu(np.ones((P, P), np.float32), 1),
        "c_iota_b": spread(np.arange(BLOCKS, dtype=np.float32)),
        "c_iota_w": spread(np.arange(W, dtype=np.float32)),
        "c_iota_e": spread(np.arange(EX0, dtype=np.float32)),
        "c_tcol": (p[:, None] + P * np.arange(TG)[None]).astype(np.float32),
        "c_valid": (p[:, None] + P * np.arange(NODE_TILES)[None] < N).astype(np.float32),
        "c_owner": (np.arange(EX0)[:, None, None] == (2 * np.arange(HC)[:, None] + p[None] // H0)[None]).astype(np.float32),
        "Win": rows(f["L0_gnn_Win"].T), "b_in": spread(f["L0_gnn_b_in"]),
        "Wq": np.stack([rows(np.repeat(w.T.reshape(D, H, 1, DH), 2, 2).reshape(D, 2 * D)) for w in f["L0_gnn_Wq"]]),
        "bq": np.stack([np.concatenate([b.reshape(H, DH).T] * 2) for b in f["L0_gnn_bq"]]),
        "Wkv": np.stack([rows(np.concatenate([k.T, v.T], 1)) for k, v in zip(f["L0_gnn_Wk"], f["L0_gnn_Wv"])]),
        "bkv": np.stack([spread(np.concatenate([k, v])) for k, v in zip(f["L0_gnn_bk"], f["L0_gnn_bv"])]),
        "Wo": np.stack([np.concatenate([w.T.reshape(H, DH, D).transpose(1, 0, 2)] * 2) for w in f["L0_gnn_Wo"]]),
        "Ee": np.stack([e.reshape(3, H, DH).transpose(2, 1, 0) for e in f["L0_gnn_Eemb"]]),
        "bo": np.stack([spread(b)[:3] for b in f["L0_gnn_bo"]]),
        "ln_g": np.stack([spread(b) for b in f["L0_gnn_ln_g"]]),
        "ln_b": np.stack([spread(b) for b in f["L0_gnn_ln_b"]]),
        "A1": rows(f["L0_gnn_W1"].T), "a1": f["L0_gnn_b1"].reshape(2, P).T,
        "A2": rows(f["L0_gnn_W2"].T), "a2": spread(f["L0_gnn_b2"]),
        "router_w": rows(f["L0_ffn_router_w"].T), "router_b": spread(f["L0_ffn_router_b"]),
        "E1": rows(f["L0_ffn_W1"].transpose(1, 0, 2).reshape(D, EX0 * H0)),
        "e1": f["L0_ffn_b1"].reshape(HC, P).T,
        "E2": rows(f["L0_ffn_W2"].reshape(EX0 * H0, D)), "e2": f["L0_ffn_b2"],
        "Ws": rows(f["L1_gnn_Ws"].transpose(1, 0, 2).reshape(D, H * DH)), "bs": spread(f["L1_gnn_bs"]),
        "aw_s": spread(f["L1_gnn_aw"][:, :DH]), "aw_d": spread(f["L1_gnn_aw"][:, DH:2 * DH]),
        "aw_e": spread(f["L1_gnn_aw"][:, 2 * DH]), "ab": spread(f["L1_gnn_ab"]),
        "Wr": rows(f["L1_ffn_Wr"]), "br": f["L1_ffn_br"].reshape(1, EX1),
        "F1": np.stack([rows(w) for w in f["L1_ffn_W1"]]),
        "f1": np.stack([b.reshape(FC, P).T for b in f["L1_ffn_b1"]]),
        "F2": np.stack([rows(w) for w in f["L1_ffn_W2"]]),
        "f2": np.stack([spread(b) for b in f["L1_ffn_b2"]]),
        "gamma": spread(f["L1_ffn_gamma"]), "beta": spread(f["L1_ffn_beta"]),
    }
    return {k: np.ascontiguousarray(v) for k, v in t.items()}


def kernel(**inputs):
    import concourse.bacc as bacc
    from concourse.bass_utils import run_bass_kernel_spmd

    nc = bacc.Bacc("TRN2", target_bir_lowering=False, num_devices=1)
    arrays = {f"in_{k}": v for k, v in host_layout(inputs).items()}
    t = {k[3:]: nc.dram_tensor(k, list(a.shape), mybir.dt.from_np(a.dtype), kind="ExternalInput").ap()
         for k, a in arrays.items()}
    out = nc.dram_tensor("out_x", [P, NODE_TILES, D], F32, kind="ExternalOutput").ap()
    build(nc, t, out)
    got = run_bass_kernel_spmd(nc, [arrays], core_ids=[0]).results[0]["out_x"]
    return np.asarray(got).transpose(1, 0, 2).reshape(NP_, D)[:N]
```

```python
from contextlib import ExitStack, contextmanager

import numpy as np

import concourse.bass as bass
from concourse import mybir

F32, BF16, I32 = mybir.dt.float32, mybir.dt.bfloat16, mybir.dt.int32
ALU = mybir.AluOpType
ACT = mybir.ActivationFunctionType
AX = mybir.AxisListType

P = 128
N, D, E = 3125, 256, 53125
H, DH, LAYERS = 4, 64, 3
W = 16
HW = H * W
NODE_TILES = -(-N // P)
NP_ = NODE_TILES * P
BLOCKS = NP_ // W
CT = 5
CHUNKS = NODE_TILES // CT
CN = CT * P
CB = CN // W
HALF = CN // 2
EC = -(-E // P)
BT = 4
FULL_BLOCKS = -(-N // W)
TILES = -(-((E - 1) // P + FULL_BLOCKS) // BT) * BT
BATCHES = TILES // BT
TG = -(-(TILES + BT) // P)
SETS = 6
FEW = 3
TW = 3 * W
FR = DH + 1
HB = 32
FROW = H * FR + H
BIG = 1e30
REC = 3
FREE = 1
EPS = 1e-5
EX0, H0 = 32, 64
XTILES = (NP_ + EX0 * (P - 1)) // P
XSETS = 8
XW = 2 * H0 + D + 1
EX1, FF = 8, 512
FC = FF // P
CAPACITY = float(-(-N * 5 // (4 * EX1)))
SRC_PAD = 4000
NOBODY = 4095
assert XTILES % XSETS == 0 and XSETS % 2 == 0 and SRC_PAD // W >= BLOCKS and NOBODY >= NP_ and CHUNKS * CT == NODE_TILES and EC % 8 == 0


@contextmanager
def phase(nc, title, *names):
    sems = {}
    for name in names:
        name, _, many = name.partition("*")
        name, _, producer = name.partition("+")
        made = [nc.alloc_semaphore(f"{title}_{name}{i}") for i in range(int(many or 1))]
        sems[name] = made if many else made[0]
        if producer:
            engine = {"pe": nc.tensor, "act": nc.scalar, "dve": nc.vector, "pool": nc.gpsimd, "sp": nc.sync}[producer]
            for sem in made:
                engine.sem_inc(sem, FREE)
    flat = [s for x in sems.values() for s in (x if isinstance(x, list) else [x])]
    with nc.Block() as block:
        yield block, type("Sems", (), sems)
    nc.clear_and_free_semaphores(flat)
    nc.all_engine_barrier()


def batches(eng, first, last, peel, step, turn=SETS):
    mid = (last - first - peel) // turn
    for b in range(first, first + peel):
        step(b, b // turn, b % turn)
    b0 = first + peel
    if mid:
        with eng.Fori(0, mid) as i:
            for j in range(turn):
                step(i * turn + (b0 + j), i + (b0 + j) // turn, (b0 + j) % turn)
    for b in range(b0 + mid * turn, last):
        step(b, b // turn, b % turn)


def after(b, k):
    return not isinstance(b, int) or b >= k


def bc(ap, axis, count):
    a = ap.unsqueeze(axis)
    shape = list(a.shape)
    shape[axis] = count
    return a.broadcast_to(shape)


def build(nc, t, out):
    ctx = ExitStack()

    def dram(name, shape, dt=F32):
        return nc.dram_tensor(name, list(shape), dt, kind="Internal").ap()

    slot_d = dram("slot_table", (P * TILES, REC))
    blk_d = dram("tile_block", (TG * P,), I32)
    keep_d = dram("tile_keep", (TG * P,))
    kv_d = dram("kv_table", (NP_, 2 * D))
    q_d = dram("q_blocks", (BLOCKS * P, P))
    x_d = dram("x_kept", (P, NODE_TILES, D))
    f_d = dram("feature_table", (NP_, FROW))
    as_d = dram("a_src", (3, NP_, H), BF16)
    xs_d = dram("expert_in", (XTILES * P, D))
    xo_d = dram("expert_out", (XTILES * P, D))
    xt_d = dram("tile_expert", (P,), I32)
    p_d = dram("pooled_sums", (BLOCKS, W, H, FR))

    with ctx:
        def sb(name, shape, dt=F32, stack=ctx):
            return stack.enter_context(nc.sbuf_tensor(name, list(shape), dt))

        def pb(stack, name, shape, dt=F32):
            return stack.enter_context(nc.psum_tensor(name, list(shape), dt))

        hid = sb("hid", (P, NODE_TILES, D))
        ident = sb("ident", (P, P))
        ident_big = sb("ident_big", (P, P), BF16)
        iota_w = sb("iota_w", (P, W))
        valid = sb("valid", (P, NODE_TILES))
        eps = sb("eps", (P, 1))
        keep = sb("keep", (P, TG * P))
        tile_blk = sb("tile_blk", (1, TG * P), I32)
        slot_dst = sb("slot_dst", (P, TILES + BT), I32)
        slot_weight = sb("slot_weight", (P, TILES))
        marks = sb("marks", (P, TILES, W), BF16)
        kv = sb("kv", (P, SETS, BT, 2 * D))
        node_sum = sb("node_sum", (P, 2))
        before_b = sb("before_b", (P, P), BF16)
        ones_b = sb("ones_b", (P, P), BF16)

        with ExitStack() as layers_st:
            type_counts = sb("type_counts", (TW, BLOCKS, W), F32, layers_st)
            with ExitStack() as st:
                x = sb("x_in", (P, NODE_TILES, D), F32, st)
                edge_sort(nc, t, sb, pb, locals())
                hidden_in(nc, t, sb, pb, locals())
            with nc.Fori(0, LAYERS) as layer:
                qkv(nc, t, sb, pb, locals(), layer)
                with ExitStack() as st:
                    sums = sb("sums", (P, BLOCKS, HW), F32, st)
                    attention_edges(nc, t, sb, pb, locals())
                    node_update(nc, t, sb, pb, locals(), layer)
        x = sb("x", (P, NODE_TILES, D))
        adjustment(nc, t, sb, pb, locals())
        with ExitStack() as st:
            expert = sb("expert", (P, NODE_TILES, EX0), F32, st)
            slot = sb("expert_slot", (P, NODE_TILES), I32, st)
            tile_expert = sb("tile_expert_row", (1, P), I32, st)
            expert_logits(nc, t, sb, pb, locals())
            expert_sort(nc, t, sb, pb, locals())
            expert_tiles(nc, t, sb, pb, locals())
            expert_add(nc, t, sb, pb, locals())
        features(nc, t, sb, pb, locals())
        with ExitStack() as st:
            sums = sb("pooled", (P, BLOCKS, FR), F32, st)
            pooling_edges(nc, t, sb, pb, locals())
            pooled_nodes(nc, t, sb, pb, locals())
        routed_ffn(nc, t, sb, pb, locals(), out)


def tile_blocks(nc, engine, table, b):
    return nc.values_load_multi_w_load_instructions(
        table[0:1, bass.ds(b * BT, BT)], engines=(engine,), min_val=0, max_val=BLOCKS - 1,
        skip_runtime_bounds_check_because="the table is clamped to the blocks where it is made")[1]


def edge_sort(nc, t, sb, pb, g):
    slot_d, blk_d, keep_d, slot_dst, slot_weight, marks = (g[k] for k in ("slot_d", "blk_d", "keep_d", "slot_dst", "slot_weight", "marks"))
    x, ident, iota_w, valid, eps = (g[k] for k in ("x", "ident", "iota_w", "valid", "eps"))
    G16, COLS, HIGH, LOW = 16, 4, 32, 8
    with ExitStack() as st:
        def s(name, shape, dt=F32):
            return sb(name, shape, dt, st)
        src = s("src_i", (P, EC), I32)
        dst = s("dst_i", (P, EC), I32)
        ety = s("ety_i", (P, EC), I32)
        ewt = s("edge_w", (P, EC))
        blk = s("edge_blk", (P, EC), I32)
        loc = s("edge_loc", (P, EC), I32)
        blk_f = s("edge_blk_f", (P, EC + 4))
        rec = s("rec", (P, EC, REC))
        kind = s("kind", (P, EC + 4))
        iota_b = s("iota_b", (P, BLOCKS))
        onehot = s("onehot", (P, 2, 8, BLOCKS), BF16)
        before = s("before", (P, P))
        before_b, ones_b = g["before_b"], g["ones_b"]
        zeros = s("zeros", (P, BLOCKS))
        zeros_b = s("zeros_b", (P, P), BF16)
        empty = s("empty", (P, TILES, REC))
        diagonal = s("diagonal", (P, W))
        count = s("count", (P, BLOCKS))
        count_i = s("count_i", (P, BLOCKS), I32)
        tiles = s("tiles", (P, BLOCKS))
        t_end = s("t_end", (P, BLOCKS))
        t_base = s("t_base", (P, BLOCKS))
        s_base = s("s_base", (P, BLOCKS))
        tcol = s("tcol", (P, TG))
        cmp = s("cmp", (P, 2, TG, BLOCKS))
        cols = s("cols", (P, 3, TG))
        cols_i = s("cols_i", (P, TG), I32)

        with ExitStack() as ps_st, phase(
                nc, "count", "loaded", "x_loaded", "const_ready", "filled", "empty_ready", "split", "parts", "hot*2",
                "counted+pe*2", "digits_ready", "own_ready", "sum_ready", "type_ready", "local_ready") as (block, m):
            hist, pairs = pb(ps_st, "hist", (P, 512)), pb(ps_st, "pairs", (P, 512))

            def own(name, shape, dt=F32):
                return sb(name, shape, dt, ps_st)
            high, low, low_i = own("high", (P, EC)), own("low", (P, EC)), own("low_i", (P, EC), I32)
            high_i, iota_h, same, spread_c = own("high_i", (P, EC), I32), own("iota_h", (P, HIGH)), own("same", (P, COLS)), own("spread_c", (P, HIGH))
            picked, digit, by_block = own("picked", (P, COLS, LOW)), own("digit", (P, LOW)), own("by_block", (P, BLOCKS))
            ones = own("ones", (P, P))
            hot_h = [onehot[:, j, 0:4, :].rearrange("p a b -> p (a b)")[:, 0:G16 * HIGH].rearrange("p (c h) -> p c h", h=HIGH) for j in range(2)]
            hot_l = [onehot[:, j, 4:8, :].rearrange("p a b -> p (a b)")[:, 0:G16 * LOW].rearrange("p (c h) -> p c h", h=LOW) for j in range(2)]

            @block.sync
            def _(sp):
                for a, b in ((src, t["src"]), (dst, t["dst"]), (ety, t["edge_type"]), (ewt, t["edge_weight"]), (iota_b, t["c_iota_b"]),
                             (before, t["c_before"]), (tcol, t["c_tcol"]), (ident, t["c_ident"]),
                             (iota_w, t["c_iota_w"]), (valid, t["c_valid"]), (iota_h, t["c_iota_e"]), (same, t["c_same"]),
                             (spread_c, t["c_spread"]), (diagonal, t["c_diagonal"])):
                    sp.dma_start(a[:, :], b).then_inc(m.loaded, 16)
                sp.dma_start(x[:, :, :], t["x"]).then_inc(m.x_loaded, 16)
                sp.wait_ge(m.empty_ready, 1)
                sp.dma_start(slot_d.rearrange("(p t) f -> p t f", p=P), empty[:, :, :]).then_inc(m.filled, 16)
                sp.wait_ge(m.x_loaded, 16)
                sp.wait_ge(m.filled, 16)

            @block.gpsimd
            def _(pool):
                pool.memset(ones_b[:, :], 1.0)
                pool.memset(zeros[:, :], 0.0)
                pool.memset(eps[:, :], EPS)
                pool.memset(ones[:, :], 1.0)
                pool.memset(zeros_b[:, :], 0.0).then_inc(m.const_ready, 1)
                pool.memset(blk_f[:, EC:EC + 4], float(BLOCKS))
                pool.memset(empty[:, :, 0], float(NOBODY))
                pool.memset(empty[:, :, 1], 99.0)
                pool.memset(kind[:, EC:EC + 4], 0.0)
                pool.memset(empty[:, :, 2], 0.0).then_inc(m.empty_ready, 1)
                pool.memset(g["kv"][:, :, :, :], 0.0)

            @block.scalar
            def _(act):
                act.wait_ge(m.loaded, 224)
                act.activation(before_b[:, :], before[:, :], ACT.Copy)
                act.activation(kind[:, 0:EC], ety[:, :], ACT.Copy, scale=float(W)).then_inc(m.type_ready, 1)
                act.activation(rec[:, :, 0], dst[:, :], ACT.Copy)
                act.activation(rec[:, :, 2], ewt[:, :], ACT.Copy)

            @block.vector
            def _(v):
                v.wait_ge(m.loaded, 224)
                v.tensor_single_scalar(blk[:, :], src[:, :], 4, ALU.logical_shift_right).then_inc(m.split, 1)
                v.tensor_single_scalar(loc[:, :], src[:, :], W - 1, ALU.bitwise_and).then_inc(m.split, 1)
                v.wait_ge(m.split, 2)
                v.tensor_single_scalar(high_i[:, :], blk[:, :], 3, ALU.logical_shift_right).then_inc(m.split, 1)
                v.tensor_single_scalar(low_i[:, :], blk[:, :], LOW - 1, ALU.bitwise_and).then_inc(m.split, 1)
                v.wait_ge(m.split, 4)
                v.tensor_copy(high[:, :], high_i[:, :]).then_inc(m.parts, 1)
                v.tensor_copy(low[:, :], low_i[:, :]).then_inc(m.parts, 1)
                v.wait_ge(m.parts, 2)
                with v.Fori(0, EC // (2 * G16)) as i:
                    for j in range(2):
                        v.wait_ge(m.counted[j], i + FREE)
                        cols = bass.ds((i * 2 + j) * G16, G16)
                        v.tensor_tensor(hot_h[j], bc(iota_h[:, :], 1, G16), bc(high[:, cols], 2, HIGH), ALU.is_equal).then_inc(m.hot[j], 1)
                        v.tensor_tensor(hot_l[j], bc(iota_h[:, 0:LOW], 1, G16), bc(low[:, cols], 2, LOW), ALU.is_equal).then_inc(m.hot[j], 1)
                v.tensor_copy(blk_f[:, 0:EC], blk[:, :])
                v.tensor_copy(rec[:, :, 1], loc[:, :]).then_inc(m.local_ready, 1)
                v.wait_ge(m.type_ready, 1)
                v.wait_ge(m.local_ready, 1)
                v.tensor_tensor(kind[:, 0:EC], kind[:, 0:EC], rec[:, :, 1], ALU.add)
                v.wait_ge(m.digits_ready, 1)
                v.tensor_tensor(picked[:, :, :], pairs[:, 0:COLS * LOW].rearrange("p (c l) -> p c l", l=LOW), bc(same[:, :], 2, LOW),
                                ALU.mult).then_inc(m.parts, 1)
                v.wait_ge(m.parts, 3)
                v.tensor_reduce(digit[:, :], picked[:, :, :].rearrange("p c l -> p l c"), axis=AX.X, op=ALU.add).then_inc(m.parts, 1)
                v.wait_ge(m.parts, 4)
                v.tensor_tensor(by_block[:, :].rearrange("p (h l) -> p h l", l=LOW), bc(digit[:, :], 1, BLOCKS // LOW),
                                bc(spread_c[:, 0:BLOCKS // LOW], 2, LOW), ALU.mult).then_inc(m.own_ready, 1)
                v.wait_ge(m.sum_ready, 1)
                v.tensor_copy(count[:, :], hist[:, 0:BLOCKS]).then_inc(m.split, 1)
                v.wait_ge(m.split, 5)
                v.tensor_single_scalar(tiles[:, :], count[:, :], float(P - 1), ALU.add).then_inc(m.split, 1)
                v.wait_ge(m.split, 6)
                v.tensor_copy(count_i[:, :], tiles[:, :]).then_inc(m.split, 1)
                v.wait_ge(m.split, 7)
                v.tensor_single_scalar(count_i[:, :], count_i[:, :], 7, ALU.logical_shift_right).then_inc(m.split, 1)
                v.wait_ge(m.split, 8)
                v.tensor_single_scalar(tiles[:, 0:FULL_BLOCKS], count_i[:, 0:FULL_BLOCKS], 1.0, ALU.max)
                v.memset(tiles[:, FULL_BLOCKS:BLOCKS], 0.0).then_inc(m.split, 1)
                v.wait_ge(m.split, 9)
                v.wait_ge(m.const_ready, 1)
                v.tensor_tensor_scan(t_end[:, :], tiles[:, :], zeros[:, :], 0.0, ALU.add, ALU.add).then_inc(m.split, 1)
                v.wait_ge(m.split, 10)
                v.tensor_tensor(t_base[:, :], t_end[:, :], tiles[:, :], ALU.subtract).then_inc(m.split, 1)
                v.wait_ge(m.split, 11)
                v.tensor_single_scalar(s_base[:, :], t_base[:, :], float(P), ALU.mult).then_inc(m.split, 1)

            @block.tensor
            def _(pe):
                pe.wait_ge(m.const_ready, 1)
                pe.matmul(pairs[:, 0:COLS * LOW], ones_b[:, :], zeros_b[:, 0:COLS * LOW], start=True, stop=False)
                with pe.Fori(0, EC // (2 * G16)) as i:
                    for j in range(2):
                        pe.wait_ge(m.hot[j], i * 2 + 2)
                        for c in range(0, G16, COLS):
                            last = pe.matmul(pairs[:, 0:COLS * LOW], hot_h[j][:, c:c + COLS, :].rearrange("p c h -> p (c h)"),
                                             hot_l[j][:, c:c + COLS, :].rearrange("p c l -> p (c l)"), start=False, stop=False)
                        last.then_inc(m.counted[j], 1)
                pe.matmul(pairs[:, 0:COLS * LOW], ones_b[:, :], zeros_b[:, 0:COLS * LOW], start=False, stop=True).then_inc(m.digits_ready, 1)
                pe.wait_ge(m.own_ready, 1)
                pe.matmul(hist[:, 0:BLOCKS], ones[:, :], by_block[:, :], start=True, stop=True).then_inc(m.sum_ready, 1)

        with phase(nc, "tables", "step", "stored", "loaded") as (block, m):
            tb = bc(tcol[:, :], 2, BLOCKS)

            @block.vector
            def _(v):
                v.tensor_tensor(cmp[:, 0, :, :], bc(t_end[:, :], 1, TG), tb, ALU.is_le).then_inc(m.step, 1)
                v.tensor_tensor(cmp[:, 1, :, :], bc(t_base[:, :], 1, TG), tb, ALU.is_equal).then_inc(m.step, 1)
                v.wait_ge(m.step, 2)
                v.tensor_reduce(cols[:, 0:2, :], cmp[:, :, :, :], axis=AX.X, op=ALU.add).then_inc(m.step, 1)
                v.wait_ge(m.step, 3)
                v.tensor_single_scalar(cols_i[:, :], cols[:, 0, :], float(BLOCKS - 1), ALU.min).then_inc(m.step, 1)
                v.tensor_scalar(cols[:, 1, :], cols[:, 1, :], -1.0, 1.0, ALU.mult, ALU.add).then_inc(m.step, 1)
                v.wait_ge(m.step, 5)
                v.tensor_single_scalar(cols[:, 2, :], cols[:, 1, :], 0.0, ALU.max).then_inc(m.step, 1)

            @block.sync
            def _(sp):
                sp.wait_ge(m.step, 6)
                with nc.allow_non_contiguous_dma("tile tables, once"):
                    sp.dma_start(blk_d.rearrange("(g p) -> p g", p=P), cols_i[:, :]).then_inc(m.stored, 16)
                    sp.dma_start(keep_d.rearrange("(g p) -> p g", p=P), cols[:, 2, :]).then_inc(m.stored, 16)
                sp.wait_ge(m.stored, 32)
                sp.dma_start(g["tile_blk"][0:1, :], blk_d.unsqueeze(0)).then_inc(m.loaded, 16)
                sp.dma_start(g["keep"][:, :], keep_d.unsqueeze(0).broadcast_to([P, TG * P])).then_inc(m.loaded, 16)
                sp.wait_ge(m.loaded, 32)

        GR = 4
        TURNS = EC // GR
        ZEROS = 4 * D
        assert (XTILES * D + BLOCKS * P) % ZEROS == 0 and (XTILES * D + BLOCKS * P) // ZEROS <= TURNS // 2
        pos = s("pos", (P, 2, GR))
        pos_i = s("pos_i", (P, 2, 3, GR), I32)
        beyond = s("beyond", (P, 2, GR))
        idx = s("idx", (P, 2, GR), I32)
        rec_c = s("rec_c", (P, 2, GR, REC))
        hot_kind = s("hot_kind", (P, 2, GR, TW), BF16)
        prod = s("prod", (P, GR, BLOCKS))
        given = s("given", (64, 2, BLOCKS), BF16)
        pick = s("pick", (64, P), BF16)
        with ExitStack() as ps_st, phase(
                nc, "place", "hot*2", "pick_ready", "ranked+dve", "prior*4", "totaled+pe", "high_ready", "given_ready", "turn", "step", "cleared",
                "idx_ready*2", "written*2", "kinds_ready") as (block, m):
            taken = pb(ps_st, "taken", (P, GR, 512))
            total = pb(ps_st, "total", (P, 2, 512))
            kinds = pb(ps_st, "kinds", (P, 512))

            @block.sync
            def _(sp):
                zero = g["kv"][:, :, :, :].rearrange("p a b c -> p (a b c)")
                xs_flat = g["xs_d"].rearrange("(p u) d -> p (u d)", p=P)
                q_flat = g["q_d"].rearrange("(p b) c -> p (b c)", p=P)
                xs_parts, q_parts = XTILES * D // ZEROS, BLOCKS * P // ZEROS
                for first, parts, flat in ((0, xs_parts, xs_flat), (xs_parts, q_parts, q_flat)):
                    with sp.Fori(0, parts) as i:
                        sp.wait_ge(m.idx_ready[0], i + (first + 1))
                        sp.dma_start(flat[:, bass.ds(i * ZEROS, ZEROS)], zero[:, 0:ZEROS]).then_inc(m.cleared, 16)
                sp.wait_ge(m.cleared, (xs_parts + q_parts) * 16)

            @block.scalar
            def _(act):
                act.activation(given[:, 0, :], s_base[0:64, :], ACT.Copy).then_inc(m.high_ready, 1)
                with act.Fori(0, TURNS // 2) as it:
                    for j in range(2):
                        act.wait_ge(m.totaled, it * 2 + (j + 1 + FREE))
                        act.activation(given[:, 1 - j, :], total[0:64, j, 0:BLOCKS], ACT.Copy).then_inc(m.high_ready, 1)

            @block.vector
            def _(v):
                def hot(i, j):
                    v.tensor_tensor(hot_kind[:, j, :, :], bc(iota_b[:, 0:TW], 1, GR),
                                    bc(kind[:, bass.ds(i * GR, GR)], 2, TW), ALU.is_equal).then_inc(m.hot[j], 1)
                    v.tensor_tensor(onehot[:, j, 0:GR, :], bc(iota_b[:, :], 1, GR),
                                    bc(blk_f[:, bass.ds(i * GR, GR)], 2, BLOCKS), ALU.is_equal).then_inc(m.hot[j], 1)
                v.memset(pick[:, :], 0.0).then_inc(m.pick_ready, 1)
                v.wait_ge(m.pick_ready, 1)
                v.memset(pick[0:1, :], 1.0)
                v.memset(pick[32:33, :], 1.0).then_inc(m.pick_ready, 1)
                v.wait_ge(m.high_ready, 1)
                v.tensor_tensor(given[32:64, 0, :], s_base[32:64, :], given[32:64, 0, :], ALU.subtract).then_inc(m.given_ready, 1)
                hot(0, 0)
                def turn(it, j):
                    i = it * 2 + j
                    v.wait_ge(m.totaled, i + FREE)
                    hot(i + 1, 1 - j)
                    v.wait_ge(m.high_ready, i + 2)
                    v.tensor_tensor(given[32:64, 1 - j, :], total[32:64, j, 0:BLOCKS], given[32:64, 1 - j, :],
                                    ALU.subtract).then_inc(m.given_ready, 1)
                    v.wait_ge(m.hot[j], it * 2 + 2)
                    for k in range(GR):
                        v.wait_ge(m.prior[k], i + 1)
                        v.tensor_tensor_reduce(out=prod[:, k, :], in0=onehot[:, j, k, :],
                                               in1=taken[:, k, 0:BLOCKS], scale=1.0, scalar=0.0, op0=ALU.mult,
                                               op1=ALU.add, accum_out=pos[:, j, k:k + 1]).then_inc(m.ranked, 1)
                    v.tensor_scalar(beyond[:, j, :], blk_f[:, bass.ds(i * GR, GR)], float(BLOCKS) - 0.5,
                                    float(1 << 24), ALU.is_ge, ALU.mult).then_inc(m.step, 1)
                    v.wait_ge(m.step, i * 4 + 1)
                    v.wait_ge(m.ranked, i * GR + (GR + FREE))
                    v.tensor_tensor(pos_i[:, j, 0, :], pos[:, j, :], beyond[:, j, :], ALU.add).then_inc(m.step, 1)
                    v.wait_ge(m.step, i * 4 + 2)
                    v.tensor_single_scalar(pos_i[:, j, 1, :], pos_i[:, j, 0, :], P - 1, ALU.bitwise_and)
                    v.tensor_single_scalar(pos_i[:, j, 2, :], pos_i[:, j, 0, :], 7,
                                           ALU.logical_shift_right).then_inc(m.step, 1)
                    v.wait_ge(m.step, i * 4 + 3)
                    if after(it, 1):
                        v.wait_ge(m.written[j], it * (16 * GR))
                    v.scalar_tensor_tensor(idx[:, j, :], pos_i[:, j, 1, :], float(TILES), pos_i[:, j, 2, :],
                                           ALU.mult, ALU.add).then_inc(m.step, 1)
                    v.tensor_copy(rec_c[:, j, :, :], rec[:, bass.ds(i * GR, GR), :]).then_inc(m.idx_ready[j], 1)
                    v.wait_ge(m.step, i * 4 + 4)

                for j in range(2):
                    turn(0, j)
                with v.Fori(0, TURNS // 2 - 1) as it:
                    for j in range(2):
                        turn(it + 1, j)
                v.wait_ge(m.kinds_ready, 1)
                v.tensor_tensor(g["type_counts"][:, :, :], bc(kinds[0:TW, 0:BLOCKS], 2, W), bc(diagonal[0:TW, :], 1, BLOCKS), ALU.mult)

            @block.tensor
            def _(pe):
                nothing = bc(zeros_b[:, 0:BLOCKS // 2], 1, 2)
                pe.matmul(kinds[0:TW, 0:BLOCKS], zeros_b[:, 0:TW], nothing, start=True, stop=False)
                pe.wait_ge(m.pick_ready, 2)
                with pe.Fori(0, TURNS // 2) as it:
                    for j in range(2):
                        i = it * 2 + j
                        pe.wait_ge(m.hot[j], it * 2 + 2)
                        pe.wait_ge(m.given_ready, i + 1)
                        pe.matmul(total[:, j, 0:BLOCKS], pick[:, :], given[:, j, :], start=True, stop=False)
                        for e in range(GR):
                            last = pe.matmul(total[:, j, 0:BLOCKS], ones_b[:, :], onehot[:, j, e, :],
                                             start=False, stop=e == GR - 1)
                        last.then_inc(m.totaled, 1)
                        for e in range(GR):
                            pe.matmul(kinds[0:TW, 0:BLOCKS], hot_kind[:, j, e, :], onehot[:, j, e, :], start=False, stop=False)
                        for k in range(GR):
                            if k == 0:
                                pe.wait_ge(m.ranked, i * GR + FREE)
                            pe.matmul(taken[:, k, 0:BLOCKS], pick[:, :], given[:, j, :], start=True, stop=False)
                            for e in range(k):
                                pe.matmul(taken[:, k, 0:BLOCKS], ones_b[:, :], onehot[:, j, e, :],
                                          start=False, stop=False)
                            pe.matmul(taken[:, k, 0:BLOCKS], before_b[:, :], onehot[:, j, k, :],
                                             start=False, stop=True).then_inc(m.prior[k], 1)
                pe.matmul(kinds[0:TW, 0:BLOCKS], zeros_b[:, 0:TW], nothing, start=False, stop=True).then_inc(m.kinds_ready, 1)

            @block.gpsimd
            def _(pool):
                with pool.Fori(0, TURNS // 2) as it:
                    for j in range(2):
                        pool.wait_ge(m.idx_ready[j], it + 1)
                        pool.sem_inc(m.turn, 1)
                        for k in range(GR):
                            pool.indirect_dma_start(
                                slot_d, bass.IndirectOffsetOnAxis(ap=idx[:, j, k:k + 1], axis=0), rec_c[:, j, k, :], None,
                                bounds_check=P * TILES - 1, oob_is_err=False).then_inc(m.written[j], 16)
                for j in range(2):
                    pool.wait_ge(m.written[j], (TURNS // 2) * 16 * GR)

        slot_rec = s("slot_rec", (P, TILES, REC))
        with phase(nc, "slots", "loaded") as (block, m):
            @block.sync
            def _(sp):
                sp.dma_start(slot_rec[:, :, :], slot_d.rearrange("(p t) f -> p t f", p=P)).then_inc(m.loaded, 16)
                sp.wait_ge(m.loaded, 16)

            @block.gpsimd
            def _(pool):
                pool.memset(slot_dst[:, TILES:TILES + BT], NOBODY)

            @block.scalar
            def _(act):
                act.activation(g["ident_big"][:, :], ident[:, :], ACT.Copy, scale=-BIG)
                act.wait_ge(m.loaded, 16)
                act.activation(slot_dst[:, 0:TILES], slot_rec[:, :, 0], ACT.Copy)
                act.activation(slot_weight[:, :], slot_rec[:, :, 2], ACT.Copy)

            @block.vector
            def _(v):
                v.wait_ge(m.loaded, 16)
                v.tensor_tensor(marks[:, :, :], bc(iota_w[:, :], 1, TILES), bc(slot_rec[:, :, 1], 2, W), ALU.not_equal)


def transposed(pe, src, banks, ident, signal):
    for u in range(CT):
        for k in range(2):
            last = pe.transpose(banks[:, u // 2, (u % 2) * D + k * P:(u % 2) * D + (k + 1) * P],
                                src[:, u, k * P:(k + 1) * P], ident[:, :])
        if u % 2 or u == CT - 1:
            last.then_inc(signal, 1)


def copy_transposed(act, c, banks, dst, ready, copied):
    for b in range(3):
        n = min(2, CT - 2 * b)
        act.wait_ge(ready, c * 3 + (b + 1))
        act.activation(dst[:, :, 2 * b * P:(2 * b + n) * P].rearrange("p k (u n) -> p u k n", u=n),
                       banks[:, b, 0:n * D].rearrange("p (u k n) -> p u k n", u=n, k=2), ACT.Copy).then_inc(copied, 1)


def normalize(v, c, src, dst, stats, mv, std, rstd, eps, m, meanwhile=None):
    for u in range(CT):
        last = v.bn_stats(stats[:, u, :], src(u))
    last.then_inc(m.ln_step, 1)
    v.wait_ge(m.ln_step, c * 4 + 1)
    v.sem_inc(m.turn, 1)
    for u in range(CT):
        last = v.bn_aggr(mv[:, u, :], stats[:, u, :])
    last.then_inc(m.ln_step, 1)
    if meanwhile:
        meanwhile()
    v.wait_ge(m.std_ready, c + 1)
    v.reciprocal(rstd[:, :], std[:, :]).then_inc(m.ln_step, 1)
    v.wait_ge(m.ln_step, c * 4 + 3)
    for u in range(CT):
        last = v.tensor_scalar(dst[:, u, :], src(u), mv[:, u, 0:1], rstd[:, u:u + 1], ALU.subtract, ALU.mult)
    last.then_inc(m.ln_step, 1)


def deviations(act, c, mv, std, eps, m):
    act.wait_ge(m.ln_step, c * 4 + 2)
    act.activation(std[:, :], mv[:, :, 1], ACT.Sqrt, bias=eps[:, 0:1]).then_inc(m.std_ready, 1)


def ln_buffers(s):
    return s("stats", (P, CT, 6)), s("mv", (P, CT, 2)), s("std", (P, CT)), s("rstd", (P, CT))


def hidden_in(nc, t, sb, pb, g):
    x, hid, ident, eps, x_d = g["x"], g["hid"], g["ident"], g["eps"], g["x_d"]
    with ExitStack() as st:
        def s(name, shape, dt=F32):
            return sb("hi_" + name, shape, dt, st)
        win, b_in = s("win", (P, 2, D)), s("b_in", (P, D))
        stats, mv, std, rstd = ln_buffers(s)
        xn, xnT = s("xn", (P, CT, D)), s("xnT", (P, 2, CN))
        banks, prod = pb(st, "hi_banks", (P, 3, 512)), pb(st, "hi_prod", (P, 3, 512))
        with phase(nc, "hid", "loaded", "turn", "ln_step", "std_ready", "banks_ready", "copied", "prod_ready", "stored+dve",
                   "x_added", "x_stored") as (block, m):
            @block.sync
            def _(sp):
                sp.dma_start(win[:, :, :], t["Win"]).then_inc(m.loaded, 16)
                sp.dma_start(b_in[:, :], t["b_in"]).then_inc(m.loaded, 16)
                with sp.Fori(0, CHUNKS) as c:
                    sp.wait_ge(m.x_added, c + 1)
                    sp.dma_start(x_d[:, bass.ds(c * CT, CT), :], x[:, bass.ds(c * CT, CT), :]).then_inc(m.x_stored, 16)
                sp.wait_ge(m.x_stored, CHUNKS * 16)

            @block.vector
            def _(v):
                v.wait_ge(m.loaded, 32)
                def norm(c, free=None):
                    normalize(v, c, lambda u: x[:, bass.ds(c * CT + u, 1), :].rearrange("p a d -> p (a d)"),
                              xn, stats, mv, std, rstd, eps, m, free)

                def hidden(c):
                    for b in range(3):
                        n = min(2, CT - 2 * b)
                        v.wait_ge(m.prod_ready, c * 3 + (b + 1))
                        v.tensor_tensor(hid[:, bass.ds(c * CT + 2 * b, n), :],
                                        prod[:, b, 0:n * D].rearrange("p (u d) -> p u d", u=n),
                                        bc(b_in[:, :], 1, n), ALU.add).then_inc(m.stored, 1)
                norm(0)
                with v.Fori(0, CHUNKS - 1) as c:
                    def free():
                        v.wait_ge(m.banks_ready, c * 3 + 3)
                        v.wait_ge(m.x_added, c + 1)
                    v.wait_ge(m.ln_step, c * 4 + 4)
                    v.sem_inc(m.turn, 1)
                    norm(c + 1, free)
                    hidden(c)
                hidden(CHUNKS - 1)

            @block.gpsimd
            def _(pool):
                with pool.Fori(0, CHUNKS) as c:
                    pool.wait_ge(m.ln_step, c * 4 + 4)
                    pool.sem_inc(m.turn, 1)
                    pool.tensor_tensor(x[:, bass.ds(c * CT, CT), :], x[:, bass.ds(c * CT, CT), :], xn[:, :, :],
                                       ALU.add).then_inc(m.x_added, 1)

            @block.scalar
            def _(act):
                deviations(act, 0, mv, std, eps, m)
                with act.Fori(0, CHUNKS - 1) as c:
                    copy_transposed(act, c, banks, xnT, m.banks_ready, m.copied)
                    deviations(act, c + 1, mv, std, eps, m)
                    act.wait_ge(m.prod_ready, c * 3 + 3)
                copy_transposed(act, CHUNKS - 1, banks, xnT, m.banks_ready, m.copied)

            @block.tensor
            def _(pe):
                pe.wait_ge(m.loaded, 32)
                with pe.Fori(0, CHUNKS) as c:
                    pe.wait_ge(m.ln_step, c * 4 + 4)
                    transposed(pe, xn, banks, ident, m.banks_ready)
                    pe.wait_ge(m.stored, c * 3 + FREE)
                    for u in range(CT):
                        pe.wait_ge(m.copied, c * 3 + (u // 2 + 1))
                        for k in range(2):
                            last = pe.matmul(prod[:, u // 2, (u % 2) * D:(u % 2 + 1) * D],
                                             xnT[:, k, u * P:(u + 1) * P], win[:, k, :], start=k == 0, stop=k == 1)
                        if u % 2 or u == CT - 1:
                            last.then_inc(m.prod_ready, 1)


def qkv(nc, t, sb, pb, g, layer):
    hid, ident, kv_d, q_d = g["hid"], g["ident"], g["kv_d"], g["q_d"]
    R = 4
    with ExitStack() as st:
        def s(name, shape, dt=F32):
            return sb("qkv_" + name, shape, dt, st)
        wq, wkv = s("wq", (P, 2, D)), s("wkv", (P, 2, 2 * D))
        bq, bqs, bkv = s("bq", (P, 2)), s("bqs", (P, 2)), s("bkv", (P, 2 * D))
        hb, hT = s("hb", (P, CT, D)), s("hT", (P, 2, CN))
        kv_row, qs = s("kv_row", (P, CT, 2 * D)), s("qs", (DH, CB, HW))
        banks = pb(st, "qkv_banks", (P, 3, 512))
        kv_ps, q_ps = pb(st, "kv_ps", (P, 2, 512)), pb(st, "q_ps", (P, 2, 512))
        with phase(nc, "qkv", "wkv_loaded", "wq_loaded", "bias_loaded", "hb_ready", "banks_ready", "copied+act", "kv_ready",
                   "kv_rows+dve", "q_ready", "q_even+act", "q_odd+dve", f"kv_stored+sp*{CT}", "q_stored+sp", "bias_ready",
                   "turn") as (block, m):
            @block.sync
            def _(sp):
                sp.dma_start(wkv[:, :, :], t["Wkv"][bass.ds(layer, 1)].rearrange("a p k n -> p (a k) n")).then_inc(m.wkv_loaded, 16)
                sp.dma_start(bkv[:, :], t["bkv"][bass.ds(layer, 1)].rearrange("a p n -> p (a n)")).then_inc(m.bias_loaded, 16)
                sp.dma_start(bq[:, :], t["bq"][bass.ds(layer, 1)].rearrange("a p n -> p (a n)")).then_inc(m.bias_loaded, 16)
                sp.dma_start(wq[:, :, :], t["Wq"][bass.ds(layer, 1)].rearrange("a p k n -> p (a k) n")).then_inc(m.wq_loaded, 16)
                kv_rows = kv_d.rearrange("(u p) d -> p u d", p=P)
                q_rows = q_d.rearrange("(b i p) c -> i p b c", i=2, p=DH)

                def keys_values(c):
                    for u in range(CT):
                        sp.wait_ge(m.kv_rows, c * CT + (u + 1 + FREE))
                        sp.dma_start(kv_rows[:, bass.ds(c * CT + u, 1), :], kv_row[:, u:u + 1, :]).then_inc(m.kv_stored[u], 16)

                def queries(c):
                    for f in range(2):
                        sp.wait_ge(m.q_even, c * 2 + (f + 1 + FREE))
                        sp.wait_ge(m.q_odd, c * 2 + (f + 1 + FREE))
                        for i in range(2):
                            sp.dma_start(q_rows[i, :, bass.ds(c * CB + f * (CB // 2), CB // 2), i * HW:(i + 1) * HW],
                                         qs[:, f * (CB // 2):(f + 1) * (CB // 2), :]).then_inc(m.q_stored, 16)
                with sp.Fori(0, CHUNKS) as c:
                    keys_values(c)
                    queries(c)
                for u in range(CT):
                    sp.wait_ge(m.kv_stored[u], CHUNKS * 16 + FREE)
                sp.wait_ge(m.q_stored, CHUNKS * 64 + FREE)

            @block.gpsimd
            def _(pool):
                with pool.Fori(0, CHUNKS) as c:
                    pool.wait_ge(m.copied, c * 3 + FREE)
                    pool.sem_inc(m.turn, 1)
                    pool.tensor_copy(hb[:, :, :], hid[:, bass.ds(c * CT, CT), :]).then_inc(m.hb_ready, 1)

            def halves(r):
                f, pair = r // 2, r % 2
                for e in range(2):
                    rows, h = slice(e * DH, (e + 1) * DH), 2 * pair + e
                    yield (qs[:, f * (CB // 2):(f + 1) * (CB // 2), h * W:(h + 1) * W],
                           q_ps[rows, r % 2, 0:HALF].rearrange("p (b w) -> p b w", w=W), bqs[rows, pair:pair + 1])

            @block.vector
            def _(v):
                v.wait_ge(m.bias_loaded, 32)
                v.wait_ge(m.bias_ready, 1)

                def keys_values(c):
                    for u in range(CT):
                        v.wait_ge(m.kv_stored[u], c * 16 + FREE)
                        v.wait_ge(m.kv_ready, c * CT + (u + 1))
                        v.tensor_tensor(kv_row[:, u, :], kv_ps[:, u % 2, :], bkv[:, :], ALU.add).then_inc(m.kv_rows, 1)

                def queries(c):
                    v.wait_ge(m.q_stored, c * 64 + FREE)
                    for r in (1, 3):
                        v.wait_ge(m.q_ready, c * R + (r + 1))
                        for dst, src, bias in halves(r):
                            last = v.tensor_scalar(dst, src, DH ** -0.5, bias, ALU.mult, ALU.add)
                        last.then_inc(m.q_odd, 1)
                with v.Fori(0, CHUNKS) as c:
                    keys_values(c)
                    queries(c)

            @block.scalar
            def _(act):
                act.wait_ge(m.bias_loaded, 32)
                act.activation(bqs[:, :], bq[:, :], ACT.Copy, scale=DH ** -0.5).then_inc(m.bias_ready, 1)
                act.wait_ge(m.bias_ready, 1)

                def queries(c, r):
                    act.wait_ge(m.q_ready, c * R + (r + 1))
                    for dst, src, bias in halves(r):
                        last = act.activation(dst, src, ACT.Identity, bias=bias, scale=DH ** -0.5)
                    last.then_inc(m.q_even, 1)

                def chunk(c):
                    act.wait_ge(m.q_stored, c * 64 + FREE)
                    queries(c, 0)
                    queries(c, 2)
                copy_transposed(act, 0, banks, hT, m.banks_ready, m.copied)
                with act.Fori(0, CHUNKS - 1) as c:
                    chunk(c)
                    act.wait_ge(m.q_ready, c * R + R)
                    copy_transposed(act, c + 1, banks, hT, m.banks_ready, m.copied)
                chunk(CHUNKS - 1)

            @block.tensor
            def _(pe):
                def transposes(c):
                    pe.wait_ge(m.hb_ready, c + 1)
                    transposed(pe, hb, banks, ident, m.banks_ready)

                def keys_values(c):
                    for u in range(CT):
                        pe.wait_ge(m.copied, c * 3 + (u // 2 + 1 + FREE))
                        pe.wait_ge(m.kv_rows, c * CT + (max(u - 1, 0) + FREE))
                        for k in range(2):
                            last = pe.matmul(kv_ps[:, u % 2, :], hT[:, k, u * P:(u + 1) * P], wkv[:, k, :],
                                             start=k == 0, stop=k == 1)
                        last.then_inc(m.kv_ready, 1)

                def queries(c):
                    for r in range(R):
                        pe.wait_ge(m.q_odd if r % 2 else m.q_even, c * (R // 2) + (r // 2 + FREE))
                        for k in range(2):
                            last = pe.matmul(q_ps[:, r % 2, 0:HALF], wq[:, k, r % 2 * P:(r % 2 + 1) * P],
                                             hT[:, k, r // 2 * HALF:(r // 2 + 1) * HALF], start=k == 0, stop=k == 1)
                        last.then_inc(m.q_ready, 1)

                transposes(0)
                pe.wait_ge(m.wkv_loaded, 16)
                pe.wait_ge(m.wq_loaded, 16)
                with pe.Fori(0, CHUNKS - 1) as c:
                    keys_values(c)
                    transposes(c + 1)
                    queries(c)
                keys_values(CHUNKS - 1)
                queries(CHUNKS - 1)


def attention_edges(nc, t, sb, pb, g):
    ident, ident_big, slot_dst, marks, kv = (g[k] for k in ("ident", "ident_big", "slot_dst", "marks", "kv"))
    keep, tile_blk, kv_d, q_d, totals = (g[k] for k in ("keep", "tile_blk", "kv_d", "q_d", "sums"))
    GH = H * H
    with ExitStack() as st:
        def s(name, shape, dt=F32):
            return sb("ae_" + name, shape, dt, st)
        idx = s("idx", (P, SETS, BT), I32)
        q = s("q", (P, FEW, BT, P))
        sel = s("sel", (P, FEW, BT, W), BF16)
        kT = s("kT", (P, BT, 2, P))
        own = s("own", (P, 2, BT, H, H))
        top = s("top", (P, 2, BT, H))
        low = s("low", (P, 2, BT, H, H))
        ex = s("ex", (P, 2, BT, H, H))
        z = s("z", (P, 2, BT, H))
        rz = s("rz", (P, 2, BT, H))
        att = s("att", (P, 2, BT, H, H))
        wgt = s("wgt", (P, 2, BT, GH, W))
        acc = s("acc", (P, FEW, BT, HW))
        kT_ps = pb(st, "kT_ps", (P, BT, 2, P))
        sc_ps = pb(st, "sc_ps", (P, 2, BT, GH * W))
        out_ps = pb(st, "out_ps", (P, 2, 512))
        with phase(nc, "ae", "idx_ready", "turn", f"kv_loaded*{SETS}", f"q_loaded*{FEW}", "const_ready", "sel_ready", "kT_ready", "kT_copied",
                   "scores_ready", "own_ready", "top_ready", "low_ready", "exp_ready", "z_ready", "rz_ready",
                   "att_ready", "weights_ready", "sums_ready", "acc_ready", "kept") as (block, m):

            @block.gpsimd
            def _(pool):
                def step(b, n, k):
                    pool.wait_ge(m.idx_ready, b - SETS + 2 if after(b, SETS) else 1)
                    pool.sem_inc(m.turn, 1)
                    for u in range(BT):
                        pool.indirect_dma_start(
                            kv[:, k, u, :], None, kv_d, bass.IndirectOffsetOnAxis(ap=idx[:, k, u:u + 1], axis=0),
                            bounds_check=NP_ - 1, oob_is_err=False).then_inc(m.kv_loaded[k], 16)
                batches(pool, 0, BATCHES, SETS, step)

            @block.sync
            def _(sp):
                def step(b, n, k):
                    blocks = tile_blocks(nc, mybir.EngineType.SP, tile_blk, b)
                    if after(b, FEW):
                        sp.wait_ge(m.scores_ready, (b - FEW) * 2 + 2)
                    for u in range(BT):
                        sp.dma_start(q[:, k % FEW, u, :], q_d[bass.ds(blocks[u] * P, P), :]).then_inc(m.q_loaded[k % FEW], 16)
                batches(sp, 0, BATCHES, SETS, step)

            @block.scalar
            def _(act):
                def copies(b):
                    for f in range(2):
                        act.wait_ge(m.kT_ready, b * 2 + (f + 1))
                        act.activation(kT[:, 2 * f:2 * f + 2, :, :], kT_ps[:, 2 * f:2 * f + 2, :, :],
                                       ACT.Copy).then_inc(m.kT_copied, 1)

                def select(b, k):
                    if after(b, FEW):
                        act.wait_ge(m.weights_ready, (b - FEW) * 2 + 2)
                        act.sem_inc(m.turn, 1)
                    act.activation(sel[:, k % FEW, :, :], marks[:, bass.ds(b * BT, BT), 0:W], ACT.Copy, bias=1.0, scale=-1.0).then_inc(m.sel_ready, 1)

                def keep_sums(b, k):
                    blocks = tile_blocks(nc, mybir.EngineType.Activation, tile_blk, b)
                    for u in range(BT):
                        if u == 0:
                            act.wait_ge(m.acc_ready, b * BT + BT)
                        act.wait_ge(m.kept, b * BT + u)
                        act.sem_inc(m.turn, 1)
                        act.activation(totals[:, bass.ds(blocks[u], 1), :], acc[:, k % FEW, u:u + 1, :], ACT.Copy).then_inc(m.kept, 1)

                def destinations(b, k):
                    if after(b, 2) and (not isinstance(b, int) or b + SETS - 2 < BATCHES):
                        act.wait_ge(m.sums_ready, b - 1)
                        act.sem_inc(m.turn, 1)
                        act.activation(idx[:, (k - 2) % SETS, :], slot_dst[:, bass.ds((b + SETS - 2) * BT, BT)], ACT.Copy).then_inc(m.idx_ready, 1)

                LATE = 4

                def step(b, n, k):
                    if not isinstance(b, int) or b + 1 < BATCHES:
                        copies(b + 1)
                    act.wait_ge(m.low_ready, b + 1)
                    act.activation(ex[:, k % 2, :, :, :], low[:, k % 2, :, :, :], ACT.Exp).then_inc(m.exp_ready, 1)
                    if not isinstance(b, int) or b + 1 < BATCHES:
                        select(b + 1, (k + 1) % SETS)
                    destinations(b, k)
                    if after(b, LATE):
                        keep_sums(b - LATE, (k - LATE) % SETS)
                act.activation(idx[:, :, :], slot_dst[:, 0:SETS * BT].rearrange("p (s u) -> p s u", u=BT), ACT.Copy).then_inc(m.idx_ready, 1)
                act.wait_ge(m.const_ready, 2)
                copies(0)
                select(0, 0)
                batches(act, 0, BATCHES - 1, SETS, step)
                step(BATCHES - 1, None, (BATCHES - 1) % SETS)
                for b in range(BATCHES - LATE, BATCHES):
                    keep_sums(b, b % SETS)

            @block.vector
            def _(v):
                def accumulate(b, k, u):
                    prev = acc[:, k % FEW, u - 1, :] if u else acc[:, (k - 1) % FEW, BT - 1, :]
                    v.scalar_tensor_tensor(acc[:, k % FEW, u, :], prev, keep[:, bass.ds(b * BT + u, 1)],
                                           out_ps[:, k % 2, u * HW:(u + 1) * HW], ALU.mult, ALU.add).then_inc(m.acc_ready, 1)

                def acc_waits(b, k):
                    v.wait_ge(m.sums_ready, b + 1)
                    if after(b, FEW):
                        v.wait_ge(m.kept, (b - FEW) * BT + BT)

                def step(b, n, k):
                    new, old, done = b < BATCHES if isinstance(b, int) else True, after(b, 1), after(b, 3)
                    j, jo, ko, bd, kd = k % 2, (k - 1) % 2, (k - 1) % SETS, b - 3, (k - 3) % SETS

                    def running(u):
                        if done:
                            if u == 0:
                                acc_waits(bd, kd)
                            v.wait_ge(m.acc_ready, bd * BT + u)
                            accumulate(bd, kd, u)

                    def best(f):
                        if new:
                            v.wait_ge(m.scores_ready, b * 2 + (f + 1))
                            v.tensor_reduce(own[:, j, 2 * f:2 * f + 2, :, :].rearrange("p u g h -> p (u g h)"),
                                            sc_ps[:, j, 2 * f:2 * f + 2, :].rearrange("p u (x w) -> p (u x) w", w=W),
                                            axis=AX.X, op=ALU.max).then_inc(m.own_ready, 1)
                    best(0)
                    if old:
                        v.wait_ge(m.exp_ready, b)
                        v.tensor_reduce(z[:, jo, :, :], ex[:, jo, :, :, :].rearrange("p u g h -> p u h g"),
                                        axis=AX.X, op=ALU.add).then_inc(m.z_ready, 1)
                    running(0)
                    best(1)
                    if old:
                        v.wait_ge(m.z_ready, b)
                        v.reciprocal(rz[:, jo, :, :], z[:, jo, :, :]).then_inc(m.rz_ready, 1)
                    running(1)
                    if new:
                        v.wait_ge(m.own_ready, b * 2 + 2)
                        v.tensor_reduce(top[:, j, :, :], own[:, j, :, :, :].rearrange("p u g h -> p u h g"),
                                        axis=AX.X, op=ALU.max).then_inc(m.top_ready, 1)
                    if old:
                        v.wait_ge(m.rz_ready, b)
                        v.tensor_tensor(att[:, jo, :, :, :], ex[:, jo, :, :, :], bc(rz[:, jo, :, :], 2, H),
                                        ALU.mult).then_inc(m.att_ready, 1)
                    running(2)
                    if new:
                        v.wait_ge(m.top_ready, b + 1)
                        v.tensor_tensor(low[:, j, :, :, :], own[:, j, :, :, :], bc(top[:, j, :, :], 2, H),
                                        ALU.subtract).then_inc(m.low_ready, 1)
                    running(3)
                    if old:
                        v.wait_ge(m.att_ready, b)
                        v.wait_ge(m.sel_ready, b)
                        for f in range(2):
                            v.tensor_tensor(wgt[:, jo, 2 * f:2 * f + 2, :, :],
                                            bc(att[:, jo, 2 * f:2 * f + 2, :, :].rearrange("p u g h -> p u (g h)"), 3, W),
                                            bc(sel[:, ko % FEW, 2 * f:2 * f + 2, :], 2, GH), ALU.mult).then_inc(m.weights_ready, 1)

                v.memset(totals[:, FULL_BLOCKS:BLOCKS, :], 0.0).then_inc(m.const_ready, 1)
                v.memset(acc[:, FEW - 1, BT - 1, :], 0.0).then_inc(m.const_ready, 1)
                batches(v, 0, BATCHES, SETS, step)
                step(BATCHES, None, BATCHES % SETS)
                for b in (BATCHES - 2, BATCHES - 1):
                    acc_waits(b, b % SETS)
                    for u in range(BT):
                        v.wait_ge(m.acc_ready, b * BT + u)
                        accumulate(b, b % SETS, u)

            @block.tensor
            def _(pe):
                def transposes(b, n, k):
                    pe.wait_ge(m.kv_loaded[k], n * (16 * BT) + 16 * BT)
                    for u in range(BT):
                        for i in range(2):
                            last = pe.transpose(kT_ps[:, u, i, :], kv[:, k, u, i * P:(i + 1) * P], ident[:, :])
                        if u % 2:
                            last.then_inc(m.kT_ready, 1)

                def scores(b, n, k):
                    if after(b, 2):
                        pe.wait_ge(m.own_ready, (b - 2) * 2 + 2)
                    pe.wait_ge(m.q_loaded[k % FEW], n * (SETS // FEW * 16 * BT) + (k // FEW + 1) * 16 * BT)
                    for u in range(BT):
                        pe.matmul(sc_ps[:, k % 2, u, :], ident_big[:, :], bc(marks[:, bass.ds(b * BT + u, 1), 0:W].rearrange("p a w -> p (a w)"), 1, GH), start=True, stop=False)
                        if u % 2 == 0:
                            pe.wait_ge(m.kT_copied, b * 2 + (u // 2 + 1))
                        for i in range(2):
                            last = pe.matmul(sc_ps[:, k % 2, u, i * P:(i + 1) * P], kT[:, u, i, :], q[:, k % FEW, u, :],
                                             start=False, stop=i == 1)
                        if u % 2:
                            last.then_inc(m.scores_ready, 1)

                def sums(b, n, k):
                    for u in range(BT):
                        if u % 2 == 0:
                            pe.wait_ge(m.weights_ready, b * 2 + (u // 2 + 1))
                        o = out_ps[:, k % 2, u * HW:(u + 1) * HW]
                        for i in range(H):
                            last = pe.matmul(o[i % 2 * DH:(i % 2 + 1) * DH, :], kv[:, k, u, D + i * DH:D + (i + 1) * DH],
                                             wgt[:, k % 2, u, i * H:(i + 1) * H, :].rearrange("p h w -> p (h w)"),
                                             start=i < 2, stop=i >= 2)
                    last.then_inc(m.sums_ready, 1)

                def step(b, n, k):
                    scores(b, n, k)
                    if not isinstance(b, int) or b + 1 < BATCHES:
                        transposes(b + 1, n + 1 if k == SETS - 1 else n, (k + 1) % SETS)
                    if after(b, 2):
                        sums(b - 2, None, (k - 2) % SETS)

                pe.wait_ge(m.const_ready, 2)
                transposes(0, 0, 0)
                batches(pe, 0, BATCHES - 1, 3, step)
                step(BATCHES - 1, (BATCHES - 1) // SETS, (BATCHES - 1) % SETS)
                for b in (BATCHES - 2, BATCHES - 1):
                    sums(b, None, b % SETS)


def node_update(nc, t, sb, pb, g, layer):
    hid, eps, totals, type_counts = g["hid"], g["eps"], g["sums"], g["type_counts"]
    with ExitStack() as st:
        def s(name, shape, dt=F32):
            return sb("nu_" + name, shape, dt, st)
        wo, ee, ew, bo = s("wo", (P, H, D)), s("ee", (DH, H, TW)), s("ew", (TW, D)), s("bo", (TW, D))
        gam, bet = s("gam", (P, D)), s("bet", (P, D))
        sums, types = s("sums", (P, H, CN)), s("types", (TW, CN))
        stats, mv, std, rstd = ln_buffers(s)
        y, yn = s("y", (P, CT, D)), s("yn", (P, CT, D))
        ew_ps, prod = pb(st, "ew_ps", (P, 512)), pb(st, "nu_prod", (P, 3, 512))
        TB = P // W
        with phase(nc, "nu", "wo_loaded", "bo_loaded", "ln_loaded", "ew_ready", "ew_done", "sums_laid", "used", "added+dve", "turn",
                   "ln_step", "std_ready", "scaled", "shifted", "done+act") as (block, m):
            @block.sync
            def _(sp):
                one = bass.ds(layer, 1)
                sp.dma_start(ee[:, :, :], t["Ee"][one].rearrange("a p h n -> p (a h) n")).then_inc(m.wo_loaded, 16)
                sp.dma_start(wo[:, :, :], t["Wo"][one].rearrange("a p h n -> p (a h) n")).then_inc(m.wo_loaded, 16)
                sp.dma_start(bo[:, :], t["bo"][one].rearrange("a p n -> p (a n)")).then_inc(m.bo_loaded, 16)
                sp.dma_start(gam[:, :], t["ln_g"][one].rearrange("a p n -> p (a n)")).then_inc(m.ln_loaded, 16)
                sp.dma_start(bet[:, :], t["ln_b"][one].rearrange("a p n -> p (a n)")).then_inc(m.ln_loaded, 16)

            @block.tensor
            def _(pe):
                pe.wait_ge(m.wo_loaded, 32)
                for h in range(H):
                    last = pe.matmul(ew_ps[0:TW, 0:D], ee[:, h, :], wo[0:DH, h, :], start=h == 0, stop=h == H - 1)
                last.then_inc(m.ew_ready, 1)
                pe.wait_ge(m.ew_done, 1)
                with pe.Fori(0, CHUNKS) as c:
                    pe.wait_ge(m.added, c * 3 + FREE)
                    for u in range(CT):
                        pe.wait_ge(m.sums_laid, c * (2 * CT) + (2 * u + 2))
                        o = prod[:, u // 2, (u % 2) * D:(u % 2 + 1) * D]
                        for h in range(H):
                            pe.matmul(o, sums[:, h, u * P:(u + 1) * P], wo[:, h, :], start=h == 0, stop=False)
                        pe.matmul(o, types[:, u * P:(u + 1) * P], ew[:, :], start=False, stop=True).then_inc(m.used, 1)

            @block.vector
            def _(v):
                v.wait_ge(m.bo_loaded, 16)
                v.wait_ge(m.ew_ready, 1)
                v.tensor_tensor(ew[:, :], ew_ps[0:TW, 0:D], bo[:, :], ALU.add).then_inc(m.ew_done, 1)
                v.wait_ge(m.ln_loaded, 32)
                with v.Fori(0, CHUNKS) as c:
                    for b in range(3):
                        n = min(2, CT - 2 * b)
                        v.wait_ge(m.used, c * CT + (2 * b + n))
                        v.tensor_tensor(y[:, 2 * b:2 * b + n, :], prod[:, b, 0:n * D].rearrange("p (u d) -> p u d", u=n),
                                        hid[:, bass.ds(c * CT + 2 * b, n), :], ALU.add).then_inc(m.added, 1)
                    v.wait_ge(m.added, c * 3 + (3 + FREE))
                    v.wait_ge(m.done, c + FREE)
                    v.sem_inc(m.turn, 1)
                    normalize(v, c, lambda u: y[:, u, :], yn, stats, mv, std, rstd, eps, m)
                    v.wait_ge(m.ln_step, c * 4 + 4)
                    v.tensor_tensor(y[:, :, :], yn[:, :, :], bc(gam[:, :], 1, CT), ALU.mult).then_inc(m.scaled, 1)
                    v.wait_ge(m.scaled, c + 1)
                    v.tensor_tensor(yn[:, :, :], y[:, :, :], bc(bet[:, :], 1, CT), ALU.add).then_inc(m.shifted, 1)
                    v.wait_ge(m.shifted, c + 1)

            @block.scalar
            def _(act):
                def lay(c, u):
                    blocks = bass.ds((c * CT + u) * TB, TB)
                    cols = slice(u * P, (u + 1) * P)
                    act.activation(sums[:, :, cols].rearrange("r h (b w) -> r b h w", w=W),
                                   totals[:, blocks, :].rearrange("r b (h w) -> r b h w", w=W), ACT.Copy).then_inc(m.sums_laid, 1)
                    act.activation(types[:, cols].rearrange("r (b w) -> r b w", w=W), type_counts[:, blocks, :],
                                   ACT.Copy).then_inc(m.sums_laid, 1)

                def finish(c):
                    deviations(act, c, mv, std, eps, m)
                    act.wait_ge(m.shifted, c + 1)
                    act.sem_inc(m.turn, 1)
                    act.activation(hid[:, bass.ds(c * CT, CT), :], yn[:, :, :], ACT.Relu).then_inc(m.done, 1)
                for u in range(CT):
                    lay(0, u)
                with act.Fori(0, CHUNKS - 1) as c:
                    for u in range(CT):
                        act.wait_ge(m.used, c * CT + (u + 1))
                        act.sem_inc(m.turn, 1)
                        lay(c + 1, u)
                    finish(c)
                finish(CHUNKS - 1)


def adjustment(nc, t, sb, pb, g):
    x, hid, ident, x_d = g["x"], g["hid"], g["ident"], g["x_d"]
    with ExitStack() as st:
        def s(name, shape, dt=F32):
            return sb("ad_" + name, shape, dt, st)
        a1w, a2w, a1, a2 = s("w1", (P, 2, D)), s("w2", (P, 2, D)), s("b1", (P, 2)), s("b2", (P, D))
        hb, hT, u1T, y = s("hb", (P, CT, D)), s("hT", (P, 2, CN)), s("u1T", (P, 2, CN)), s("y", (P, CT, D))
        banks, u_ps, prod = pb(st, "ad_banks", (P, 3, 512)), pb(st, "ad_u", (P, 2, 512)), pb(st, "ad_prod", (P, 3, 512))
        with phase(nc, "ad", "loaded", "x_loaded", "hb_ready", "turn", "banks_ready", "copied+act", "u_ready", "relu_ready+act", "prod_ready+pe",
                   "biased+dve", "added+dve") as (block, m):
            @block.sync
            def _(sp):
                for a, b in ((a1w[:, :, :], "A1"), (a2w[:, :, :], "A2"), (a1[:, :], "a1"), (a2[:, :], "a2")):
                    sp.dma_start(a, t[b]).then_inc(m.loaded, 16)
                sp.dma_start(x[:, :, :], x_d).then_inc(m.x_loaded, 16)

            @block.gpsimd
            def _(pool):
                with pool.Fori(0, CHUNKS) as c:
                    pool.wait_ge(m.copied, c * 3 + FREE)
                    pool.sem_inc(m.turn, 1)
                    pool.tensor_copy(hb[:, :, :], hid[:, bass.ds(c * CT, CT), :]).then_inc(m.hb_ready, 1)

            @block.scalar
            def _(act):
                def hidden(c):
                    act.wait_ge(m.prod_ready, c * 3 + FREE)
                    for r in range(4):
                        act.wait_ge(m.u_ready, c * 4 + (r + 1))
                        act.activation(u1T[:, r // 2, (r % 2) * HALF:(r % 2 + 1) * HALF], u_ps[:, r % 2, 0:HALF], ACT.Relu,
                                       bias=a1[:, r // 2:r // 2 + 1]).then_inc(m.relu_ready, 1)
                act.wait_ge(m.loaded, 64)
                copy_transposed(act, 0, banks, hT, m.banks_ready, m.copied)
                with act.Fori(0, CHUNKS - 1) as c:
                    hidden(c)
                    copy_transposed(act, c + 1, banks, hT, m.banks_ready, m.copied)
                hidden(CHUNKS - 1)

            @block.vector
            def _(v):
                v.wait_ge(m.loaded, 64)
                v.wait_ge(m.x_loaded, 16)
                with v.Fori(0, CHUNKS) as c:
                    v.wait_ge(m.added, c + FREE)
                    for b in range(3):
                        n = min(2, CT - 2 * b)
                        v.wait_ge(m.prod_ready, c * 3 + (b + 1 + FREE))
                        v.tensor_tensor(y[:, 2 * b:2 * b + n, :], prod[:, b, 0:n * D].rearrange("p (u d) -> p u d", u=n),
                                        bc(a2[:, :], 1, n), ALU.add).then_inc(m.biased, 1)
                    v.wait_ge(m.biased, c * 3 + (3 + FREE))
                    v.tensor_tensor(x[:, bass.ds(c * CT, CT), :], x[:, bass.ds(c * CT, CT), :], y[:, :, :],
                                    ALU.add).then_inc(m.added, 1)
                v.wait_ge(m.added, CHUNKS + FREE)

            @block.tensor
            def _(pe):
                def transposes(c):
                    pe.wait_ge(m.hb_ready, c + 1)
                    transposed(pe, hb, banks, ident, m.banks_ready)

                def chunk(c, more):
                    pe.wait_ge(m.copied, c * 3 + (3 + FREE))
                    for r in range(4):
                        pe.wait_ge(m.relu_ready, c * 4 + (max(r - 1, 0) + FREE))
                        for k in range(2):
                            last = pe.matmul(u_ps[:, r % 2, 0:HALF], a1w[:, k, (r // 2) * P:(r // 2 + 1) * P],
                                             hT[:, k, (r % 2) * HALF:(r % 2 + 1) * HALF], start=k == 0, stop=k == 1)
                        last.then_inc(m.u_ready, 1)
                    if more:
                        transposes(c + 1)
                    pe.wait_ge(m.relu_ready, c * 4 + (4 + FREE))
                    pe.wait_ge(m.biased, c * 3 + FREE)
                    for u in range(CT):
                        for k in range(2):
                            last = pe.matmul(prod[:, u // 2, (u % 2) * D:(u % 2 + 1) * D], u1T[:, k, u * P:(u + 1) * P],
                                             a2w[:, k, :], start=k == 0, stop=k == 1)
                        if u % 2 or u == CT - 1:
                            last.then_inc(m.prod_ready, 1)
                transposes(0)
                pe.wait_ge(m.loaded, 64)
                with pe.Fori(0, CHUNKS - 1) as c:
                    chunk(c, True)
                chunk(CHUNKS - 1, False)


def expert_logits(nc, t, sb, pb, g):
    x, hid, ident, eps, expert = (g[k] for k in ("x", "hid", "ident", "eps", "expert"))
    with ExitStack() as st:
        def s(name, shape, dt=F32):
            return sb("el_" + name, shape, dt, st)
        rw, rb = s("rw", (P, 2, EX0)), s("rb", (P, EX0))
        stats, mv, std, rstd = ln_buffers(s)
        xnT = s("xnT", (P, 2, CN))
        banks, lg_ps = pb(st, "el_banks", (P, 3, 512)), pb(st, "el_lg", (P, 512))
        with phase(nc, "el", "loaded", "turn", "ln_step", "std_ready", "banks_ready", "copied", "logits_ready",
                   "biased") as (block, m):
            @block.sync
            def _(sp):
                sp.dma_start(rw[:, :, :], t["router_w"]).then_inc(m.loaded, 16)
                sp.dma_start(rb[:, :], t["router_b"]).then_inc(m.loaded, 16)

            @block.vector
            def _(v):
                def norm(c):
                    if c:
                        v.wait_ge(m.ln_step, c * 4)
                    normalize(v, c, lambda u: x[:, c * CT + u, :], hid[:, c * CT:(c + 1) * CT, :], stats, mv, std, rstd, eps, m)

                def logits(c):
                    v.wait_ge(m.logits_ready, c + 1)
                    v.tensor_tensor(expert[:, c * CT:(c + 1) * CT, :], lg_ps[:, 0:CT * EX0].rearrange("p (u e) -> p u e", u=CT),
                                    bc(rb[:, :], 1, CT), ALU.add).then_inc(m.biased, 1)
                norm(0)
                v.wait_ge(m.loaded, 32)
                for c in range(CHUNKS):
                    if c + 1 < CHUNKS:
                        norm(c + 1)
                    logits(c)

            @block.scalar
            def _(act):
                deviations(act, 0, mv, std, eps, m)
                for c in range(CHUNKS):
                    if c:
                        act.wait_ge(m.logits_ready, c)
                    copy_transposed(act, c, banks, xnT, m.banks_ready, m.copied)
                    if c + 1 < CHUNKS:
                        deviations(act, c + 1, mv, std, eps, m)

            @block.tensor
            def _(pe):
                pe.wait_ge(m.loaded, 32)
                for c in range(CHUNKS):
                    pe.wait_ge(m.ln_step, c * 4 + 4)
                    if c:
                        pe.wait_ge(m.copied, c * 3)
                    transposed(pe, hid[:, c * CT:(c + 1) * CT, :], banks, ident, m.banks_ready)
                    if c:
                        pe.wait_ge(m.biased, c)
                    for u in range(CT):
                        pe.wait_ge(m.copied, c * 3 + (u // 2 + 1))
                        for k in range(2):
                            last = pe.matmul(lg_ps[:, u * EX0:(u + 1) * EX0], xnT[:, k, u * P:(u + 1) * P], rw[:, k, :],
                                             start=k == 0, stop=k == 1)
                    last.then_inc(m.logits_ready, 1)


def expert_sort(nc, t, sb, pb, g):
    hid, expert, slot, before_b, ones_b, xs_d, xt_d = (g[k] for k in ("hid", "expert", "slot", "before_b", "ones_b", "xs_d", "xt_d"))
    U = NODE_TILES
    SPLIT = (slice(0, 13), slice(13, U))
    with ExitStack() as st:
        def s(name, shape, dt=F32):
            return sb("es_" + name, shape, dt, st)
        iota, tcol = s("iota", (P, EX0)), s("tcol", (P, TG))
        best, first = s("best", (P, U)), s("first", (P, U))
        eq, hot = s("eq", (P, U, EX0)), s("hot", (P, U, EX0), BF16)
        given = s("given", (P, U + 1, EX0))
        tiles, t_end, s_base = s("tiles", (P, EX0)), s("t_end", (P, EX0)), s("s_base", (P, EX0))
        tiles_i, zeros = s("tiles_i", (P, EX0), I32), s("zeros", (P, EX0))
        ended, own, own_i = s("ended", (P, EX0)), s("own", (P, 1)), s("own_i", (P, 1), I32)
        ahead, total = pb(st, "es_ahead", (P, 2, 512)), pb(st, "es_total", (P, 2, 512))
        with phase(nc, "es", "loaded", "hot_ready", "counted", "step", "slot_ready", "table_ready", "table_stored", "table_loaded",
                   "scattered") as (block, m):
            @block.sync
            def _(sp):
                sp.dma_start(iota[:, :], t["c_iota_e"]).then_inc(m.loaded, 16)
                sp.dma_start(tcol[:, :], t["c_tcol"]).then_inc(m.loaded, 16)
                sp.wait_ge(m.table_ready, 1)
                sp.dma_start(xt_d.unsqueeze(1), own_i[:, :]).then_inc(m.table_stored, 16)
                sp.wait_ge(m.table_stored, 16)
                sp.dma_start(g["tile_expert"][0:1, :], xt_d.unsqueeze(0)).then_inc(m.table_loaded, 16)
                sp.wait_ge(m.table_loaded, 16)

            @block.tensor
            def _(pe):
                pe.wait_ge(m.hot_ready, 1)
                for b, us in enumerate(SPLIT):
                    rows = hot[:, us, :].rearrange("p u e -> p (u e)")
                    n = (us.stop - us.start) * EX0
                    pe.matmul(ahead[:, b, 0:n], before_b[:, :], rows, start=True, stop=True).then_inc(m.counted, 1)
                    pe.matmul(total[:, b, 0:n], ones_b[:, :], rows, start=True, stop=True).then_inc(m.counted, 1)

            @block.vector
            def _(v):
                done = [0]

                def then(ins):
                    done[0] += 1
                    ins.then_inc(m.step, 1)
                    v.wait_ge(m.step, done[0])
                v.wait_ge(m.loaded, 32)
                then(v.tensor_single_scalar(iota[:, :], iota[:, :], -float(EX0), ALU.add))
                then(v.tensor_reduce(best[:, :], expert[:, :, :], axis=AX.X, op=ALU.max))
                then(v.tensor_tensor(eq[:, :, :], expert[:, :, :], bc(best[:, :], 2, EX0), ALU.is_equal))
                then(v.tensor_tensor(expert[:, :, :], eq[:, :, :], bc(iota[:, :], 1, U), ALU.mult))
                then(v.tensor_reduce(first[:, :], expert[:, :, :], axis=AX.X, op=ALU.min))
                v.tensor_tensor(hot[:, :, :], bc(first[:, :], 2, EX0), bc(iota[:, :], 1, U), ALU.is_equal).then_inc(m.hot_ready, 1)
                then(v.memset(given[:, 0, :], 0.0))
                then(v.memset(zeros[:, :], 0.0))
                v.wait_ge(m.counted, 4)
                for u in range(U):
                    b = u // 13
                    cols = slice((u - b * 13) * EX0, (u - b * 13 + 1) * EX0)
                    then(v.tensor_tensor(given[:, u + 1, :], given[:, u, :], total[:, b, cols], ALU.add))
                then(v.tensor_single_scalar(tiles[:, :], given[:, U, :], float(P - 1), ALU.add))
                then(v.tensor_copy(tiles_i[:, :], tiles[:, :]))
                then(v.tensor_single_scalar(tiles_i[:, :], tiles_i[:, :], 7, ALU.logical_shift_right))
                then(v.tensor_copy(tiles[:, :], tiles_i[:, :]))
                then(v.tensor_tensor_scan(t_end[:, :], tiles[:, :], zeros[:, :], 0.0, ALU.add, ALU.add))
                then(v.tensor_tensor(ended[:, :], t_end[:, :], bc(tcol[:, 0], 1, EX0), ALU.is_le))
                then(v.tensor_reduce(own[:, :], ended[:, :], axis=AX.X, op=ALU.add))
                v.tensor_single_scalar(own_i[:, :], own[:, :], float(EX0 - 1), ALU.min).then_inc(m.table_ready, 1)
                then(v.tensor_tensor(s_base[:, :], t_end[:, :], tiles[:, :], ALU.subtract))
                then(v.tensor_single_scalar(s_base[:, :], s_base[:, :], float(P), ALU.mult))
                then(v.tensor_tensor(eq[:, :, :], given[:, 0:U, :], bc(s_base[:, :], 1, U), ALU.add))
                for b, us in enumerate(SPLIT):
                    n = us.stop - us.start
                    then(v.tensor_tensor(expert[:, us, :], eq[:, us, :], ahead[:, b, 0:n * EX0].rearrange("p (u e) -> p u e", e=EX0), ALU.add))
                then(v.tensor_tensor(eq[:, :, :], expert[:, :, :], hot[:, :, :], ALU.mult))
                then(v.tensor_reduce(first[:, :], eq[:, :, :], axis=AX.X, op=ALU.add))
                v.tensor_copy(slot[:, :], first[:, :]).then_inc(m.slot_ready, 1)

            @block.gpsimd
            def _(pool):
                pool.wait_ge(m.slot_ready, 1)
                for u in range(U):
                    pool.indirect_dma_start(xs_d, bass.IndirectOffsetOnAxis(ap=slot[:, u:u + 1], axis=0), hid[:, u, :], None,
                                            bounds_check=XTILES * P - 1, oob_is_err=False).then_inc(m.scattered, 16)
                pool.wait_ge(m.scattered, 16 * U)


def expert_tiles(nc, t, sb, pb, g):
    ident, tile_expert, xs_d, xo_d = (g[k] for k in ("ident", "tile_expert", "xs_d", "xo_d"))
    with ExitStack() as st:
        def s(name, shape, dt=F32):
            return sb("et_" + name, shape, dt, st)
        w = s("w", (P, XSETS, XW))
        xs, xT = s("xs", (P, XSETS, D)), s("xT", (P, 2, 2, P))
        hs = s("hs", (H0 + 1, 2, P))
        o = s("o", (P, XSETS, D))
        xT_ps, h_ps, o_ps = pb(st, "et_xTp", (P, 2, 512)), pb(st, "et_hp", (P, 2, 512)), pb(st, "et_op", (P, 2, 512))
        with phase(nc, "et", f"w_loaded*{XSETS}", f"x_loaded*{XSETS}", "ones_ready", "xT_ready", "xT_copied", "h_ready", "relu_ready",
                   "o_ready", "o_done", "turn", f"stored*{XSETS}") as (block, m):
            @block.sync
            def _(sp):
                experts = []

                def step(b, n, k):
                    if k == 0:
                        experts[:] = nc.values_load_multi_w_load_instructions(
                            tile_expert[0:1, bass.ds(b, XSETS)], engines=(mybir.EngineType.SP,), min_val=0, max_val=EX0 - 1,
                            skip_runtime_bounds_check_because="the table is clamped to the experts where it is made")[1]
                    if after(b, XSETS):
                        sp.wait_ge(m.o_ready, b - XSETS + 1)
                    sp.dma_start(xs[:, k, :], xs_d[bass.ds(b * P, P), :]).then_inc(m.x_loaded[k], 16)
                    sp.dma_start(w[:, k, :], t["EW"][bass.ds(experts[k], 1)].rearrange("a p c -> p (a c)")).then_inc(m.w_loaded[k], 16)
                batches(sp, 0, XTILES, XSETS, step, XSETS)

            @block.scalar
            def _(act):
                def copy(b, k):
                    act.wait_ge(m.xT_ready, b + 1)
                    if after(b, 2):
                        act.wait_ge(m.h_ready, b - 1)
                    act.activation(xT[:, k % 2, :, :], xT_ps[:, k % 2, 0:D].rearrange("p (k n) -> p k n", n=P), ACT.Copy).then_inc(m.xT_copied, 1)

                def step(b, n, k):
                    if not isinstance(b, int) or b + 1 < XTILES:
                        copy(b + 1, k + 1)
                    act.wait_ge(m.h_ready, b + 1)
                    if after(b, 2):
                        act.wait_ge(m.o_ready, b - 1)
                    act.activation(hs[0:H0, k % 2, :], h_ps[0:H0, k % 2, 0:P], ACT.Relu, bias=w[0:H0, k, XW - 1:XW]).then_inc(m.relu_ready, 1)
                copy(0, 0)
                batches(act, 0, XTILES - 1, XSETS, step, XSETS)
                step(XTILES - 1, None, (XTILES - 1) % XSETS)

            @block.gpsimd
            def _(pool):
                def step(b, n, k):
                    pool.wait_ge(m.o_done, b + 1)
                    pool.sem_inc(m.turn, 1)
                    pool.dma_start(xo_d[bass.ds(b * P, P), :], o[:, k, :]).then_inc(m.stored[k], 16)
                batches(pool, 0, XTILES, XSETS, step, XSETS)
                for k in range(XSETS):
                    pool.wait_ge(m.stored[k], XTILES // XSETS * 16)

            @block.vector
            def _(v):
                v.memset(hs[H0:H0 + 1, :, :], 1.0).then_inc(m.ones_ready, 1)

                def step(b, n, k):
                    v.wait_ge(m.o_ready, b + 1)
                    if after(b, XSETS):
                        v.wait_ge(m.stored[k], n * 16)
                    v.tensor_single_scalar(o[:, k, :], o_ps[:, k % 2, 0:D], 0.0, ALU.max).then_inc(m.o_done, 1)
                batches(v, 0, XTILES, XSETS, step, XSETS)

            @block.tensor
            def _(pe):
                def transposes(b, n, k):
                    pe.wait_ge(m.x_loaded[k], n * 16 + 16)
                    if after(b, 2):
                        pe.wait_ge(m.xT_copied, b - 1)
                    for i in range(2):
                        last = pe.transpose(xT_ps[:, k % 2, i * P:(i + 1) * P], xs[:, k, i * P:(i + 1) * P], ident[:, :])
                    last.then_inc(m.xT_ready, 1)

                def hidden(b, n, k):
                    pe.wait_ge(m.w_loaded[k], n * 16 + 16)
                    pe.wait_ge(m.xT_copied, b + 1)
                    if after(b, 2):
                        pe.wait_ge(m.relu_ready, b - 1)
                    for i in range(2):
                        last = pe.matmul(h_ps[0:H0, k % 2, 0:P], w[:, k, i * H0:(i + 1) * H0], xT[:, k % 2, i, :], start=i == 0, stop=i == 1)
                    last.then_inc(m.h_ready, 1)

                def outs(b, k):
                    pe.wait_ge(m.relu_ready, b + 1)
                    if after(b, 2):
                        pe.wait_ge(m.o_done, b - 1)
                    pe.matmul(o_ps[:, k % 2, 0:D], hs[:, k % 2, :], w[0:H0 + 1, k, 2 * H0:2 * H0 + D], start=True, stop=True).then_inc(m.o_ready, 1)

                def step(b, n, k):
                    if not isinstance(b, int) or b + 1 < XTILES:
                        transposes(b + 1, n + 1 if k == XSETS - 1 else n, (k + 1) % XSETS)
                    hidden(b, n, k)
                    if after(b, 1):
                        outs(b - 1, (k - 1) % XSETS)
                pe.wait_ge(m.ones_ready, 1)
                transposes(0, 0, 0)
                batches(pe, 0, XTILES - 1, XSETS, step, XSETS)
                step(XTILES - 1, (XTILES - 1) // XSETS, (XTILES - 1) % XSETS)
                outs(XTILES - 1, (XTILES - 1) % XSETS)


def expert_add(nc, t, sb, pb, g):
    x, slot, xo_d = g["x"], g["slot"], g["xo_d"]
    with ExitStack() as st:
        row = sb("ea_row", (P, XSETS, D), F32, st)
        with phase(nc, "ea", f"loaded*{XSETS}", "added") as (block, m):
            @block.gpsimd
            def _(pool):
                for u in range(NODE_TILES):
                    if u >= XSETS:
                        pool.wait_ge(m.added, u - XSETS + 1)
                    pool.indirect_dma_start(row[:, u % XSETS, :], None, xo_d, bass.IndirectOffsetOnAxis(ap=slot[:, u:u + 1], axis=0),
                                            bounds_check=XTILES * P - 1, oob_is_err=False).then_inc(m.loaded[u % XSETS], 16)

            @block.vector
            def _(v):
                for u in range(NODE_TILES):
                    v.wait_ge(m.loaded[u % XSETS], u // XSETS * 16 + 16)
                    v.tensor_tensor(x[:, u, :], x[:, u, :], row[:, u % XSETS, :], ALU.add).then_inc(m.added, 1)


def features(nc, t, sb, pb, g):
    x, ident, eps, f_d, as_d = g["x"], g["ident"], g["eps"], g["f_d"], g["as_d"]
    with ExitStack() as st:
        def s(name, shape, dt=F32):
            return sb("fe_" + name, shape, dt, st)
        ws, bs = s("ws", (P, 2, D)), s("bs", (P, D))
        aws, awd = s("aws", (P, D)), s("awd", (P, D))
        stats, mv, std, rstd = ln_buffers(s)
        xn, xnT = s("xn", (P, CT, D)), s("xnT", (P, 2, CN))
        row, a_src = s("row", (P, CT, FROW)), s("a_src", (P, 2, CT * H))
        wa, ba, wa_tmp, ba_tmp = s("wa", (P, 2, 2 * H)), s("ba", (P, 2 * H)), s("wa_tmp", (P, 2, 2, D)), s("ba_tmp", (P, 2, D))
        parts = s("parts", (P, 3, CT * H), BF16)
        banks, prod, dots = pb(st, "fe_banks", (P, 3, 512)), pb(st, "fe_prod", (P, 3, 512)), pb(st, "fe_dots", (P, 512))
        dot = dots[:, 0:CT * 2 * H].rearrange("p (u a h) -> p u a h", a=2, h=H)
        heads = row[:, :, 0:H * FR].rearrange("p u (h c) -> p u h c", c=FR)
        with phase(nc, "fe", "loaded", "turn", "ln_step", "std_ready", "banks_ready", "copied", "prod_ready", "biased+dve", "weighted",
                   "wa_ready", "dots_ready", "rows_ready+dve", "rows_stored+sp", "ones_ready") as (block, m):
            @block.sync
            def _(sp):
                for a, b in ((ws[:, :, :], "Ws"), (bs[:, :], "bs"), (aws[:, :], "aw_s"), (awd[:, :], "aw_d")):
                    sp.dma_start(a, t[b]).then_inc(m.loaded, 16)
                f_rows = f_d.rearrange("(u p) c -> p u c", p=P)
                as_rows = as_d.rearrange("a (u p) h -> p a u h", p=P)
                with sp.Fori(0, CHUNKS) as c:
                    sp.wait_ge(m.rows_ready, c * 6 + (6 + FREE))
                    sp.dma_start(f_rows[:, bass.ds(c * CT, CT), :], row[:, :, :]).then_inc(m.rows_stored, 16)
                    for a in range(3):
                        sp.dma_start(as_rows[:, a, bass.ds(c * CT, CT), :],
                                     parts[:, a, :].rearrange("p (u h) -> p u h", h=H)).then_inc(m.rows_stored, 16)
                sp.wait_ge(m.rows_stored, CHUNKS * 64 + FREE)

            @block.gpsimd
            def _(pool):
                pool.memset(heads[:, :, :, DH], 1.0).then_inc(m.ones_ready, 1)

            @block.vector
            def _(v):
                def norm(c):
                    normalize(v, c, lambda u: x[:, bass.ds(c * CT + u, 1), :].rearrange("p a d -> p (a d)"),
                              xn, stats, mv, std, rstd, eps, m)

                def rows(c):
                    v.wait_ge(m.rows_stored, c * 64 + FREE)
                    for b in range(3):
                        n = min(2, CT - 2 * b)
                        v.wait_ge(m.prod_ready, c * 3 + (b + 1))
                        for u in range(2 * b, 2 * b + n):
                            last = v.tensor_tensor(heads[:, u, :, 0:DH],
                                                   prod[:, b, (u % 2) * D:(u % 2 + 1) * D].rearrange("p (h d) -> p h d", h=H),
                                                   bs[:, :].rearrange("p (h d) -> p h d", h=H), ALU.add)
                        last.then_inc(m.biased, 1)
                    v.wait_ge(m.biased, c * 3 + (3 + FREE))
                    v.wait_ge(m.dots_ready, c + 1)
                    v.tensor_tensor(a_src[:, 0, :].rearrange("p (u h) -> p u h", h=H), dot[:, :, 0, :], bc(ba[:, 0:H], 1, CT),
                                    ALU.add).then_inc(m.rows_ready, 1)
                    v.tensor_tensor(row[:, :, H * FR:FROW], dot[:, :, 1, :], bc(ba[:, H:2 * H], 1, CT), ALU.add).then_inc(m.rows_ready, 1)
                    for a in range(2):
                        v.wait_ge(m.rows_ready, c * 6 + (2 + 2 * a + FREE))
                        v.tensor_copy(parts[:, a, :], a_src[:, a, :]).then_inc(m.rows_ready, 1)
                        v.wait_ge(m.rows_ready, c * 6 + (3 + 2 * a + FREE))
                        rest = parts[:, 2, :] if a else a_src[:, 1, :]
                        v.tensor_tensor(rest, a_src[:, a, :], parts[:, a, :], ALU.subtract).then_inc(m.rows_ready, 1)
                    v.wait_ge(m.rows_ready, c * 6 + (6 + FREE))
                norm(0)
                v.wait_ge(m.loaded, 64)
                for a, aw in enumerate((aws, awd)):
                    v.tensor_tensor(wa_tmp[:, a, :, :], ws[:, :, :], bc(aw[:, :], 1, 2), ALU.mult).then_inc(m.weighted, 1)
                    v.tensor_tensor(ba_tmp[:, a, :], bs[:, :], aw[:, :], ALU.mult).then_inc(m.weighted, 1)
                v.wait_ge(m.weighted, 4)
                for a in range(2):
                    v.tensor_reduce(wa[:, :, a * H:(a + 1) * H], wa_tmp[:, a, :, :].rearrange("p k (h d) -> p k h d", h=H),
                                    axis=AX.X, op=ALU.add).then_inc(m.wa_ready, 1)
                v.tensor_reduce(ba[:, :].rearrange("p (a h) -> p a h", a=2), ba_tmp[:, :, :].rearrange("p a (h d) -> p a h d", h=H),
                                axis=AX.X, op=ALU.add).then_inc(m.wa_ready, 1)
                v.wait_ge(m.wa_ready, 3)
                v.wait_ge(m.ones_ready, 1)
                with v.Fori(0, CHUNKS - 1) as c:
                    v.wait_ge(m.banks_ready, c * 3 + 3)
                    v.sem_inc(m.turn, 1)
                    norm(c + 1)
                    rows(c)
                rows(CHUNKS - 1)

            @block.scalar
            def _(act):
                deviations(act, 0, mv, std, eps, m)
                with act.Fori(0, CHUNKS - 1) as c:
                    copy_transposed(act, c, banks, xnT, m.banks_ready, m.copied)
                    deviations(act, c + 1, mv, std, eps, m)
                    act.wait_ge(m.dots_ready, c + 1)
                copy_transposed(act, CHUNKS - 1, banks, xnT, m.banks_ready, m.copied)

            @block.tensor
            def _(pe):
                pe.wait_ge(m.loaded, 64)
                with pe.Fori(0, CHUNKS) as c:
                    pe.wait_ge(m.ln_step, c * 4 + 4)
                    transposed(pe, xn, banks, ident, m.banks_ready)
                    pe.wait_ge(m.biased, c * 3 + FREE)
                    for u in range(CT):
                        pe.wait_ge(m.copied, c * 3 + (u // 2 + 1))
                        for k in range(2):
                            last = pe.matmul(prod[:, u // 2, (u % 2) * D:(u % 2 + 1) * D],
                                             xnT[:, k, u * P:(u + 1) * P], ws[:, k, :], start=k == 0, stop=k == 1)
                        if u % 2 or u == CT - 1:
                            last.then_inc(m.prod_ready, 1)
                    pe.wait_ge(m.wa_ready, 2)
                    pe.wait_ge(m.rows_ready, c * 6 + FREE)
                    for u in range(CT):
                        for k in range(2):
                            last = pe.matmul(dots[:, u * 2 * H:(u + 1) * 2 * H], xnT[:, k, u * P:(u + 1) * P], wa[:, k, :],
                                             start=k == 0, stop=k == 1)
                    last.then_inc(m.dots_ready, 1)


def pooling_edges(nc, t, sb, pb, g):
    ident_big, slot_dst, slot_weight, marks = (g[k] for k in ("ident_big", "slot_dst", "slot_weight", "marks"))
    keep, tile_blk, f_d, as_d, totals = (g[k] for k in ("keep", "tile_blk", "f_d", "as_d", "sums"))
    feat = g["kv"][:, :, :, 0:FROW]
    with ExitStack() as st:
        def s(name, shape, dt=F32):
            return sb("pe_" + name, shape, dt, st)
        idx = s("idx", (P, SETS, BT), I32)
        a_src = s("a_src", (3, FEW, BT, HW), BF16)
        ones = s("ones", (3, P), BF16)
        awe, ab = s("awe", (P, H)), s("ab", (P, H))
        sel = s("sel", (P, FEW, BT, W), BF16)
        edge = s("edge", (P, FEW, BT, H))
        own = s("own", (P, 2, BT, H))
        part = s("part", (P, 2, BT, H))
        low = s("low", (P, 2, BT, H))
        ex = s("ex", (P, 2, BT, H))
        wgt = s("wgt", (P, 2, BT, H, HB))
        acc = s("acc", (P, FEW, BT, FR))
        sc_ps, out_ps = pb(st, "pe_sc", (P, 2, 512)), pb(st, "pe_out", (P, 2, 512))
        with phase(nc, "pe", "loaded", "const_ready", "turn", "idx_ready", f"feat_loaded*{SETS}", f"src_loaded*{FEW}", "edge_step",
                   "sel_ready", "scores_ready", "own_ready", "part_ready", "sum_ready", "low_ready", "exp_ready", "weights_ready",
                   "sums_ready", "acc_ready", "kept") as (block, m):

            @block.gpsimd
            def _(pool):
                def step(b, n, k):
                    pool.wait_ge(m.idx_ready, b - SETS + 2 if after(b, SETS) else 1)
                    pool.sem_inc(m.turn, 1)
                    for u in range(BT):
                        pool.indirect_dma_start(
                            feat[:, k, u, :], None, f_d, bass.IndirectOffsetOnAxis(ap=idx[:, k, u:u + 1], axis=0),
                            bounds_check=NP_ - 1, oob_is_err=False).then_inc(m.feat_loaded[k], 16)
                batches(pool, 0, BATCHES, SETS, step)

            @block.sync
            def _(sp):
                sp.dma_start(awe[:, :], t["aw_e"]).then_inc(m.loaded, 16)
                sp.dma_start(ab[:, :], t["ab"]).then_inc(m.loaded, 16)

                def step(b, n, k):
                    blocks = tile_blocks(nc, mybir.EngineType.SP, tile_blk, b)
                    if after(b, FEW):
                        sp.wait_ge(m.scores_ready, b - FEW + 1)
                    for u in range(BT):
                        sp.dma_start(a_src[:, k % FEW, u, :], as_d[:, bass.ds(blocks[u] * W, W), :].rearrange("a w h -> a (w h)")).then_inc(m.src_loaded[k % FEW], 16)
                batches(sp, 0, BATCHES, SETS, step)

            @block.scalar
            def _(act):
                def select(b, k):
                    if after(b, FEW):
                        act.wait_ge(m.weights_ready, b - FEW + 1)
                        act.sem_inc(m.turn, 1)
                    act.activation(sel[:, k % FEW, :, :], marks[:, bass.ds(b * BT, BT), 0:W], ACT.Copy, bias=1.0, scale=-1.0).then_inc(m.sel_ready, 1)

                def keep_sums(b, k):
                    blocks = tile_blocks(nc, mybir.EngineType.Activation, tile_blk, b)
                    for u in range(BT):
                        if u == 0:
                            act.wait_ge(m.acc_ready, b * BT + BT)
                        act.wait_ge(m.kept, b * BT + u)
                        act.sem_inc(m.turn, 1)
                        act.activation(totals[:, bass.ds(blocks[u], 1), :], acc[:, k % FEW, u:u + 1, :], ACT.Copy).then_inc(m.kept, 1)

                def destinations(b, k):
                    if after(b, 2) and (not isinstance(b, int) or b + SETS - 2 < BATCHES):
                        act.wait_ge(m.sums_ready, b - 1)
                        act.sem_inc(m.turn, 1)
                        act.activation(idx[:, (k - 2) % SETS, :], slot_dst[:, bass.ds((b + SETS - 2) * BT, BT)], ACT.Copy).then_inc(m.idx_ready, 1)

                LATE = 3

                def step(b, n, k):
                    if not isinstance(b, int) or b + 1 < BATCHES:
                        select(b + 1, (k + 1) % SETS)
                    act.wait_ge(m.low_ready, b + 1)
                    act.activation(ex[:, k % 2, :, :], low[:, k % 2, :, :], ACT.Exp, scale=-1.0).then_inc(m.exp_ready, 1)
                    destinations(b, k)
                    if after(b, LATE):
                        keep_sums(b - LATE, (k - LATE) % SETS)
                act.activation(idx[:, :, :], slot_dst[:, 0:SETS * BT].rearrange("p (s u) -> p s u", u=BT), ACT.Copy).then_inc(m.idx_ready, 1)
                act.wait_ge(m.const_ready, 4)
                select(0, 0)
                batches(act, 0, BATCHES - 1, SETS, step)
                step(BATCHES - 1, None, (BATCHES - 1) % SETS)
                for b in range(BATCHES - LATE, BATCHES):
                    keep_sums(b, b % SETS)

            @block.vector
            def _(v):
                def edges(b, k):
                    v.tensor_tensor(part[:, k % 2, :, :], bc(slot_weight[:, bass.ds(b * BT, BT)], 2, H),
                                    bc(awe[:, :], 1, BT), ALU.mult).then_inc(m.edge_step, 1)
                    v.wait_ge(m.edge_step, b * 2 + 1)
                    v.tensor_tensor(edge[:, k % FEW, :, :], part[:, k % 2, :, :], bc(ab[:, :], 1, BT), ALU.add).then_inc(m.edge_step, 1)

                def accumulate(b, k, u):
                    prev = acc[:, k % FEW, u - 1, :] if u else acc[:, (k - 1) % FEW, BT - 1, :]
                    v.scalar_tensor_tensor(acc[:, k % FEW, u, :], prev, keep[:, bass.ds(b * BT + u, 1)],
                                           out_ps[:, k % 2, u * FR:(u + 1) * FR], ALU.mult, ALU.add).then_inc(m.acc_ready, 1)

                def acc_waits(b, k):
                    v.wait_ge(m.sums_ready, b + 1)
                    if after(b, FEW):
                        v.wait_ge(m.kept, (b - FEW) * BT + BT)

                def step(b, n, k):
                    j = k % 2
                    v.wait_ge(m.scores_ready, b + 1)
                    v.tensor_reduce(own[:, j, :, :].rearrange("p u h -> p (u h)"),
                                    sc_ps[:, j, 0:BT * HW].rearrange("p (x w) -> p x w", w=W),
                                    axis=AX.X, op=ALU.max).then_inc(m.own_ready, 1)
                    if not isinstance(b, int) or b + 1 < BATCHES:
                        edges(b + 1, (k + 1) % SETS)
                    v.wait_ge(m.own_ready, b + 1)
                    v.wait_ge(m.feat_loaded[k], n * (16 * BT) + 16 * BT)
                    v.tensor_tensor(part[:, j, :, :], own[:, j, :, :], feat[:, k, :, H * FR:FROW], ALU.add).then_inc(m.part_ready, 1)
                    old = after(b, 2)
                    if old:
                        bo, ko = b - 2, (k - 2) % SETS
                        acc_waits(bo, ko)
                        v.wait_ge(m.acc_ready, bo * BT)
                        accumulate(bo, ko, 0)
                    v.wait_ge(m.part_ready, b + 1)
                    v.wait_ge(m.edge_step, b * 2 + 2)
                    v.tensor_tensor(own[:, j, :, :], part[:, j, :, :], edge[:, k % FEW, :, :], ALU.add).then_inc(m.sum_ready, 1)
                    if old:
                        v.wait_ge(m.acc_ready, bo * BT + 1)
                        accumulate(bo, ko, 1)
                    v.wait_ge(m.sum_ready, b + 1)
                    v.tensor_scalar(low[:, j, :, :], own[:, j, :, :], 1.0 / 20.0, 0.0, ALU.mult, ALU.max).then_inc(m.low_ready, 1)
                    for u in (2, 3):
                        if old:
                            v.wait_ge(m.acc_ready, bo * BT + u)
                            accumulate(bo, ko, u)
                    v.wait_ge(m.exp_ready, b + 1)
                    v.wait_ge(m.sel_ready, b + 1)
                    v.tensor_tensor(wgt[:, j, :, :, 0:W], bc(ex[:, j, :, :], 3, W), bc(sel[:, k % FEW, :, :], 2, H),
                                    ALU.mult).then_inc(m.weights_ready, 1)

                v.memset(totals[:, FULL_BLOCKS:BLOCKS, :], 0.0).then_inc(m.const_ready, 1)
                v.memset(acc[:, :, :, :], 0.0).then_inc(m.const_ready, 1)
                v.memset(wgt[:, :, :, :, :], 0.0).then_inc(m.const_ready, 1)
                v.memset(ones[:, :], 1.0).then_inc(m.const_ready, 1)
                v.wait_ge(m.const_ready, 4)
                v.wait_ge(m.loaded, 32)
                edges(0, 0)
                batches(v, 0, BATCHES - 1, SETS, step)
                step(BATCHES - 1, (BATCHES - 1) // SETS, (BATCHES - 1) % SETS)
                for b in (BATCHES - 2, BATCHES - 1):
                    acc_waits(b, b % SETS)
                    for u in range(BT):
                        v.wait_ge(m.acc_ready, b * BT + u)
                        accumulate(b, b % SETS, u)

            @block.tensor
            def _(pe):
                def scores(b, n, k):
                    pe.wait_ge(m.src_loaded[k % FEW], n * (SETS // FEW * 16 * BT) + (k // FEW + 1) * 16 * BT)
                    for u in range(BT):
                        o = sc_ps[:, k % 2, u * HW:(u + 1) * HW]
                        pe.matmul(o, ident_big[:, :], bc(marks[:, bass.ds(b * BT + u, 1), 0:W].rearrange("p a w -> p (a w)"), 1, H), start=True, stop=False)
                        last = pe.matmul(o, ones[:, :], a_src[:, k % FEW, u, :].rearrange("a (w h) -> a h w", h=H),
                                         start=False, stop=True)
                    last.then_inc(m.scores_ready, 1)

                def sums(b, n, k):
                    pe.wait_ge(m.weights_ready, b + 1)
                    pe.wait_ge(m.feat_loaded[k], n * (16 * BT) + 16 * BT)
                    for u in range(BT):
                        for h in range(H):
                            last = pe.matmul(out_ps[h * HB:(h + 1) * HB, k % 2, u * FR:(u + 1) * FR], wgt[:, k % 2, u, h, :],
                                             feat[:, k, u, h * FR:(h + 1) * FR], start=True, stop=True)
                    last.then_inc(m.sums_ready, 1)

                def step(b, n, k):
                    scores(b, n, k)
                    if after(b, 1):
                        sums(b - 1, n if k else n - 1, (k - 1) % SETS)

                pe.wait_ge(m.const_ready, 4)
                batches(pe, 0, BATCHES, 1, step)
                sums(BATCHES - 1, (BATCHES - 1) // SETS, (BATCHES - 1) % SETS)


def pooled_nodes(nc, t, sb, pb, g):
    x, hid, eps, totals, p_d, valid, node_sum = (g[k] for k in ("x", "hid", "eps", "sums", "p_d", "valid", "node_sum"))
    with ExitStack() as st:
        def s(name, shape, dt=F32):
            return sb("pn_" + name, shape, dt, st)
        sums = s("sums", (P, 2, CT, H, FR))
        stats, mv, std, rstd = ln_buffers(s)
        padding, total, inv = s("padding", (P, NODE_TILES)), s("total", (P, CT, H)), s("inv", (P, CT, H))
        y = s("y", (P, CT, D))
        col_ps = pb(st, "pn_col", (P, 2, 512))
        with phase(nc, "pn", f"laid*{CHUNKS}", "sums_loaded*2", "turn", "padding_ready", "pool_step", "added", "ln_step",
                   "std_ready", "cols_ready") as (block, m):
            @block.sync
            def _(sp):
                rows = p_d.rearrange("b w h c -> (b w) (h c)").rearrange("(u p) c -> p u c", p=P)
                for c in range(CHUNKS + 1):
                    if c < CHUNKS:
                        blocks = slice(c * CB, (c + 1) * CB)
                        with nc.allow_non_contiguous_dma("rows of a head"):
                            for head in range(H):
                                sp.dma_start(p_d.rearrange("b w h c -> w h b c")[:, head, blocks, :],
                                             totals[head * HB:head * HB + W, blocks, :]).then_inc(m.laid[c], 16)
                    if c >= 1:
                        sp.wait_ge(m.laid[c - 1], H * 16)
                        if c >= 3:
                            sp.wait_ge(m.added, c - 2)
                        sp.dma_start(sums[:, (c - 1) % 2, :, :, :].rearrange("p u h c -> p u (h c)"),
                                     rows[:, (c - 1) * CT:c * CT, :]).then_inc(m.sums_loaded[(c - 1) % 2], 16)

            @block.scalar
            def _(act):
                for c in range(CHUNKS):
                    deviations(act, c, mv, std, eps, m)

            @block.vector
            def _(v):
                v.tensor_scalar(padding[:, :], valid[:, :], -1.0, 1.0, ALU.mult, ALU.add).then_inc(m.padding_ready, 1)
                v.wait_ge(m.padding_ready, 1)

                def pool(c):
                    b = c % 2
                    v.wait_ge(m.sums_loaded[b], c // 2 * 16 + 16)
                    v.tensor_tensor(total[:, :, :], sums[:, b, :, :, DH], bc(padding[:, c * CT:(c + 1) * CT], 2, H),
                                    ALU.add).then_inc(m.pool_step, 1)
                    v.wait_ge(m.pool_step, c * 3 + 1)
                    v.reciprocal(inv[:, :, :], total[:, :, :]).then_inc(m.pool_step, 1)
                    v.wait_ge(m.pool_step, c * 3 + 2)
                    if c:
                        v.wait_ge(m.added, c)
                    for u in range(CT):
                        last = v.tensor_tensor(y[:, u, :].rearrange("p (h d) -> p h d", h=H), sums[:, b, u, :, 0:DH],
                                               bc(inv[:, u, :], 2, DH), ALU.mult)
                    last.then_inc(m.pool_step, 1)
                    v.wait_ge(m.pool_step, c * 3 + 3)
                    xc = x[:, c * CT:(c + 1) * CT, :]
                    v.tensor_tensor(xc, xc, y[:, :, :], ALU.add).then_inc(m.added, 1)

                pool(0)
                for c in range(CHUNKS):
                    v.wait_ge(m.added, c + 1)
                    if c:
                        v.wait_ge(m.ln_step, c * 4)
                    normalize(v, c, lambda u: x[:, c * CT + u, :], hid[:, c * CT:(c + 1) * CT, :], stats, mv, std, rstd, eps, m,
                              (lambda: pool(c + 1)) if c + 1 < CHUNKS else None)
                v.wait_ge(m.cols_ready, 1)
                v.tensor_copy(node_sum[:, :], col_ps[:, :, 0])

            @block.tensor
            def _(pe):
                for c in range(CHUNKS):
                    pe.wait_ge(m.ln_step, c * 4 + 4)
                    for u in range(c * CT, (c + 1) * CT):
                        for k in range(2):
                            last = pe.matmul(col_ps[:, k, 0:1], hid[:, u, k * P:(k + 1) * P], valid[:, u:u + 1],
                                             start=u == 0, stop=u == NODE_TILES - 1)
                last.then_inc(m.cols_ready, 1)


def routed_ffn(nc, t, sb, pb, g, out):
    x, hid, ident, eps, node_sum = (g[k] for k in ("x", "hid", "ident", "eps", "node_sum"))
    with ExitStack() as st:
        def s(name, shape, dt=F32):
            return sb("rf_" + name, shape, dt, st)
        wr, br, iota = s("wr", (P, 2, EX1)), s("br", (1, EX1)), s("iota", (1, EX1))
        r = s("r", (1, 14, EX1))
        c1 = s("c1", (1, 14))
        pick = s("pick", (1, 2), I32)
        ones = s("ones", (1, P))
        wts, ws = s("wts", (1, 2)), s("ws", (P, 2))
        f1w, f2w, f1, f2 = s("f1w", (P, 2, 2, FF)), s("f2w", (P, 2, FC, D)), s("f1", (P, 2, FC)), s("f2", (P, 2, D))
        f2s, bias = s("f2s", (P, 2, FC, D)), s("bias", (P, 2, D))
        with ExitStack() as ps_st, phase(nc, "ro", "loaded", "ones_ready", "logits_ready", "step", "exp_ready", "picked", "weights_ready",
                                         "experts_loaded", "spread_ready", "ws_ready") as (block, m):
            lg_ps, ws_ps = pb(ps_st, "ro_lg", (P, 512)), pb(ps_st, "ro_ws", (P, 512))

            @block.sync
            def _(sp):
                sp.dma_start(wr[:, :, :], t["Wr"]).then_inc(m.loaded, 16)
                sp.dma_start(br[:, :], t["br"]).then_inc(m.loaded, 16)
                sp.dma_start(iota[:, :], t["c_iota_e"][0:1, 0:EX1]).then_inc(m.loaded, 16)
                sp.wait_ge(m.picked, 2)
                for e in range(2):
                    w = sp.value_load(pick[0:1, e:e + 1], min_val=0, max_val=EX1 - 1)
                    one = bass.ds(w, 1)
                    sp.dma_start(f1w[:, e, :, :], t["F1"][one].rearrange("a p k n -> p (a k) n")).then_inc(m.experts_loaded, 16)
                    sp.dma_start(f2w[:, e, :, :], t["F2"][one].rearrange("a p k n -> p (a k) n")).then_inc(m.experts_loaded, 16)
                    sp.dma_start(f1[:, e, :], t["f1"][one].rearrange("a p k -> p (a k)")).then_inc(m.experts_loaded, 16)
                    sp.dma_start(f2[:, e, :], t["f2"][one].rearrange("a p k -> p (a k)")).then_inc(m.experts_loaded, 16)
                sp.wait_ge(m.experts_loaded, 128)

            @block.tensor
            def _(pe):
                pe.wait_ge(m.loaded, 48)
                for k in range(2):
                    last = pe.matmul(lg_ps[0:1, 0:EX1], node_sum[:, k:k + 1], wr[:, k, :], start=k == 0, stop=k == 1)
                last.then_inc(m.logits_ready, 1)
                pe.wait_ge(m.ones_ready, 1)
                pe.wait_ge(m.weights_ready, 2)
                pe.matmul(ws_ps[:, 0:2], ones[0:1, :], wts[0:1, :], start=True, stop=True).then_inc(m.spread_ready, 1)

            @block.scalar
            def _(act):
                for n, (src, dst, neg, tot) in enumerate(((0, 1, 0, 1), (4, 5, 2, 3))):
                    act.wait_ge(m.step, 2 if n == 0 else 9)
                    act.activation(r[0:1, dst, :], r[0:1, src, :], ACT.Exp, bias=c1[0:1, neg:neg + 1],
                                   accum_out=c1[0:1, tot:tot + 1]).then_inc(m.exp_ready, 1)
                act.wait_ge(m.step, 21)
                act.activation(c1[0:1, 10:11], c1[0:1, 9:10], ACT.Exp).then_inc(m.exp_ready, 1)
                act.wait_ge(m.ws_ready, 1)
                act.wait_ge(m.experts_loaded, 128)
                for e in range(2):
                    act.activation(f2s[:, e, :, :], f2w[:, e, :, :], ACT.Copy, scale=ws[:, e:e + 1])

            @block.vector
            def _(v):
                done = [0]

                def then(ins):
                    done[0] += 1
                    ins.then_inc(m.step, 1)
                    v.wait_ge(m.step, done[0])

                def row(i):
                    return r[0:1, i, :]

                def one(i):
                    return c1[0:1, i:i + 1]
                v.memset(ones[:, :], 1.0).then_inc(m.ones_ready, 1)
                v.wait_ge(m.loaded, 48)
                v.wait_ge(m.logits_ready, 1)
                then(v.scalar_tensor_tensor(row(0), lg_ps[0:1, 0:EX1], 1.0 / N, br[0:1, :], ALU.mult, ALU.add))
                then(v.tensor_reduce(one(0), row(0), axis=AX.X, op=ALU.max, negate=True))
                v.wait_ge(m.exp_ready, 1)
                then(v.reciprocal(one(4), one(1)))
                then(v.tensor_scalar(row(2), row(1), one(4), None, ALU.mult))
                then(v.tensor_single_scalar(row(3), row(2), float(N), ALU.mult))
                then(v.reciprocal(row(6), row(3)))
                then(v.tensor_scalar(row(7), row(6), CAPACITY, 1.0, ALU.mult, ALU.min))
                then(v.tensor_tensor(row(4), row(2), row(7), ALU.mult))
                then(v.tensor_reduce(one(2), row(4), axis=AX.X, op=ALU.max, negate=True))
                then(v.tensor_single_scalar(iota[0:1, :], iota[0:1, :], -float(EX1), ALU.add))
                v.wait_ge(m.exp_ready, 2)
                then(v.reciprocal(one(5), one(3)))
                then(v.tensor_scalar(row(8), row(5), one(5), None, ALU.mult))
                for n in range(2):
                    then(v.tensor_reduce(one(6 + n), row(8), axis=AX.X, op=ALU.max))
                    then(v.scalar_tensor_tensor(row(9), row(8), one(6 + n), iota[0:1, :], ALU.is_equal, ALU.mult))
                    then(v.tensor_reduce(one(8), row(9), axis=AX.X, op=ALU.min))
                    v.tensor_single_scalar(pick[0:1, n:n + 1], one(8), float(EX1), ALU.add).then_inc(m.picked, 1)
                    if n == 0:
                        then(v.tensor_scalar(row(10), iota[0:1, :], one(8), -4.0, ALU.is_equal, ALU.mult))
                        then(v.tensor_tensor(row(8), row(8), row(10), ALU.add))
                then(v.tensor_tensor(one(9), one(7), one(6), ALU.subtract))
                assert done[0] == 21, done
                v.wait_ge(m.exp_ready, 3)
                then(v.tensor_single_scalar(one(11), one(10), 1.0, ALU.add))
                then(v.reciprocal(one(12), one(11)))
                v.tensor_copy(wts[0:1, 0:1], one(12)).then_inc(m.weights_ready, 1)
                v.tensor_tensor(wts[0:1, 1:2], one(12), one(10), ALU.mult).then_inc(m.weights_ready, 1)
                v.wait_ge(m.spread_ready, 1)
                v.tensor_copy(ws[:, :], ws_ps[:, 0:2]).then_inc(m.ws_ready, 1)
                v.wait_ge(m.ws_ready, 1)
                v.wait_ge(m.experts_loaded, 128)
                then(v.tensor_scalar(bias[:, 1, :], f2[:, 0, :], ws[:, 0:1], None, ALU.mult))
                then(v.scalar_tensor_tensor(bias[:, 0, :], f2[:, 1, :], ws[:, 1:2], bias[:, 1, :], ALU.mult, ALU.add))

        gam, bet = s("gam", (P, D)), s("bet", (P, D))
        hb, hT, hs = s("hb", (P, CT, D)), s("hT", (P, 2, CN)), s("hs", (P, 2, FC, CN))
        stats, mv, std, rstd = ln_buffers(s)
        y, z = s("y", (P, CT, D)), s("z", (P, CT, D))
        banks, h_ps, prod = pb(st, "rf_banks", (P, 3, 512)), pb(st, "rf_h", (P, 2, 512)), pb(st, "rf_prod", (P, 3, 512))
        R = 2 * FC * 2
        with phase(nc, "rf", "loaded", "hb_ready", "turn", "banks_ready", "copied+act", "h_ready", "gelu_ready+act", "prod_ready",
                   "biased+dve", "with_hid", "ln_step", "std_ready", "scaled", "shifted", "summed", "stored+sp") as (block, m):
            @block.sync
            def _(sp):
                sp.dma_start(gam[:, :], t["gamma"]).then_inc(m.loaded, 16)
                sp.dma_start(bet[:, :], t["beta"]).then_inc(m.loaded, 16)
                with sp.Fori(0, CHUNKS) as c:
                    sp.wait_ge(m.summed, c + 1)
                    sp.dma_start(out[:, bass.ds(c * CT, CT), :], z[:, :, :]).then_inc(m.stored, 16)
                sp.wait_ge(m.stored, CHUNKS * 16 + FREE)

            @block.gpsimd
            def _(pool):
                with pool.Fori(0, CHUNKS) as c:
                    pool.wait_ge(m.copied, c * 3 + FREE)
                    pool.sem_inc(m.turn, 1)
                    pool.tensor_copy(hb[:, :, :], hid[:, bass.ds(c * CT, CT), :]).then_inc(m.hb_ready, 1)

            @block.scalar
            def _(act):
                def hidden(c, first, last):
                    for n in range(first, last):
                        e, j, f = n // (2 * FC), n // 2 % FC, n % 2
                        act.wait_ge(m.h_ready, c * R + (n + 1))
                        act.activation(hs[:, e, j, f * HALF:(f + 1) * HALF], h_ps[:, f, 0:HALF], ACT.Gelu,
                                       bias=f1[:, e, j:j + 1]).then_inc(m.gelu_ready, 1)

                def copy(c):
                    copy_transposed(act, c, banks, hT, m.banks_ready, m.copied)
                EARLY = 8
                copy(0)
                hidden(0, 0, R)
                with act.Fori(0, CHUNKS - 1) as c:
                    copy(c + 1)
                    act.wait_ge(m.prod_ready, c * 3 + 3)
                    hidden(c + 1, 0, EARLY)
                    deviations(act, c, mv, std, eps, m)
                    hidden(c + 1, EARLY, R)
                deviations(act, CHUNKS - 1, mv, std, eps, m)

            @block.tensor
            def _(pe):
                def transposes(c):
                    pe.wait_ge(m.hb_ready, c + 1)
                    transposed(pe, hb, banks, ident, m.banks_ready)

                def chunk(c, more):
                    pe.wait_ge(m.copied, c * 3 + (3 + FREE))
                    for n in range(R):
                        e, j, f = n // (2 * FC), n // 2 % FC, n % 2
                        pe.wait_ge(m.gelu_ready, c * R + (max(n - 1, 0) + FREE))
                        for k in range(2):
                            last = pe.matmul(h_ps[:, f, 0:HALF], f1w[:, e, k, j * P:(j + 1) * P],
                                             hT[:, k, f * HALF:(f + 1) * HALF], start=k == 0, stop=k == 1)
                        last.then_inc(m.h_ready, 1)
                    if more:
                        transposes(c + 1)
                    pe.wait_ge(m.gelu_ready, c * R + (R + FREE))
                    pe.wait_ge(m.biased, c * 3 + FREE)
                    for u in range(CT):
                        for n in range(2 * FC):
                            last = pe.matmul(prod[:, u // 2, (u % 2) * D:(u % 2 + 1) * D], hs[:, n // FC, n % FC, u * P:(u + 1) * P],
                                             f2s[:, n // FC, n % FC, :], start=n == 0, stop=n == 2 * FC - 1)
                        if u % 2 or u == CT - 1:
                            last.then_inc(m.prod_ready, 1)
                transposes(0)
                with pe.Fori(0, CHUNKS - 1) as c:
                    chunk(c, True)
                chunk(CHUNKS - 1, False)

            @block.vector
            def _(v):
                v.wait_ge(m.loaded, 32)
                with v.Fori(0, CHUNKS) as c:
                    for b in range(3):
                        n = min(2, CT - 2 * b)
                        v.wait_ge(m.prod_ready, c * 3 + (b + 1))
                        v.tensor_tensor(y[:, 2 * b:2 * b + n, :], prod[:, b, 0:n * D].rearrange("p (u d) -> p u d", u=n),
                                        bc(bias[:, 0, :], 1, n), ALU.add).then_inc(m.biased, 1)
                    v.wait_ge(m.biased, c * 3 + (3 + FREE))
                    v.wait_ge(m.stored, c * 16 + FREE)
                    v.tensor_tensor(z[:, :, :], y[:, :, :], hid[:, bass.ds(c * CT, CT), :], ALU.add).then_inc(m.with_hid, 1)
                    v.wait_ge(m.with_hid, c + 1)
                    normalize(v, c, lambda u: z[:, u, :], y, stats, mv, std, rstd, eps, m)
                    v.wait_ge(m.ln_step, c * 4 + 4)
                    v.tensor_tensor(z[:, :, :], y[:, :, :], bc(gam[:, :], 1, CT), ALU.mult).then_inc(m.scaled, 1)
                    v.wait_ge(m.scaled, c + 1)
                    v.tensor_tensor(y[:, :, :], z[:, :, :], bc(bet[:, :], 1, CT), ALU.add).then_inc(m.shifted, 1)
                    v.wait_ge(m.shifted, c + 1)
                    v.tensor_tensor(z[:, :, :], y[:, :, :], x[:, bass.ds(c * CT, CT), :], ALU.add).then_inc(m.summed, 1)
                    v.wait_ge(m.summed, c + 1)


def host_layout(i):
    f = {k: np.ascontiguousarray(v) for k, v in i.items()}

    def edges(a, pad):
        out = np.full(P * EC, pad, a.dtype)
        out[:E] = a
        return out.reshape(P, EC)

    def rows(a):
        return np.ascontiguousarray(a.reshape(-1, P, a.shape[-1]).transpose(1, 0, 2))

    def experts(w1, w2, b2, b1):
        out = np.zeros((EX0, P, XW), np.float32)
        out[:, :, 0:2 * H0] = w1.reshape(EX0, 2, P, H0).transpose(0, 2, 1, 3).reshape(EX0, P, 2 * H0)
        out[:, 0:H0, 2 * H0:2 * H0 + D] = w2
        out[:, H0, 2 * H0:2 * H0 + D] = b2
        out[:, 0:H0, XW - 1] = b1
        return out

    def spread(a):
        return np.ascontiguousarray(np.broadcast_to(a.reshape(1, -1), (P, a.size)))

    x = np.zeros((NP_, D), np.float32)
    x[:N] = f["x"]
    p = np.arange(P)
    t = {
        "x": x.reshape(NODE_TILES, P, D).transpose(1, 0, 2),
        "src": edges(f["src"], SRC_PAD), "dst": edges(f["dst"], 0), "edge_type": edges(f["edge_type_3"], 0),
        "edge_weight": edges(f["edge_weight"], 0),
        "c_ident": np.eye(P, dtype=np.float32),
        "c_before": np.triu(np.ones((P, P), np.float32), 1),
        "c_same": (p[:, None] // 32 == np.arange(4)[None]).astype(np.float32),
        "c_spread": (p[:, None] % 32 == np.arange(32)[None]).astype(np.float32),
        "c_diagonal": (p[:, None] % W == np.arange(W)[None]).astype(np.float32),
        "c_iota_b": spread(np.arange(BLOCKS, dtype=np.float32)),
        "c_iota_w": spread(np.arange(W, dtype=np.float32)),
        "c_iota_e": spread(np.arange(EX0, dtype=np.float32)),
        "c_tcol": (p[:, None] + P * np.arange(TG)[None]).astype(np.float32),
        "c_valid": (p[:, None] + P * np.arange(NODE_TILES)[None] < N).astype(np.float32),
        "Win": rows(f["L0_gnn_Win"].T), "b_in": spread(f["L0_gnn_b_in"]),
        "Wq": np.stack([rows(w.T) for w in f["L0_gnn_Wq"]]),
        "bq": np.stack([b.reshape(2, P).T for b in f["L0_gnn_bq"]]),
        "Wkv": np.stack([rows(np.concatenate([k.T, v.T], 1)) for k, v in zip(f["L0_gnn_Wk"], f["L0_gnn_Wv"])]),
        "bkv": np.stack([spread(np.concatenate([k, v])) for k, v in zip(f["L0_gnn_bk"], f["L0_gnn_bv"])]),
        "Wo": np.stack([np.concatenate([w.T.reshape(H, DH, D).transpose(1, 0, 2)] * 2) for w in f["L0_gnn_Wo"]]),
        "Ee": np.stack([np.repeat(e.reshape(3, H, DH).transpose(2, 1, 0), W, axis=2) for e in f["L0_gnn_Eemb"]]),
        "bo": np.stack([spread(b)[:TW] for b in f["L0_gnn_bo"]]),
        "ln_g": np.stack([spread(b) for b in f["L0_gnn_ln_g"]]),
        "ln_b": np.stack([spread(b) for b in f["L0_gnn_ln_b"]]),
        "A1": rows(f["L0_gnn_W1"].T), "a1": f["L0_gnn_b1"].reshape(2, P).T,
        "A2": rows(f["L0_gnn_W2"].T), "a2": spread(f["L0_gnn_b2"]),
        "router_w": rows(f["L0_ffn_router_w"].T), "router_b": spread(f["L0_ffn_router_b"]),
        "EW": experts(f["L0_ffn_W1"], f["L0_ffn_W2"], f["L0_ffn_b2"], f["L0_ffn_b1"]),
        "Ws": rows(f["L1_gnn_Ws"].transpose(1, 0, 2).reshape(D, H * DH)), "bs": spread(f["L1_gnn_bs"]),
        "aw_s": spread(f["L1_gnn_aw"][:, :DH]), "aw_d": spread(f["L1_gnn_aw"][:, DH:2 * DH]),
        "aw_e": spread(f["L1_gnn_aw"][:, 2 * DH]), "ab": spread(f["L1_gnn_ab"]),
        "Wr": rows(f["L1_ffn_Wr"]), "br": f["L1_ffn_br"].reshape(1, EX1),
        "F1": np.stack([rows(w) for w in f["L1_ffn_W1"]]),
        "f1": np.stack([b.reshape(FC, P).T for b in f["L1_ffn_b1"]]),
        "F2": np.stack([rows(w) for w in f["L1_ffn_W2"]]),
        "f2": np.stack([spread(b) for b in f["L1_ffn_b2"]]),
        "gamma": spread(f["L1_ffn_gamma"]), "beta": spread(f["L1_ffn_beta"]),
    }
    return {k: np.ascontiguousarray(v) for k, v in t.items()}


def kernel(**inputs):
    import concourse.bacc as bacc
    from concourse.bass_utils import run_bass_kernel_spmd

    nc = bacc.Bacc("TRN2", target_bir_lowering=False, num_devices=1)
    arrays = {f"in_{k}": v for k, v in host_layout(inputs).items()}
    t = {k[3:]: nc.dram_tensor(k, list(a.shape), mybir.dt.from_np(a.dtype), kind="ExternalInput").ap()
         for k, a in arrays.items()}
    out = nc.dram_tensor("out_x", [P, NODE_TILES, D], F32, kind="ExternalOutput").ap()
    build(nc, t, out)
    got = run_bass_kernel_spmd(nc, [arrays], core_ids=[0]).results[0]["out_x"]
    return np.asarray(got).transpose(1, 0, 2).reshape(NP_, D)[:N]
```
